# Optimizing a Trainium2 kernel written in Bass

```python
import numpy as np
import jax
import jax.numpy as jnp

def _softmax(x, axis=-1):
    return jax.nn.softmax(x, axis=axis)

def _gelu(x):
    return jax.nn.gelu(x, approximate=True)

def _silu(x):
    return jax.nn.silu(x)

def _sigmoid(x):
    return jax.nn.sigmoid(x)

def _layernorm(x, axis=-1, eps=1e-05):
    m = jnp.mean(x, axis=axis, keepdims=True)
    v = jnp.var(x, axis=axis, keepdims=True)
    return (x - m) / jnp.sqrt(v + eps)

def _scatter_add(tgt, idx, src, axis=0):
    return tgt.at[idx].add(src)

def _segment_sum(src, seg, n):
    return jax.ops.segment_sum(src, seg, n)
kernel_name = 'mk_decoder_preln_d2_seqx_r4_373668'

def setup_inputs(seed: int=0):
    np.random.seed(seed)
    _w = jnp.asarray

    def _rec_inputs():
        import jax
        import jax.numpy as jnp
        _rk = jax.random.key(seed)
        x = 7.22e-05 + 1 * jax.random.normal(jax.random.fold_in(_rk, 1), (16, 256, 256), jnp.float32)
        _lenS = 256 - jax.random.randint(jax.random.fold_in(_rk, 7), (16,), 0, max(1, 256 // 4) + 1, jnp.int32)
        _lenS2 = 77 - jax.random.randint(jax.random.fold_in(_rk, 8), (16,), 0, max(1, 77 // 4) + 1, jnp.int32)
        _ctx_768P = jax.random.normal(jax.random.fold_in(_rk, 11), (16, 16, 192), jnp.float32)
        _ctx_768c = jax.random.dirichlet(jax.random.fold_in(_rk, 511), 0.3 * jnp.ones((16,), jnp.float32), (16, 77))
        _ctx_768t = jnp.einsum('bsk,bkd->bsd', _ctx_768c, _ctx_768P)
        _ctx_768t = _ctx_768t * jax.lax.rsqrt(jnp.mean(jnp.square(_ctx_768t)) + 1e-12) * 0.953939
        ctx_768 = -0.000191848 + 0.999787 * (_ctx_768t + 0.3 * jax.random.normal(jax.random.fold_in(_rk, 611), (16, 77, 192), jnp.float32))
        _validS = jnp.arange(256)[None, :] < _lenS[:, None]
        _validS2 = jnp.arange(77)[None, :] < _lenS2[:, None]
        _causal = jnp.tril(jnp.ones((256, 256), dtype=bool))
        mask_BxS2_bk0 = jnp.logical_not(jnp.broadcast_to(_validS2[:, :], (16, 77)))
        mask_BxS_bf1 = jnp.ones((16, 256), dtype=bool)
        mask_BxS2_bf1 = jnp.ones((16, 77), dtype=bool)
        return (x, ctx_768, mask_BxS2_bk0, mask_BxS_bf1, mask_BxS2_bf1)
    x, ctx_768, mask_BxS2_bk0, mask_BxS_bf1, mask_BxS2_bf1 = _rec_inputs()

    def _L0_attn_setup():
        import jax, jax.numpy as jnp
        import numpy as np
        BATCH, SEQ, HIDDEN = (8, 512, 256)
        WSIZE = 64
        NEG_INF = -1000000000.0
        key = jax.random.key(seed)
        k1, k2 = jax.random.split(key)
        repr_ = jax.random.normal(k1, (BATCH, SEQ, HIDDEN), dtype=jnp.float32)
        W = jax.random.normal(k2, (HIDDEN, HIDDEN), dtype=jnp.float32) * 0.02
        return {'repr': repr_, 'W': W}
    _L0_attn_all = _L0_attn_setup()
    _L0_attn_in = {k: v for k, v in _L0_attn_all.items() if k in ('W',)}
    del _L0_attn_all

    def _L0_xattn_setup():
        import jax, jax.numpy as jnp
        import numpy as np
        HEADS = 8
        DIM_HEAD = 64
        QUERY_DIM = 256
        CONTEXT_DIM = 192
        INNER = HEADS * DIM_HEAD
        key = jax.random.key(seed)
        ks = jax.random.split(key, 8)
        b, n, j = (4, 512, 512)
        x = jax.random.normal(ks[0], (b, n, QUERY_DIM), dtype=jnp.float32)
        context = jax.random.normal(ks[1], (b, j, CONTEXT_DIM), dtype=jnp.float32)
        mask = jax.random.randint(ks[2], (b, j), 0, 2).astype(jnp.bool_)
        W_q = jax.random.normal(ks[3], (QUERY_DIM, INNER), dtype=jnp.float32) / np.sqrt(QUERY_DIM)
        W_k = jax.random.normal(ks[4], (CONTEXT_DIM, INNER), dtype=jnp.float32) / np.sqrt(CONTEXT_DIM)
        W_v = jax.random.normal(ks[5], (CONTEXT_DIM, INNER), dtype=jnp.float32) / np.sqrt(CONTEXT_DIM)
        W_o = jax.random.normal(ks[6], (INNER, QUERY_DIM), dtype=jnp.float32) / np.sqrt(INNER)
        b_o = jax.random.normal(ks[7], (QUERY_DIM,), dtype=jnp.float32) * 0.01
        return {'x': x, 'context': context, 'mask': mask, 'W_q': W_q, 'W_k': W_k, 'W_v': W_v, 'W_o': W_o, 'b_o': b_o}
    _L0_xattn_all = _L0_xattn_setup()
    _L0_xattn_in = {k: v for k, v in _L0_xattn_all.items() if k in ('W_q', 'W_k', 'W_v', 'W_o', 'b_o')}
    del _L0_xattn_all

    def _L0_ffn_setup():
        import jax, jax.numpy as jnp
        import numpy as np
        B, L, D, F, E = (2, 256, 256, 1024, 8)
        key = jax.random.key(seed)
        ks = jax.random.split(key, 7)
        return {'x': jax.random.normal(ks[0], (B, L, D), dtype=jnp.float32), 'router_w': jax.random.normal(ks[1], (D, E), dtype=jnp.float32) * 0.02, 'router_b': jax.random.normal(ks[2], (E,), dtype=jnp.float32) * 0.02, 'W1': jax.random.normal(ks[3], (E, D, F), dtype=jnp.float32) * (1.0 / np.sqrt(D)), 'b1': jax.random.normal(ks[4], (E, F), dtype=jnp.float32) * 0.02, 'W2': jax.random.normal(ks[5], (E, F, D), dtype=jnp.float32) * (1.0 / np.sqrt(F)), 'b2': jax.random.normal(ks[6], (E, D), dtype=jnp.float32) * 0.02}
    _L0_ffn_all = _L0_ffn_setup()
    _L0_ffn_in = {k: v for k, v in _L0_ffn_all.items() if k in ('router_w', 'router_b', 'W1', 'b1', 'W2', 'b2')}
    del _L0_ffn_all

    def _L1_attn_setup():
        import jax, jax.numpy as jnp
        import numpy as np
        T, B, C = (256, 16, 256)
        FF = 4 * C

        def _ln(x, g, b):
            m = x.mean(-1, keepdims=True)
            v = jnp.var(x, axis=-1, keepdims=True)
            return (x - m) * jax.lax.rsqrt(v + 1e-05) * g + b

        def _wkv(w, u, k, v):
            b_, c_ = (k.shape[1], k.shape[2])
            init = (jnp.zeros((b_, c_), k.dtype), jnp.zeros((b_, c_), k.dtype), jnp.full((b_, c_), -1e+38, k.dtype))

            def step(carry, kv):
                aa, bb, pp = carry
                kt, vt = kv
                ww = u + kt
                qq = jnp.maximum(pp, ww)
                e1 = jnp.exp(pp - qq)
                e2 = jnp.exp(ww - qq)
                out = (e1 * aa + e2 * vt) / (e1 * bb + e2)
                ww2 = pp + w
                qq2 = jnp.maximum(ww2, kt)
                e1 = jnp.exp(ww2 - qq2)
                e2 = jnp.exp(kt - qq2)
                return ((e1 * aa + e2 * vt, e1 * bb + e2, qq2), out)
            _, out = jax.lax.scan(step, init, (k, v))
            return out

        def _shift(x):
            return jnp.concatenate([jnp.zeros_like(x[:1]), x[:-1]], axis=0)
        key = jax.random.key(seed)
        ks = jax.random.split(key, 16)
        sc = 1.0 / np.sqrt(C)
        return {'x': jax.random.normal(ks[0], (T, B, C), dtype=jnp.float32), 'ln1_g': jnp.ones((C,), jnp.float32), 'ln1_b': jnp.zeros((C,), jnp.float32), 'ln2_g': jnp.ones((C,), jnp.float32), 'ln2_b': jnp.zeros((C,), jnp.float32), 'time_mix_k': jax.random.uniform(ks[1], (C,), jnp.float32), 'time_mix_v': jax.random.uniform(ks[2], (C,), jnp.float32), 'time_mix_r': jax.random.uniform(ks[3], (C,), jnp.float32), 'time_decay': jax.random.normal(ks[4], (C,), jnp.float32) * 0.1, 'time_first': jax.random.normal(ks[5], (C,), jnp.float32) * 0.1, 'Wk': jax.random.normal(ks[6], (C, C), jnp.float32) * sc, 'Wv': jax.random.normal(ks[7], (C, C), jnp.float32) * sc, 'Wr': jax.random.normal(ks[8], (C, C), jnp.float32) * sc, 'Wo': jax.random.normal(ks[9], (C, C), jnp.float32) * sc, 'cmix_k': jax.random.uniform(ks[10], (C,), jnp.float32), 'cmix_r': jax.random.uniform(ks[11], (C,), jnp.float32), 'Wck': jax.random.normal(ks[12], (FF, C), jnp.float32) * sc, 'Wcv': jax.random.normal(ks[13], (C, FF), jnp.float32) * (1.0 / np.sqrt(FF)), 'Wcr': jax.random.normal(ks[14], (C, C), jnp.float32) * sc}
    _L1_attn_all = _L1_attn_setup()
    _L1_attn_in = {k: v for k, v in _L1_attn_all.items() if k in ('ln1_g', 'ln1_b', 'ln2_g', 'ln2_b', 'time_mix_k', 'time_mix_v', 'time_mix_r', 'time_decay', 'time_first', 'Wk', 'Wv', 'Wr', 'Wo', 'cmix_k', 'cmix_r', 'Wck', 'Wcv', 'Wcr')}
    del _L1_attn_all

    def _L1_xattn_setup():
        import jax, jax.numpy as jnp
        import numpy as np
        B, T, DT, G, DV = (16, 128, 256, 144, 192)
        H, DH = (4, 32)
        INNER = H * DH
        HID = 4 * DT
        N_STATE = 64
        K_TOP = 32

        def layernorm(x, g, b, eps=1e-05):
            m = x.mean(-1, keepdims=True)
            v = x.var(-1, keepdims=True)
            return (x - m) * jax.lax.rsqrt(v + eps) * g + b

        def s4d(x, log_dt, A_re, A_im, C_re, C_im, D_skip):
            Bb, L, D = x.shape
            dt = jnp.exp(log_dt)
            A = A_re + 1j * A_im
            C = C_re + 1j * C_im
            dtA = dt[:, None] * A
            dC = C * (jnp.exp(dtA) - 1.0) / A
            powers = jnp.exp(dtA[:, :, None] * jnp.arange(L))
            K = 2.0 * jnp.einsum('dn,dnl->dl', dC, powers).real
            n = 2 * L
            Kf = jnp.fft.rfft(K, n=n, axis=-1)
            xf = jnp.fft.rfft(x, n=n, axis=1)
            y = jnp.fft.irfft(xf * Kf.T[None], n=n, axis=1)[:, :L]
            return y + x * D_skip
        key = jax.random.key(seed)
        ks = jax.random.split(key, 16)
        s = 0.02
        inp = {'x_text': jax.random.normal(ks[0], (B, T, DT), jnp.float32), 'x_vision': jax.random.normal(ks[1], (B, G, DV), jnp.float32), 'text_mask': jnp.ones((B, T), bool), 'vision_mask': jnp.ones((B, G), bool), 'Wq': jax.random.normal(ks[2], (DT, INNER), jnp.float32) * s, 'Wk': jax.random.normal(ks[3], (DV, INNER), jnp.float32) * s, 'Wv': jax.random.normal(ks[4], (DV, DT), jnp.float32) * s, 'W_film_in': jax.random.normal(ks[5], (DT, 2 * DT), jnp.float32) * s, 'b_film_in': jnp.zeros((2 * DT,), jnp.float32), 'W_film_out': jax.random.normal(ks[6], (DT, 2 * DT), jnp.float32) * s, 'b_film_out': jnp.zeros((2 * DT,), jnp.float32), 'g_norm_in': jnp.ones((DT,), jnp.float32), 'b_norm_in': jnp.zeros((DT,), jnp.float32), 'g_norm_out': jnp.ones((DT,), jnp.float32), 'b_norm_out': jnp.zeros((DT,), jnp.float32), 'g_ffn': jnp.ones((DT,), jnp.float32), 'b_ffn': jnp.zeros((DT,), jnp.float32), 'W1': jax.random.normal(ks[7], (DT, HID), jnp.float32) * s, 'b1': jnp.zeros((HID,), jnp.float32), 'W2': jax.random.normal(ks[8], (HID, DT), jnp.float32) * s, 'b2': jnp.zeros((DT,), jnp.float32), 'log_dt': jnp.log(0.001) + jax.random.uniform(ks[9], (DT,), jnp.float32) * (jnp.log(0.1) - jnp.log(0.001)), 'A_re': -0.5 * jnp.ones((DT, N_STATE), jnp.float32), 'A_im': jnp.tile(jnp.pi * jnp.arange(N_STATE, dtype=jnp.float32), (DT, 1)), 'C_re': jax.random.normal(ks[10], (DT, N_STATE), jnp.float32) * 0.5 ** 0.5, 'C_im': jax.random.normal(ks[11], (DT, N_STATE), jnp.float32) * 0.5 ** 0.5, 'D_skip': jax.random.normal(ks[12], (DT,), jnp.float32), 'mod_gate': jnp.array(0.5, jnp.float32)}
        return inp
    _L1_xattn_all = _L1_xattn_setup()
    _L1_xattn_in = {k: v for k, v in _L1_xattn_all.items() if k in ('Wq', 'Wk', 'Wv', 'W_film_in', 'b_film_in', 'W_film_out', 'b_film_out', 'g_norm_in', 'b_norm_in', 'g_norm_out', 'b_norm_out', 'g_ffn', 'b_ffn', 'W1', 'b1', 'W2', 'b2', 'log_dt', 'A_re', 'A_im', 'C_re', 'C_im', 'D_skip', 'mod_gate')}
    del _L1_xattn_all

    def _L1_ffn_setup():
        import jax, jax.numpy as jnp
        import numpy as np
        MAX_VAL = 100.0
        key = jax.random.key(seed)
        k1, k2, k3 = jax.random.split(key, 3)
        B, S, D_IN, D_OUT = (4, 2048, 256, 256)
        x = jax.random.normal(k1, (B, S, D_IN), dtype=jnp.float32)
        weights = jax.random.normal(k2, (D_OUT, D_IN), dtype=jnp.float32)
        scale = jnp.ones((D_OUT,), dtype=jnp.float32)
        bias = jax.random.normal(k3, (D_OUT,), dtype=jnp.float32)
        return {'x': x, 'weights': weights, 'scale': scale, 'bias': bias}
    _L1_ffn_all = _L1_ffn_setup()
    _L1_ffn_in = {k: v for k, v in _L1_ffn_all.items() if k in ('weights', 'scale', 'bias')}
    del _L1_ffn_all
    return {'x': x, 'ctx_768': ctx_768, 'mask_BxS2_bk0': mask_BxS2_bk0, 'mask_BxS_bf1': mask_BxS_bf1, 'mask_BxS2_bf1': mask_BxS2_bf1, 'L0_attn_W': _L0_attn_in['W'], 'L0_xattn_W_q': _L0_xattn_in['W_q'], 'L0_xattn_W_k': _L0_xattn_in['W_k'], 'L0_xattn_W_v': _L0_xattn_in['W_v'], 'L0_xattn_W_o': _L0_xattn_in['W_o'], 'L0_xattn_b_o': _L0_xattn_in['b_o'], 'L0_ffn_router_w': _L0_ffn_in['router_w'], 'L0_ffn_router_b': _L0_ffn_in['router_b'], 'L0_ffn_W1': _L0_ffn_in['W1'], 'L0_ffn_b1': _L0_ffn_in['b1'], 'L0_ffn_W2': _L0_ffn_in['W2'], 'L0_ffn_b2': _L0_ffn_in['b2'], 'L1_attn_ln1_g': _L1_attn_in['ln1_g'], 'L1_attn_ln1_b': _L1_attn_in['ln1_b'], 'L1_attn_ln2_g': _L1_attn_in['ln2_g'], 'L1_attn_ln2_b': _L1_attn_in['ln2_b'], 'L1_attn_time_mix_k': _L1_attn_in['time_mix_k'], 'L1_attn_time_mix_v': _L1_attn_in['time_mix_v'], 'L1_attn_time_mix_r': _L1_attn_in['time_mix_r'], 'L1_attn_time_decay': _L1_attn_in['time_decay'], 'L1_attn_time_first': _L1_attn_in['time_first'], 'L1_attn_Wk': _L1_attn_in['Wk'], 'L1_attn_Wv': _L1_attn_in['Wv'], 'L1_attn_Wr': _L1_attn_in['Wr'], 'L1_attn_Wo': _L1_attn_in['Wo'], 'L1_attn_cmix_k': _L1_attn_in['cmix_k'], 'L1_attn_cmix_r': _L1_attn_in['cmix_r'], 'L1_attn_Wck': _L1_attn_in['Wck'], 'L1_attn_Wcv': _L1_attn_in['Wcv'], 'L1_attn_Wcr': _L1_attn_in['Wcr'], 'L1_xattn_Wq': _L1_xattn_in['Wq'], 'L1_xattn_Wk': _L1_xattn_in['Wk'], 'L1_xattn_Wv': _L1_xattn_in['Wv'], 'L1_xattn_W_film_in': _L1_xattn_in['W_film_in'], 'L1_xattn_b_film_in': _L1_xattn_in['b_film_in'], 'L1_xattn_W_film_out': _L1_xattn_in['W_film_out'], 'L1_xattn_b_film_out': _L1_xattn_in['b_film_out'], 'L1_xattn_g_norm_in': _L1_xattn_in['g_norm_in'], 'L1_xattn_b_norm_in': _L1_xattn_in['b_norm_in'], 'L1_xattn_g_norm_out': _L1_xattn_in['g_norm_out'], 'L1_xattn_b_norm_out': _L1_xattn_in['b_norm_out'], 'L1_xattn_g_ffn': _L1_xattn_in['g_ffn'], 'L1_xattn_b_ffn': _L1_xattn_in['b_ffn'], 'L1_xattn_W1': _L1_xattn_in['W1'], 'L1_xattn_b1': _L1_xattn_in['b1'], 'L1_xattn_W2': _L1_xattn_in['W2'], 'L1_xattn_b2': _L1_xattn_in['b2'], 'L1_xattn_log_dt': _L1_xattn_in['log_dt'], 'L1_xattn_A_re': _L1_xattn_in['A_re'], 'L1_xattn_A_im': _L1_xattn_in['A_im'], 'L1_xattn_C_re': _L1_xattn_in['C_re'], 'L1_xattn_C_im': _L1_xattn_in['C_im'], 'L1_xattn_D_skip': _L1_xattn_in['D_skip'], 'L1_xattn_mod_gate': _L1_xattn_in['mod_gate'], 'L1_ffn_weights': _L1_ffn_in['weights'], 'L1_ffn_scale': _L1_ffn_in['scale'], 'L1_ffn_bias': _L1_ffn_in['bias']}

def reference(x, ctx_768, mask_BxS2_bk0, mask_BxS_bf1, mask_BxS2_bf1, L0_attn_W, L0_xattn_W_q, L0_xattn_W_k, L0_xattn_W_v, L0_xattn_W_o, L0_xattn_b_o, L0_ffn_router_w, L0_ffn_router_b, L0_ffn_W1, L0_ffn_b1, L0_ffn_W2, L0_ffn_b2, L1_attn_ln1_g, L1_attn_ln1_b, L1_attn_ln2_g, L1_attn_ln2_b, L1_attn_time_mix_k, L1_attn_time_mix_v, L1_attn_time_mix_r, L1_attn_time_decay, L1_attn_time_first, L1_attn_Wk, L1_attn_Wv, L1_attn_Wr, L1_attn_Wo, L1_attn_cmix_k, L1_attn_cmix_r, L1_attn_Wck, L1_attn_Wcv, L1_attn_Wcr, L1_xattn_Wq, L1_xattn_Wk, L1_xattn_Wv, L1_xattn_W_film_in, L1_xattn_b_film_in, L1_xattn_W_film_out, L1_xattn_b_film_out, L1_xattn_g_norm_in, L1_xattn_b_norm_in, L1_xattn_g_norm_out, L1_xattn_b_norm_out, L1_xattn_g_ffn, L1_xattn_b_ffn, L1_xattn_W1, L1_xattn_b1, L1_xattn_W2, L1_xattn_b2, L1_xattn_log_dt, L1_xattn_A_re, L1_xattn_A_im, L1_xattn_C_re, L1_xattn_C_im, L1_xattn_D_skip, L1_xattn_mod_gate, L1_ffn_weights, L1_ffn_scale, L1_ffn_bias):
    import jax
    import jax.numpy as jnp

    def _L0_attn_ref(repr, W):
        import jax, jax.numpy as jnp
        import numpy as np
        BATCH, SEQ, HIDDEN = (8, 512, 256)
        WSIZE = 64
        NEG_INF = -1000000000.0
        b, s, d = repr.shape
        idx = jnp.arange(s)
        mask = jnp.abs(idx[:, None] - idx[None, :]) > WSIZE
        scores = jnp.einsum('bqd,de,bke->bqk', repr, W, repr)
        scores = jnp.where(mask[None, :, :], NEG_INF, scores)
        probs = jax.nn.softmax(scores, axis=-1)
        ra = jnp.einsum('bqk,bkd->bqd', probs, repr)
        return repr + jax.nn.relu(ra)

    def _L0_xattn_ref(x, context, mask, W_q, W_k, W_v, W_o, b_o):
        import jax, jax.numpy as jnp
        import numpy as np
        HEADS = 8
        DIM_HEAD = 64
        QUERY_DIM = 256
        CONTEXT_DIM = 192
        INNER = HEADS * DIM_HEAD
        b, n, _ = x.shape
        j = context.shape[1]
        scale = DIM_HEAD ** (-0.5)
        q = (x @ W_q).reshape(b, n, HEADS, DIM_HEAD)
        k = (context @ W_k).reshape(b, j, HEADS, DIM_HEAD)
        v = (context @ W_v).reshape(b, j, HEADS, DIM_HEAD)
        sim = jnp.einsum('bihd,bjhd->bhij', q, k) * scale
        max_neg = -jnp.finfo(sim.dtype).max
        sim = jnp.where(mask[:, None, None, :], sim, max_neg)
        attn = jax.nn.softmax(sim, axis=-1)
        out = jnp.einsum('bhij,bjhd->bihd', attn, v).reshape(b, n, INNER)
        return out @ W_o + b_o

    def _L0_ffn_ref(x, router_w, router_b, W1, b1, W2, b2):
        import jax, jax.numpy as jnp
        import numpy as np
        B, L, D, F, E = (2, 256, 256, 1024, 8)
        b, l, d = x.shape
        xf = x.reshape(b * l, d)
        logits = xf @ router_w + router_b
        top1 = jnp.argmax(logits, axis=-1)
        h = jax.nn.gelu(jnp.einsum('td,edf->etf', xf, W1) + b1[:, None, :], approximate=False)
        y_all = jnp.einsum('etf,efd->etd', h, W2) + b2[:, None, :]
        onehot = jax.nn.one_hot(top1, E, dtype=x.dtype)
        yf = jnp.einsum('te,etd->td', onehot, y_all)
        return yf.reshape(b, l, d)

    def _L1_attn_ref(x, ln1_g, ln1_b, ln2_g, ln2_b, time_mix_k, time_mix_v, time_mix_r, time_decay, time_first, Wk, Wv, Wr, Wo, cmix_k, cmix_r, Wck, Wcv, Wcr):
        import jax, jax.numpy as jnp
        import numpy as np
        T, B, C = (256, 16, 256)
        FF = 4 * C

        def _ln(x, g, b):
            m = x.mean(-1, keepdims=True)
            v = jnp.var(x, axis=-1, keepdims=True)
            return (x - m) * jax.lax.rsqrt(v + 1e-05) * g + b

        def _wkv(w, u, k, v):
            b_, c_ = (k.shape[1], k.shape[2])
            init = (jnp.zeros((b_, c_), k.dtype), jnp.zeros((b_, c_), k.dtype), jnp.full((b_, c_), -1e+38, k.dtype))

            def step(carry, kv):
                aa, bb, pp = carry
                kt, vt = kv
                ww = u + kt
                qq = jnp.maximum(pp, ww)
                e1 = jnp.exp(pp - qq)
                e2 = jnp.exp(ww - qq)
                out = (e1 * aa + e2 * vt) / (e1 * bb + e2)
                ww2 = pp + w
                qq2 = jnp.maximum(ww2, kt)
                e1 = jnp.exp(ww2 - qq2)
                e2 = jnp.exp(kt - qq2)
                return ((e1 * aa + e2 * vt, e1 * bb + e2, qq2), out)
            _, out = jax.lax.scan(step, init, (k, v))
            return out

        def _shift(x):
            return jnp.concatenate([jnp.zeros_like(x[:1]), x[:-1]], axis=0)
        xx = _ln(x, ln1_g, ln1_b)
        xs = _shift(xx)
        k = jnp.einsum('tbc,oc->tbo', xx * time_mix_k + xs * (1 - time_mix_k), Wk)
        v = jnp.einsum('tbc,oc->tbo', xx * time_mix_v + xs * (1 - time_mix_v), Wv)
        r = jax.nn.sigmoid(jnp.einsum('tbc,oc->tbo', xx * time_mix_r + xs * (1 - time_mix_r), Wr))
        wkv = _wkv(-jnp.exp(time_decay), time_first, k, v)
        x = x + jnp.einsum('tbc,oc->tbo', r * wkv, Wo)
        yy = _ln(x, ln2_g, ln2_b)
        ys = _shift(yy)
        kk = jnp.einsum('tbc,fc->tbf', yy * cmix_k + ys * (1 - cmix_k), Wck)
        vv = jnp.einsum('tbf,of->tbo', jnp.square(jax.nn.relu(kk)), Wcv)
        rr = jax.nn.sigmoid(jnp.einsum('tbc,oc->tbo', yy * cmix_r + ys * (1 - cmix_r), Wcr))
        return x + rr * vv

    def _L1_xattn_ref(x_text, x_vision, text_mask, vision_mask, Wq, Wk, Wv, W_film_in, b_film_in, W_film_out, b_film_out, g_norm_in, b_norm_in, g_norm_out, b_norm_out, g_ffn, b_ffn, W1, b1, W2, b2, log_dt, A_re, A_im, C_re, C_im, D_skip, mod_gate):
        import jax, jax.numpy as jnp
        import numpy as np
        B, T, DT, G, DV = (16, 128, 256, 144, 192)
        H, DH = (4, 32)
        INNER = H * DH
        HID = 4 * DT
        N_STATE = 64
        K_TOP = 32

        def layernorm(x, g, b, eps=1e-05):
            m = x.mean(-1, keepdims=True)
            v = x.var(-1, keepdims=True)
            return (x - m) * jax.lax.rsqrt(v + eps) * g + b

        def s4d(x, log_dt, A_re, A_im, C_re, C_im, D_skip):
            Bb, L, D = x.shape
            dt = jnp.exp(log_dt)
            A = A_re + 1j * A_im
            C = C_re + 1j * C_im
            dtA = dt[:, None] * A
            dC = C * (jnp.exp(dtA) - 1.0) / A
            powers = jnp.exp(dtA[:, :, None] * jnp.arange(L))
            K = 2.0 * jnp.einsum('dn,dnl->dl', dC, powers).real
            n = 2 * L
            Kf = jnp.fft.rfft(K, n=n, axis=-1)
            xf = jnp.fft.rfft(x, n=n, axis=1)
            y = jnp.fft.irfft(xf * Kf.T[None], n=n, axis=1)[:, :L]
            return y + x * D_skip
        Bb, Tt, D = x_text.shape
        Gg = x_vision.shape[1]
        Q = (x_text @ Wq).reshape(Bb, Tt, H, DH)
        K = (x_vision @ Wk).reshape(Bb, Gg, H, DH)
        scores = jnp.einsum('bthd,bghd->bhtg', Q, K) / np.sqrt(DH).astype(np.float32)
        scores = jnp.where(vision_mask[:, None, None, :], scores, -jnp.inf)
        topv, topi = jax.lax.top_k(scores, K_TOP)
        probs = jax.nn.softmax(topv, axis=-1)
        bi = jnp.arange(Bb)[:, None, None, None]
        hi = jnp.arange(H)[None, :, None, None]
        ti = jnp.arange(Tt)[None, None, :, None]
        attn = jnp.zeros_like(scores).at[bi, hi, ti, topi].set(probs)
        attn_mean = attn.mean(axis=1)
        V = x_vision @ Wv
        c_t = jnp.einsum('btg,bgd->btd', attn_mean, V)
        c_t = c_t * text_mask[..., None]
        x = layernorm(x_text, g_norm_in, b_norm_in)
        scale_in, shift_in = jnp.split(c_t @ W_film_in + b_film_in, 2, axis=-1)
        x = x * (1.0 + mod_gate * scale_in) + mod_gate * shift_in
        y = s4d(x, log_dt, A_re, A_im, C_re, C_im, D_skip)
        scale_out, shift_out = jnp.split(c_t @ W_film_out + b_film_out, 2, axis=-1)
        y = y * (1.0 + mod_gate * scale_out) + mod_gate * shift_out
        xt = x_text + y
        h = layernorm(xt, g_ffn, b_ffn)
        h = jax.nn.gelu(h @ W1 + b1, approximate=False) @ W2 + b2
        xt = xt + h
        return layernorm(xt, g_norm_out, b_norm_out)

    def _L1_ffn_ref(x, weights, scale, bias):
        import jax, jax.numpy as jnp
        import numpy as np
        MAX_VAL = 100.0
        w = (weights >= 0.0).astype(x.dtype) * 2.0 - 1.0
        y = jnp.einsum('bsi,oi->bso', x, w)
        y = y * scale + bias
        y = jnp.clip(y, -MAX_VAL, MAX_VAL)
        return y
    x = x + _L0_attn_ref(_layernorm(x, axis=-1), L0_attn_W)
    x = x + _L0_xattn_ref(_layernorm(x, axis=-1), ctx_768, mask_BxS2_bk0, L0_xattn_W_q, L0_xattn_W_k, L0_xattn_W_v, L0_xattn_W_o, L0_xattn_b_o)
    x = x + _L0_ffn_ref(_layernorm(x, axis=-1), L0_ffn_router_w, L0_ffn_router_b, L0_ffn_W1, L0_ffn_b1, L0_ffn_W2, L0_ffn_b2)
    x = x + _L1_attn_ref(_layernorm(x, axis=-1), L1_attn_ln1_g, L1_attn_ln1_b, L1_attn_ln2_g, L1_attn_ln2_b, L1_attn_time_mix_k, L1_attn_time_mix_v, L1_attn_time_mix_r, L1_attn_time_decay, L1_attn_time_first, L1_attn_Wk, L1_attn_Wv, L1_attn_Wr, L1_attn_Wo, L1_attn_cmix_k, L1_attn_cmix_r, L1_attn_Wck, L1_attn_Wcv, L1_attn_Wcr)
    x = x + _L1_xattn_ref(_layernorm(x, axis=-1), ctx_768, mask_BxS_bf1, mask_BxS2_bf1, L1_xattn_Wq, L1_xattn_Wk, L1_xattn_Wv, L1_xattn_W_film_in, L1_xattn_b_film_in, L1_xattn_W_film_out, L1_xattn_b_film_out, L1_xattn_g_norm_in, L1_xattn_b_norm_in, L1_xattn_g_norm_out, L1_xattn_b_norm_out, L1_xattn_g_ffn, L1_xattn_b_ffn, L1_xattn_W1, L1_xattn_b1, L1_xattn_W2, L1_xattn_b2, L1_xattn_log_dt, L1_xattn_A_re, L1_xattn_A_im, L1_xattn_C_re, L1_xattn_C_im, L1_xattn_D_skip, L1_xattn_mod_gate)
    x = x + _L1_ffn_ref(_layernorm(x, axis=-1), L1_ffn_weights, L1_ffn_scale, L1_ffn_bias)
    return x

_drawn_inputs = setup_inputs


def setup_inputs(seed=0):
    import zlib

    import numpy as np

    out = dict(_drawn_inputs(seed))
    spreads = {'L1_attn_ln1_g': (1.0, 0.6),
     'L1_attn_ln1_b': (0.0, 0.472),
     'L1_attn_ln2_g': (1.0, 0.2),
     'L1_attn_ln2_b': (0.0, 0.388),
     'L1_xattn_b_film_in': (0.0, 0.503),
     'L1_xattn_b_film_out': (0.0, 0.651),
     'L1_xattn_g_norm_in': (1.0, 0.2),
     'L1_xattn_b_norm_in': (0.0, 0.317),
     'L1_xattn_g_norm_out': (1.0, 0.2),
     'L1_xattn_b_norm_out': (0.0, 0.31),
     'L1_xattn_g_ffn': (1.0, 0.6),
     'L1_xattn_b_ffn': (0.0, 0.8),
     'L1_xattn_b1': (0.0, 0.8),
     'L1_xattn_b2': (0.0, 2.0),
     'L1_xattn_A_re': (-0.5, 0.6),
     'L1_ffn_scale': (1.0, 0.2)}
    factors = {'L0_xattn_b_o': 3.206,
     'L0_ffn_b1': 8.0,
     'L0_ffn_b2': 6.189,
     'L1_attn_time_mix_r': 3.331,
     'L1_attn_time_decay': 8.0,
     'L1_attn_time_first': 8.0,
     'L1_xattn_Wq': 8.0,
     'L1_xattn_Wk': 8.0,
     'L1_xattn_Wv': 6.26,
     'L1_xattn_W_film_in': 7.901,
     'L1_xattn_W_film_out': 8.0,
     'L1_xattn_W1': 3.712,
     'L1_xattn_W2': 3.468}
    for name, (base, spread) in spreads.items():
        noise = np.random.default_rng([zlib.crc32(name.encode()), seed]).standard_normal(out[name].shape)
        drawn = base * np.exp(spread * noise) if base else spread * noise
        out[name] = jnp.asarray(drawn.astype(out[name].dtype))
    for name, factor in factors.items():
        out[name] = (out[name] * factor).astype(out[name].dtype)
    return out
```

```python
from contextlib import ExitStack

import numpy as np

import concourse.bass as bass
from concourse import mybir

F32 = mybir.dt.float32
I32 = mybir.dt.int32
U32 = mybir.dt.uint32
U8 = mybir.dt.uint8
ALU = mybir.AluOpType
ACT = mybir.ActivationFunctionType
AX = mybir.AxisListType

P = 128
B, S, D = 16, 256, 256
KD = D // P
NT = B * S // P
EPS = 1e-5
LOWEST = -3.4028234663852886e38


def done(i):
    return i + 2


def before(i):
    return i + 1


def settle(engine, s):
    engine.sem_inc(s["settled"], 1)


def semaphores(nc, ctx, prefix, names):
    sems = {n: nc.alloc_semaphore(f"{prefix}_{n}") for n in names.split()}

    def clear():
        nc.clear_and_free_semaphores(list(sems.values()))
        nc.all_engine_barrier()

    ctx.callback(clear)
    return sems


def give_credit(engine, sems):
    for s in sems.values():
        engine.sem_inc(s, 1)


def setup_constants(nc, args, X, k, lasting):
    with ExitStack() as ctx:
        s = semaphores(nc, ctx, "set", "zero ident eps load")
        block = ctx.enter_context(nc.Block())

        @block.sync
        def _(sp):
            for b in range(0, B, 4):
                sp.dma_start(X[:, 2 * b:2 * b + 8, :],
                             args["x"][b:b + 4].rearrange("b (s p) d -> p (b s) d", p=P)).then_inc(s["load"], 16)
            sp.wait_ge(s["load"], 16 * 4)

        @block.gpsimd
        def _(pool):
            nc.gpsimd.memset(k["zero"][:], 0.0).then_inc(s["zero"], 1)
            nc.gpsimd.memset(k["minus_half"][:], -0.5).then_inc(s["eps"], 1)
            pool.wait_ge(s["zero"], 1)
            nc.gpsimd.affine_select(out=k["ident"][:], in_=k["zero"][:], compare_op=ALU.not_equal, fill=1.0,
                                    base=0, pattern=[[-1, P]], channel_multiplier=1).then_inc(s["ident"], 1)
            pool.wait_ge(s["ident"], 1)


def norm_stats(nc, dve, s, x_tiles, st, mv, i):
    dve.wait_ge(s["rstd"], before(i))
    settle(dve, s)
    for t, x in enumerate(x_tiles):
        last = nc.vector.bn_stats(st[:, t, :], x)
    last.then_inc(s["stats"], 1)
    dve.wait_ge(s["stats"], done(i))
    settle(dve, s)
    for t in range(len(x_tiles)):
        last = nc.vector.bn_aggr(mv[:, t, :], st[:, t, :])
    last.then_inc(s["aggr"], 1)


def norm_rstd(nc, pool, s, mv, var, rstd, k, i):
    pool.wait_ge(s["aggr"], done(i))
    settle(pool, s)
    nc.gpsimd.tensor_scalar(var[:], mv[:, :, 1], EPS, None, ALU.add).then_inc(s["var"], 1)
    pool.wait_ge(s["var"], done(i))
    settle(pool, s)
    nc.gpsimd.tensor_tensor(rstd[:], var[:], k["minus_half"][:, 0:var.shape[1]], ALU.pow).then_inc(s["rstd"], 1)


NORM = "stats aggr var rstd"


def self_attention(nc, args, X, k):
    WINDOW = 64
    with ExitStack() as ctx:
        def sb(name, shape, dt=F32):
            return ctx.enter_context(nc.sbuf_tensor("A_" + name, shape, dt))

        def ps(name, shape):
            return ctx.enter_context(nc.psum_tensor("A_" + name, shape, F32))

        W = sb("W", [P, KD, D])
        band = sb("band", [P, 2, S])
        st, mv = sb("st", [P, 2, 6]), sb("mv", [P, 2, 2])
        var, rstd = sb("var", [P, 2]), sb("rstd", [P, 2])
        h, hT, qT = sb("h", [P, 2, D]), sb("hT", [P, KD, S]), sb("qT", [P, KD, S])
        sc, pr, prT = sb("sc", [P, 2, S]), sb("pr", [P, 2, S]), sb("prT", [P, 2, S])
        mx, nmx, sm, rs = sb("mx", [P, 2]), sb("nmx", [P, 2]), sb("sm", [P, 2]), sb("rs", [P, 2])
        ra = sb("ra", [P, 2, D])
        p_hT, p_q, p_s, p_prT, p_o = (ps(n, [P, 2, 256]) for n in ("phT", "pq", "ps", "pprT", "po"))
        s = semaphores(nc, ctx, "A", NORM + " settled h xh hTp hT qp q scp sc nmx pr rs prTp prT op ra xa")
        ld = semaphores(nc, ctx, "Ald", "w band")
        block = ctx.enter_context(nc.Block())

        @block.sync
        def _(sp):
            sp.dma_start(W[:], args["L0_attn_W"].rearrange("(k p) n -> p k n", p=P)).then_inc(ld["w"], 16)
            give_credit(sp, s)

        @block.gpsimd
        def _(pool):
            nc.gpsimd.memset(band[:], 0.0).then_inc(ld["band"], 1)
            pool.wait_ge(ld["band"], 1)
            nc.gpsimd.affine_select(out=band[:], in_=band[:], compare_op=ALU.is_ge, fill=-1e9, base=WINDOW,
                                    pattern=[[P, 2], [-1, S]], channel_multiplier=1).then_inc(ld["band"], 1)
            pool.wait_ge(ld["band"], 2)
            nc.gpsimd.affine_select(out=band[:], in_=band[:], compare_op=ALU.is_ge, fill=-1e9, base=WINDOW,
                                    pattern=[[-P, 2], [1, S]], channel_multiplier=-1).then_inc(ld["band"], 1)
            with pool.Fori(0, B) as i:
                x2 = X[:, bass.ds(2 * i, 2), :]
                norm_rstd(nc, pool, s, mv, var, rstd, k, i)
                pool.wait_ge(s["h"], done(i))
                settle(pool, s)
                nc.gpsimd.tensor_tensor(x2, x2, h[:], ALU.add).then_inc(s["xh"], 1)
                pool.wait_ge(s["xh"], done(i))
                pool.wait_ge(s["ra"], done(i))
                settle(pool, s)
                nc.gpsimd.tensor_tensor(x2, x2, ra[:], ALU.add).then_inc(s["xa"], 1)
            pool.wait_ge(s["xa"], done(B - 1))

        @block.vector
        def _(dve):
            dve.wait_ge(ld["band"], 3)
            with dve.Fori(0, B) as i:
                norm_stats(nc, dve, s, [X[:, 2 * i, :], X[:, 2 * i + 1, :]], st, mv, i)
                dve.wait_ge(s["rstd"], done(i))
                dve.wait_ge(s["op"], before(i))
                dve.wait_ge(s["xh"], before(i))
                for t in range(2):
                    last = nc.vector.tensor_scalar(h[:, t, :], X[:, 2 * i + t, :], mv[:, t, 0:1],
                                                   rstd[:, t:t + 1], ALU.subtract, ALU.mult)
                last.then_inc(s["h"], 1)
                dve.wait_ge(s["scp"], done(i))
                dve.wait_ge(s["pr"], before(i))
                settle(dve, s)
                for t in range(2):
                    last = nc.vector.tensor_tensor_reduce(sc[:, t, :], p_s[:, t, :], band[:, t, :], 1.0, LOWEST,
                                                          ALU.add, ALU.max, mx[:, t:t + 1])
                last.then_inc(s["sc"], 1)
                dve.wait_ge(s["sc"], done(i))
                nc.vector.tensor_scalar(nmx[:], mx[:], -1.0, None, ALU.mult).then_inc(s["nmx"], 1)
                dve.wait_ge(s["pr"], done(i))
                dve.wait_ge(s["ra"], before(i))
                nc.vector.reciprocal(rs[:], sm[:]).then_inc(s["rs"], 1)
                dve.wait_ge(s["prTp"], done(i))
                nc.vector.tensor_copy(prT[:], p_prT[:]).then_inc(s["prT"], 1)

        @block.scalar
        def _(act):
            with act.Fori(0, B) as i:
                act.wait_ge(s["hTp"], done(i))
                nc.scalar.activation(hT[:], p_hT[:], ACT.Copy).then_inc(s["hT"], 1)
                act.wait_ge(s["qp"], done(i))
                nc.scalar.activation(qT[:], p_q[:], ACT.Copy).then_inc(s["q"], 1)
                act.wait_ge(s["nmx"], done(i))
                act.wait_ge(s["prTp"], before(i))
                act.wait_ge(s["rs"], before(i))
                for t in range(2):
                    last = nc.scalar.activation(pr[:, t, :], sc[:, t, :], ACT.Exp, bias=nmx[:, t:t + 1],
                                                accum_out=sm[:, t:t + 1])
                last.then_inc(s["pr"], 1)
                act.wait_ge(s["op"], done(i))
                act.wait_ge(s["rs"], done(i))
                act.wait_ge(s["xa"], before(i))
                for t in range(2):
                    last = nc.scalar.activation(ra[:, t, :], p_o[:, t, :], ACT.Relu, scale=rs[:, t:t + 1])
                last.then_inc(s["ra"], 1)

        @block.tensor
        def _(pe):
            pe.wait_ge(ld["w"], 16)
            with pe.Fori(0, B) as i:
                pe.wait_ge(s["h"], done(i))
                pe.wait_ge(s["hT"], before(i))
                for t in range(2):
                    for kb in range(KD):
                        last = nc.tensor.transpose(p_hT[:, kb, t * P:(t + 1) * P], h[:, t, kb * P:(kb + 1) * P],
                                                   k["ident"][:])
                last.then_inc(s["hTp"], 1)
                pe.wait_ge(s["hT"], done(i))
                for e in range(KD):
                    for kb in range(KD):
                        last = nc.tensor.matmul(p_q[:, e, :], W[:, kb, e * P:(e + 1) * P], hT[:, kb, :],
                                                start=kb == 0, stop=kb == KD - 1)
                last.then_inc(s["qp"], 1)
                pe.wait_ge(s["q"], done(i))
                pe.wait_ge(s["sc"], before(i))
                for t in range(2):
                    for e in range(KD):
                        last = nc.tensor.matmul(p_s[:, t, :], qT[:, e, t * P:(t + 1) * P], hT[:, e, :],
                                                start=e == 0, stop=e == KD - 1)
                last.then_inc(s["scp"], 1)
                pe.wait_ge(s["pr"], done(i))
                pe.wait_ge(s["prT"], before(i))
                for t in range(2):
                    for kb in range(2):
                        last = nc.tensor.transpose(p_prT[:, kb, t * P:(t + 1) * P], pr[:, t, kb * P:(kb + 1) * P],
                                                   k["ident"][:])
                last.then_inc(s["prTp"], 1)
                pe.wait_ge(s["prT"], done(i))
                pe.wait_ge(s["ra"], before(i))
                for t in range(2):
                    for kb in range(2):
                        last = nc.tensor.matmul(p_o[:, t, :], prT[:, kb, t * P:(t + 1) * P], h[:, kb, :],
                                                start=kb == 0, stop=kb == 1)
                last.then_inc(s["op"], 1)


def cross_attention(nc, args, X, k):
    J, C, H, DH = 77, 192, 8, 64
    C1 = C - P
    INNER = H * DH
    MB = INNER // P
    with ExitStack() as ctx:
        def sb(name, shape, dt=F32):
            return ctx.enter_context(nc.sbuf_tensor("B_" + name, shape, dt))

        def ps(name, shape):
            return ctx.enter_context(nc.psum_tensor("B_" + name, shape, F32))

        Wq, Wo, bo = sb("Wq", [P, KD, INNER]), sb("Wo", [P, MB, D]), sb("bo", [P, 2, D])
        Wk, Wv = sb("Wk", [P, 2, INNER]), sb("Wv", [P, 2, INNER])
        mask, bias = sb("mask", [P, B * J], U8), sb("bias", [P, B, J])
        cx, cxT = sb("cx", [J, C]), sb("cxT", [P, 2, J])
        st, mv = sb("st", [P, 2, 6]), sb("mv", [P, 2, 2])
        var, rstd = sb("var", [P, 2]), sb("rstd", [P, 2])
        h, hT, qT = sb("h", [P, 2, D]), sb("hT", [P, KD, S]), sb("qT", [P, MB, S])
        kT, v = sb("kT", [P, MB, J]), sb("v", [J, INNER])
        sc, pr, prT = sb("sc", [P, 2, H, J]), sb("pr", [P, 2, H, J]), sb("prT", [J, 2, H, P])
        mx, sm, rs = sb("mx", [P, 2, H]), sb("sm", [P, 2, H]), sb("rs", [P, 2, H])
        av, aT = sb("av", [P, 2, INNER]), sb("aT", [P, 2, MB, P])
        p_hT = ps("phT", [P, 2, 256])
        p_q = ps("pq", [P, 2, 512])
        p_s = ps("ps", [P, 2, 512])
        p_k = ps("pk", [P, 512])
        p_av, p_o = ps("pav", [P, INNER]), ps("po", [P, 512])
        s = semaphores(nc, ctx, "B", NORM + " settled h xb hTp hT cxp cxT kp kT vp v qp q")
        t_ = semaphores(nc, ctx, "Bt", "settled simp sc mx sub pr sm rs prTp prT avp av aTp aT op x")
        ld = semaphores(nc, ctx, "Bld", "w mask")
        cxl = semaphores(nc, ctx, "B", "cxl")["cxl"]
        block = ctx.enter_context(nc.Block())

        @block.sync
        def _(sp):
            give_credit(sp, s)
            give_credit(sp, t_)
            sp.dma_start(mask[:], args["mask_BxS2_bk0"].rearrange("b j -> (b j)").partition_broadcast(P)).then_inc(ld["mask"], 16)
            sp.dma_start(Wk[:, 0, :], args["L0_xattn_W_k"][0:P]).then_inc(ld["w"], 16)
            sp.dma_start(Wk[0:C1, 1, :], args["L0_xattn_W_k"][P:C]).then_inc(ld["w"], 16)
            sp.dma_start(Wv[:, 0, :], args["L0_xattn_W_v"][0:P]).then_inc(ld["w"], 16)
            sp.dma_start(Wv[0:C1, 1, :], args["L0_xattn_W_v"][P:C]).then_inc(ld["w"], 16)
            sp.dma_start(Wq[:], args["L0_xattn_W_q"].rearrange("(k p) n -> p k n", p=P)).then_inc(ld["w"], 16)
            sp.dma_start(Wo[:], args["L0_xattn_W_o"].rearrange("(k p) n -> p k n", p=P)).then_inc(ld["w"], 16)
            for t in range(2):
                sp.dma_start(bo[:, t, :], args["L0_xattn_b_o"].partition_broadcast(P)).then_inc(ld["w"], 16)
            with sp.Fori(0, B) as i:
                sp.wait_ge(s["cxp"], before(i))
                sp.dma_start(cx[:], args["ctx_768"][bass.ds(i, 1)].rearrange("a j c -> (a j) c")).then_inc(cxl, 16)

        @block.gpsimd
        def _(pool):
            pool.wait_ge(ld["w"], 16 * 8)
            with pool.Fori(0, B) as i:
                norm_rstd(nc, pool, s, mv, var, rstd, k, i)
                x2 = X[:, bass.ds(2 * i, 2), :]
                pool.wait_ge(s["h"], done(i))
                settle(pool, s)
                nc.gpsimd.tensor_tensor(x2, x2, bo[:], ALU.add).then_inc(s["xb"], 1)

        @block.vector
        def _(dve):
            dve.wait_ge(ld["mask"], 16)
            nc.vector.tensor_scalar(bias[:].rearrange("p b j -> p (b j)"), mask[:], 1.0, -LOWEST,
                                    ALU.subtract, ALU.mult).then_inc(ld["mask"], 1)
            dve.wait_ge(ld["mask"], 17)
            with dve.Fori(0, B) as i:
                norm_stats(nc, dve, s, [X[:, 2 * i, :], X[:, 2 * i + 1, :]], st, mv, i)
                dve.wait_ge(s["rstd"], done(i))
                dve.wait_ge(s["hTp"], before(i))
                for t in range(2):
                    last = nc.vector.tensor_scalar(h[:, t, :], X[:, 2 * i + t, :], mv[:, t, 0:1],
                                                   rstd[:, t:t + 1], ALU.subtract, ALU.mult)
                last.then_inc(s["h"], 1)
                dve.wait_ge(s["kp"], done(i))
                nc.vector.tensor_copy(kT[:], p_k[:, 0:MB * J].rearrange("p (m j) -> p m j", m=MB)).then_inc(s["kT"], 1)
                for t in range(2):
                    n = 2 * i + t
                    dve.wait_ge(t_["simp"], done(n))
                    if t == 0:
                        dve.wait_ge(t_["pr"], before(n))
                    mb = bias[:, bass.ds(i, 1), :].to_broadcast([P, 4, J])
                    for g in range(2):
                        last = nc.vector.tensor_tensor(
                            sc[:, t].rearrange("p (m g) j -> p g m j", g=2)[:, g],
                            p_s[:, g, 0:4 * J].rearrange("p (h j) -> p h j", h=4), mb, ALU.add)
                    last.then_inc(t_["sc"], 1)
                    dve.wait_ge(t_["sc"], done(n))
                    nc.vector.tensor_reduce(mx[:, t, :], sc[:, t], AX.X, ALU.max).then_inc(t_["mx"], 1)
                    dve.wait_ge(t_["mx"], done(n))
                    nc.vector.tensor_tensor(sc[:, t], sc[:, t], mx[:, t, :].unsqueeze(2).to_broadcast([P, H, J]),
                                            ALU.subtract).then_inc(t_["sub"], 1)
                for t in range(2):
                    n = 2 * i + t
                    dve.wait_ge(t_["pr"], done(n))
                    nc.vector.tensor_reduce(sm[:, t, :], pr[:, t], AX.X, ALU.add).then_inc(t_["sm"], 1)
                    dve.wait_ge(t_["sm"], done(n))
                    nc.vector.reciprocal(rs[:, t, :], sm[:, t, :]).then_inc(t_["rs"], 1)
                for t in range(2):
                    n = 2 * i + t
                    dve.wait_ge(t_["rs"], done(n))
                    dve.wait_ge(t_["avp"], done(n))
                    if t == 0:
                        dve.wait_ge(t_["aTp"], before(n))
                    nc.vector.tensor_tensor(av[:, t, :].rearrange("p (h d) -> p h d", h=H),
                                            p_av[:].rearrange("p (h d) -> p h d", h=H),
                                            rs[:, t, :].unsqueeze(2).to_broadcast([P, H, DH]),
                                            ALU.mult).then_inc(t_["av"], 1)
                dve.wait_ge(s["xb"], done(i))
                for t in range(2):
                    n = 2 * i + t
                    dve.wait_ge(t_["op"], done(n))
                    xt = X[:, 2 * i + t, :]
                    nc.vector.tensor_tensor(xt, xt, p_o[:, t * D:(t + 1) * D], ALU.add).then_inc(t_["x"], 1)

        @block.scalar
        def _(act):
            with act.Fori(0, B) as i:
                act.wait_ge(s["cxp"], done(i))
                act.wait_ge(s["vp"], before(i))
                nc.scalar.activation(cxT[:, 0, :], p_hT[:, 0, 0:J], ACT.Copy)
                nc.scalar.activation(cxT[0:C1, 1, :], p_hT[0:C1, 1, 0:J], ACT.Copy).then_inc(s["cxT"], 1)
                act.wait_ge(s["hTp"], done(i))
                nc.scalar.activation(hT[:], p_hT[:], ACT.Copy).then_inc(s["hT"], 1)
                act.wait_ge(s["vp"], done(i))
                nc.scalar.activation(v[:], p_s[0:J, 0, :], ACT.Copy).then_inc(s["v"], 1)
                act.wait_ge(s["qp"], done(i))
                nc.scalar.activation(qT[:].rearrange("p (a b) c -> p a (b c)", a=2), p_q[:], ACT.Copy,
                                     scale=float(DH) ** -0.5).then_inc(s["q"], 1)
                for t in range(2):
                    n = 2 * i + t
                    act.wait_ge(t_["sub"], done(n))
                    act.wait_ge(t_["sm"], before(n))
                    nc.scalar.activation(pr[:, t], sc[:, t], ACT.Exp).then_inc(t_["pr"], 1)
                for t in range(2):
                    n = 2 * i + t
                    act.wait_ge(t_["prTp"], done(n))
                    if t == 0:
                        act.wait_ge(t_["avp"], before(n))
                    nc.scalar.activation(prT[:, t].rearrange("j (a b) q -> j a (b q)", a=2), p_q[0:J],
                                         ACT.Copy).then_inc(t_["prT"], 1)
                for t in range(2):
                    n = 2 * i + t
                    act.wait_ge(t_["aTp"], done(n))
                    if t == 0:
                        act.wait_ge(t_["op"], before(n))
                    nc.scalar.activation(aT[:, t], p_k[:].rearrange("p (m q) -> p m q", m=MB),
                                         ACT.Copy).then_inc(t_["aT"], 1)

        @block.tensor
        def _(pe):
            pe.wait_ge(ld["w"], 16 * 8)

            def transposed_probs(n, t):
                pe.wait_ge(t_["pr"], done(n))
                pe.wait_ge(t_["prT"], before(n))
                for hd in range(H):
                    last = nc.tensor.transpose(p_q[0:J, hd // 4, (hd % 4) * P:(hd % 4 + 1) * P], pr[:, t, hd, :],
                                               k["ident"][:])
                last.then_inc(t_["prTp"], 1)

            def head_outputs(n, t):
                pe.wait_ge(t_["prT"], done(n))
                pe.wait_ge(t_["av"], before(n))
                for hd in range(H):
                    last = nc.tensor.matmul(p_av[:, hd * DH:(hd + 1) * DH], prT[:, t, hd, :],
                                            v[:, hd * DH:(hd + 1) * DH], start=True, stop=True)
                last.then_inc(t_["avp"], 1)

            def transposed_outputs(n, t):
                pe.wait_ge(t_["av"], done(n))
                pe.wait_ge(t_["aT"], before(n))
                for m in range(MB):
                    last = nc.tensor.transpose(p_k[:, m * P:(m + 1) * P], av[:, t, m * P:(m + 1) * P],
                                               k["ident"][:])
                last.then_inc(t_["aTp"], 1)

            def project(n, t):
                pe.wait_ge(t_["aT"], done(n))
                pe.wait_ge(t_["x"], before(n))
                for m in range(MB):
                    last = nc.tensor.matmul(p_o[:, t * D:(t + 1) * D], aT[:, t, m, :], Wo[:, m, :],
                                            start=m == 0, stop=m == MB - 1)
                last.then_inc(t_["op"], 1)

            with pe.Fori(0, B) as i:
                pe.wait_ge(cxl, 16 * i + 16)
                pe.wait_ge(s["hT"], before(i))
                nc.tensor.transpose(p_hT[:, 0, 0:J], cx[:, 0:P], k["ident"][0:J, 0:J])
                nc.tensor.transpose(p_hT[0:C1, 1, 0:J], cx[:, P:C], k["ident"][0:J, 0:J]).then_inc(s["cxp"], 1)
                pe.wait_ge(s["h"], done(i))
                pe.wait_ge(s["cxT"], done(i))
                for t in range(2):
                    for kb in range(KD):
                        last = nc.tensor.transpose(p_hT[:, kb, t * P:(t + 1) * P], h[:, t, kb * P:(kb + 1) * P],
                                                   k["ident"][:])
                last.then_inc(s["hTp"], 1)
                pe.wait_ge(t_["aT"], before(2 * i))
                for m in range(MB):
                    for kb in range(2):
                        rows = P if kb == 0 else C1
                        last = nc.tensor.matmul(p_k[:, m * J:(m + 1) * J], Wk[0:rows, kb, m * P:(m + 1) * P],
                                                cxT[0:rows, kb, :], start=kb == 0, stop=kb == 1)
                last.then_inc(s["kp"], 1)
                pe.wait_ge(t_["sc"], before(2 * i))
                for kb in range(2):
                    rows = P if kb == 0 else C1
                    last = nc.tensor.matmul(p_s[0:J, 0, :], cxT[0:rows, kb, :], Wv[0:rows, kb, :],
                                            start=kb == 0, stop=kb == 1)
                last.then_inc(s["vp"], 1)
                pe.wait_ge(s["hT"], done(i))
                pe.wait_ge(t_["prT"], before(2 * i))
                for m in range(MB):
                    for kb in range(KD):
                        last = nc.tensor.matmul(p_q[:, m // 2, (m % 2) * S:(m % 2 + 1) * S],
                                                Wq[:, kb, m * P:(m + 1) * P], hT[:, kb, :],
                                                start=kb == 0, stop=kb == KD - 1)
                last.then_inc(s["qp"], 1)
                pe.wait_ge(s["q"], done(i))
                pe.wait_ge(s["kT"], done(i))
                pe.wait_ge(s["v"], done(i))
                for t in range(2):
                    n = 2 * i + t
                    if t:
                        pe.wait_ge(t_["sc"], before(n))
                    for hd in range(H):
                        r = DH * (hd % 2)
                        last = nc.tensor.matmul(p_s[:, hd % 2, (hd // 2) * J:(hd // 2 + 1) * J],
                                                qT[r:r + DH, hd // 2, t * P:(t + 1) * P], kT[r:r + DH, hd // 2, :],
                                                start=True, stop=True)
                    last.then_inc(t_["simp"], 1)
                transposed_probs(2 * i, 0)
                head_outputs(2 * i, 0)
                transposed_probs(2 * i + 1, 1)
                transposed_outputs(2 * i, 0)
                head_outputs(2 * i + 1, 1)
                project(2 * i, 0)
                transposed_outputs(2 * i + 1, 1)
                project(2 * i + 1, 1)


def experts(nc, args, X, k):
    E, F = 8, 1024
    BLOCKS = (B * S + E * (P - 1)) // P
    FB = F // P
    with ExitStack() as ctx:
        def sb(name, shape, dt=F32):
            return ctx.enter_context(nc.sbuf_tensor("C_" + name, shape, dt))

        place = sb("place", [P, NT], I32)
        owner = sb("owner", [P, BLOCKS], I32)
        xs_dram = nc.dram_tensor("sorted_x", (BLOCKS * P, D), F32).ap()
        ys_dram = nc.dram_tensor("sorted_y", (BLOCKS * P, D), F32).ap()
        with ExitStack() as weights:
            W1 = weights.enter_context(nc.sbuf_tensor("C_W1", [P, E, KD, F], F32))
            W2 = weights.enter_context(nc.sbuf_tensor("C_W2", [P, E, FB, D], F32))
            loaded = semaphores(nc, weights, "C", "loaded")["loaded"]
            route(nc, args, X, k, place, owner, xs_dram, W1, W2, loaded, E, F, BLOCKS)
            expert_blocks(nc, args, k, owner, xs_dram, ys_dram, W1, W2, loaded, E, F, BLOCKS)
        gather_rows(nc, X, place, ys_dram)


def route(nc, args, X, k, place, owner, xs_dram, W1, W2, loaded, E, F, BLOCKS):
    with ExitStack() as ctx:
        def sb(name, shape, dt=F32):
            return ctx.enter_context(nc.sbuf_tensor("R_" + name, shape, dt))

        def ps(name, shape):
            return ctx.enter_context(nc.psum_tensor("R_" + name, shape, F32))

        rw, rb = sb("rw", [P, KD, E]), sb("rb", [P, E])
        st, mv = sb("st", [P, 2, 6]), sb("mv", [P, 2, 2])
        var, rstd = sb("var", [P, 2]), sb("rstd", [P, 2])
        h, hT = sb("h", [P, 2, D]), sb("hT", [P, KD, S])
        lg, top, at, atf = sb("lg", [P, 2, E]), sb("top", [P, 2, 8]), sb("at", [P, 2, 8], U32), sb("atf", [P, 2])
        number = sb("number", [P, E])
        hot = sb("hot", [P, NT, E])
        ones, tri = sb("ones", [P, P]), sb("tri", [P, P])
        tot, cum, row = sb("tot", [P, NT, E]), sb("cum", [P, NT, E]), sb("row", [P, NT, E])
        nbi, nb, nbx, end = sb("nbi", [P, E], I32), sb("nb", [P, E]), sb("nbx", [P, E]), sb("end", [P, E])
        start = sb("start", [P, E])
        number_b, past = sb("number_b", [P, BLOCKS, E]), sb("past", [P, BLOCKS, E])
        placef, ownerf = sb("placef", [P, NT]), sb("ownerf", [P, BLOCKS])
        p_hT, p_lg = ps("phT", [P, 2, 256]), ps("plg", [P, 512])
        p_in, p_tot = ps("pin", [P, 512]), ps("ptot", [P, 512])
        s = semaphores(nc, ctx, "R", NORM + " settled h hTp hT lgp lg top at atf hot")
        c = semaphores(nc, ctx, "Rc", "number ones tri counts_in counts_tot tot cum step place owner zeroed scattered")
        ld = semaphores(nc, ctx, "R", "ld")["ld"]
        block = ctx.enter_context(nc.Block())

        @block.sync
        def _(sp):
            give_credit(sp, s)
            sp.dma_start(rw[:], args["L0_ffn_router_w"].rearrange("(k p) e -> p k e", p=P)).then_inc(ld, 16)
            sp.dma_start(rb[:], args["L0_ffn_router_b"].partition_broadcast(P)).then_inc(ld, 16)
            sp.dma_start(xs_dram.rearrange("(p b) d -> p (b d)", p=P).rearrange("p (c z) -> p c z", z=P),
                         k["zero"][:].unsqueeze(1).to_broadcast([P, 2 * BLOCKS, P])).then_inc(c["zeroed"], 16)
            for e in range(E):
                sp.dma_start(W1[:, e], args["L0_ffn_W1"][e].rearrange("(k p) f -> p k f", p=P)).then_inc(loaded, 16)
                sp.dma_start(W2[:, e], args["L0_ffn_W2"][e].rearrange("(k p) d -> p k d", p=P)).then_inc(loaded, 16)

        @block.gpsimd
        def _(pool):
            nc.gpsimd.iota(number[:], [[1, E]], base=0, channel_multiplier=0,
                           allow_small_or_imprecise_dtypes=True).then_inc(c["number"], 1)
            nc.gpsimd.iota(number_b[:], [[1, BLOCKS], [0, E]], base=0, channel_multiplier=0,
                           allow_small_or_imprecise_dtypes=True).then_inc(c["number"], 1)
            nc.gpsimd.memset(ones[:], 1.0).then_inc(c["ones"], 1)
            pool.wait_ge(c["ones"], 1)
            nc.gpsimd.affine_select(out=tri[:], in_=ones[:], compare_op=ALU.is_gt, fill=0.0, base=0,
                                    pattern=[[1, P]], channel_multiplier=-1).then_inc(c["tri"], 1)
            with pool.Fori(0, B) as i:
                norm_rstd(nc, pool, s, mv, var, rstd, k, i)
            pool.wait_ge(c["place"], 2)
            pool.wait_ge(c["zeroed"], 16)
            for n in range(NT):
                nc.gpsimd.indirect_dma_start(
                    out=xs_dram, out_offset=bass.IndirectOffsetOnAxis(ap=place[:, n:n + 1].bitcast(U32), axis=0),
                    in_=X[:, n, :], in_offset=None).then_inc(c["scattered"], 16)
            pool.wait_ge(c["scattered"], 16 * NT)

        @block.vector
        def _(dve):
            dve.wait_ge(ld, 32)
            dve.wait_ge(c["number"], 2)
            with dve.Fori(0, B) as i:
                norm_stats(nc, dve, s, [X[:, 2 * i, :], X[:, 2 * i + 1, :]], st, mv, i)
                dve.wait_ge(s["rstd"], done(i))
                dve.wait_ge(s["hTp"], before(i))
                for t in range(2):
                    last = nc.vector.tensor_scalar(h[:, t, :], X[:, 2 * i + t, :], mv[:, t, 0:1],
                                                   rstd[:, t:t + 1], ALU.subtract, ALU.mult)
                last.then_inc(s["h"], 1)
                dve.wait_ge(s["lgp"], done(i))
                nc.vector.tensor_tensor(lg[:], p_lg[:, 0:2 * E].rearrange("p (t e) -> p t e", t=2),
                                        rb[:].unsqueeze(1).to_broadcast([P, 2, E]), ALU.add).then_inc(s["lg"], 1)
                dve.wait_ge(s["lg"], done(i))
                settle(dve, s)
                for t in range(2):
                    last = nc.vector.max(top[:, t, :], lg[:, t, :])
                last.then_inc(s["top"], 1)
                dve.wait_ge(s["top"], done(i))
                settle(dve, s)
                for t in range(2):
                    last = nc.vector.max_index(at[:, t, :], top[:, t, :], lg[:, t, :])
                last.then_inc(s["at"], 1)
                dve.wait_ge(s["at"], done(i))
                nc.vector.tensor_copy(atf[:], at[:, :, 0]).then_inc(s["atf"], 1)
                dve.wait_ge(s["atf"], done(i))
                for t in range(2):
                    last = nc.vector.tensor_scalar(hot[:, 2 * i + t, :], number[:], atf[:, t:t + 1], None,
                                                   ALU.is_equal)
                last.then_inc(s["hot"], 1)
            steps = 0

            def step(instruction):
                nonlocal steps
                steps += 1
                instruction.then_inc(c["step"], 1)
                dve.wait_ge(c["step"], steps)

            dve.wait_ge(c["counts_tot"], 1)
            step(nc.vector.tensor_copy(tot[:], p_tot[:, 0:NT * E].rearrange("p (n e) -> p n e", e=E)))
            for e in range(E):
                last = nc.vector.tensor_tensor_scan(cum[:, :, e], ones[:, 0:NT], tot[:, :, e], 0.0, ALU.mult, ALU.add)
            step(last)
            step(nc.vector.tensor_scalar(nbx[:], cum[:, NT - 1, :], float(P - 1), 1.0 / P, ALU.add, ALU.mult))
            step(nc.vector.tensor_scalar(nbi[:], nbx[:], -(P - 1) / (2.0 * P), None, ALU.add))
            step(nc.vector.tensor_copy(nb[:], nbi[:]))
            step(nc.vector.tensor_tensor_scan(end[:], ones[:, 0:E], nb[:], 0.0, ALU.mult, ALU.add))
            step(nc.vector.tensor_tensor(start[:], end[:], nb[:], ALU.subtract))
            step(nc.vector.tensor_scalar(start[:], start[:], float(P), None, ALU.mult))
            step(nc.vector.tensor_tensor(row[:], cum[:], tot[:], ALU.subtract))
            step(nc.vector.tensor_tensor(row[:], row[:], p_in[:, 0:NT * E].rearrange("p (n e) -> p n e", e=E), ALU.add))
            step(nc.vector.tensor_tensor(row[:], row[:], start[:].unsqueeze(1).to_broadcast([P, NT, E]), ALU.add))
            step(nc.vector.tensor_tensor(row[:], row[:], hot[:], ALU.mult))
            nc.vector.tensor_reduce(placef[:], row[:], AX.X, ALU.add).then_inc(c["place"], 1)
            dve.wait_ge(c["place"], 1)
            nc.vector.tensor_copy(place[:], placef[:]).then_inc(c["place"], 1)
            step(nc.vector.tensor_tensor(past[:], number_b[:], end[:].unsqueeze(1).to_broadcast([P, BLOCKS, E]),
                                         ALU.is_ge))
            step(nc.vector.tensor_reduce(ownerf[:], past[:], AX.X, ALU.add))
            nc.vector.tensor_scalar(owner[:], ownerf[:], float(E - 1), None, ALU.min).then_inc(c["owner"], 1)
            dve.wait_ge(c["owner"], 1)

        @block.scalar
        def _(act):
            with act.Fori(0, B) as i:
                act.wait_ge(s["hTp"], done(i))
                act.wait_ge(s["lgp"], before(i))
                nc.scalar.activation(hT[:], p_hT[:], ACT.Copy).then_inc(s["hT"], 1)

        @block.tensor
        def _(pe):
            pe.wait_ge(ld, 32)
            with pe.Fori(0, B) as i:
                pe.wait_ge(s["h"], done(i))
                pe.wait_ge(s["hT"], before(i))
                for t in range(2):
                    for kb in range(KD):
                        last = nc.tensor.transpose(p_hT[:, kb, t * P:(t + 1) * P], h[:, t, kb * P:(kb + 1) * P],
                                                   k["ident"][:])
                last.then_inc(s["hTp"], 1)
                pe.wait_ge(s["hT"], done(i))
                pe.wait_ge(s["lg"], before(i))
                for t in range(2):
                    for kb in range(KD):
                        last = nc.tensor.matmul(p_lg[:, t * E:(t + 1) * E], hT[:, kb, t * P:(t + 1) * P],
                                                rw[:, kb, :], start=kb == 0, stop=kb == KD - 1)
                last.then_inc(s["lgp"], 1)
            pe.wait_ge(s["hot"], done(B - 1))
            pe.wait_ge(c["tri"], 1)
            every = hot[:].rearrange("p n e -> p (n e)")
            nc.tensor.matmul(p_in[:, 0:NT * E], tri[:], every, start=True, stop=True).then_inc(c["counts_in"], 1)
            nc.tensor.matmul(p_tot[:, 0:NT * E], ones[:], every, start=True, stop=True).then_inc(c["counts_tot"], 1)


def expert_blocks(nc, args, k, owner, xs_dram, ys_dram, W1, W2, loaded, E, F, BLOCKS):
    FB = F // P
    with ExitStack() as ctx:
        def sb(name, shape, dt=F32):
            return ctx.enter_context(nc.sbuf_tensor("F_" + name, shape, dt))

        def ps(name, shape):
            return ctx.enter_context(nc.psum_tensor("F_" + name, shape, F32))

        xs, b1, b2 = sb("xs", [P, D]), sb("b1", [P, F]), sb("b2", [P, D])
        st, mv = sb("st", [P, 1, 6]), sb("mv", [P, 1, 2])
        var, rstd = sb("var", [P, 1]), sb("rstd", [P, 1])
        h, hT = sb("h", [P, D]), sb("hT", [P, KD, P])
        u, uT, y = sb("u", [P, F]), sb("uT", [P, FB, P]), sb("y", [P, D])
        p_hT, p_u, p_uT, p_y = ps("phT", [P, 512]), ps("pu", [P, 2, 512]), ps("puT", [P, 2, 512]), ps("py", [P, 512])
        s = semaphores(nc, ctx, "F", NORM + " settled h hTp hT up u uTp uT yp y")
        dma = semaphores(nc, ctx, "Fd", "xs b1 b2 stored")
        block = ctx.enter_context(nc.Block())

        @block.sync
        def _(sp):
            give_credit(sp, s)
            sp.sem_inc(dma["stored"], 16)
            with sp.Fori(0, BLOCKS) as i:
                e = sp.value_load(owner[0:1, bass.ds(i, 1)], min_val=0, max_val=E - 1)
                sp.wait_ge(s["h"], before(i))
                sp.dma_start(xs[:], xs_dram[bass.ds(i * P, P)]).then_inc(dma["xs"], 16)
                sp.wait_ge(s["u"], before(i))
                sp.dma_start(b1[:], args["L0_ffn_b1"][bass.ds(e, 1)].rearrange("a f -> (a f)").partition_broadcast(P)
                             ).then_inc(dma["b1"], 16)
                sp.wait_ge(s["y"], before(i))
                sp.dma_start(b2[:], args["L0_ffn_b2"][bass.ds(e, 1)].rearrange("a f -> (a f)").partition_broadcast(P)
                             ).then_inc(dma["b2"], 16)

        @block.gpsimd
        def _(pool):
            with pool.Fori(0, BLOCKS) as i:
                norm_rstd(nc, pool, s, mv, var, rstd, k, i)

        @block.vector
        def _(dve):
            def normalise(i):
                dve.wait_ge(dma["xs"], 16 * i + 16)
                norm_stats(nc, dve, s, [xs[:]], st, mv, i)
                dve.wait_ge(s["rstd"], done(i))
                dve.wait_ge(s["hTp"], before(i))
                nc.vector.tensor_scalar(h[:], xs[:], mv[:, 0, 0:1], rstd[:, 0:1], ALU.subtract,
                                        ALU.mult).then_inc(s["h"], 1)

            def add_b1(i):
                dve.wait_ge(s["up"], done(i))
                dve.wait_ge(dma["b1"], 16 * i + 16)
                dve.wait_ge(s["uTp"], before(i))
                nc.vector.tensor_tensor(u[:].rearrange("p (a f) -> p a f", a=2), p_u[:],
                                        b1[:].rearrange("p (a f) -> p a f", a=2), ALU.add).then_inc(s["u"], 1)

            def add_b2(i):
                dve.wait_ge(s["yp"], done(i))
                dve.wait_ge(dma["b2"], 16 * i + 16)
                dve.wait_ge(dma["stored"], 16 * i + 16)
                nc.vector.tensor_tensor(y[:], p_y[:, 0:D], b2[:], ALU.add).then_inc(s["y"], 1)

            normalise(0)
            with dve.Fori(0, BLOCKS - 1) as i:
                add_b1(i)
                normalise(i + 1)
                add_b2(i)
            add_b1(BLOCKS - 1)
            add_b2(BLOCKS - 1)

        @block.scalar
        def _(act):
            def copy_hT(i):
                act.wait_ge(s["hTp"], done(i))
                act.wait_ge(s["up"], before(i))
                nc.scalar.activation(hT[:], p_hT[:, 0:D].rearrange("p (k q) -> p k q", k=KD),
                                     ACT.Copy).then_inc(s["hT"], 1)

            def gelu(i):
                act.wait_ge(s["uTp"], done(i))
                act.wait_ge(s["yp"], before(i))
                nc.scalar.activation(uT[:].rearrange("p (a b) q -> p a (b q)", a=2), p_uT[:],
                                     ACT.Gelu).then_inc(s["uT"], 1)

            def store(i):
                act.wait_ge(s["y"], done(i))
                act.dma_start(ys_dram[bass.ds(i * P, P)] if not isinstance(i, int) else ys_dram[i * P:(i + 1) * P],
                              y[:]).then_inc(dma["stored"], 16)

            copy_hT(0)
            with act.Fori(0, BLOCKS - 1) as i:
                gelu(i)
                copy_hT(i + 1)
                store(i)
            gelu(BLOCKS - 1)
            store(BLOCKS - 1)
            act.wait_ge(dma["stored"], 16 * (BLOCKS + 1))

        @block.tensor
        def _(pe):
            def first(i):
                pe.wait_ge(s["h"], done(i))
                pe.wait_ge(s["hT"], before(i))
                for kb in range(KD):
                    last = nc.tensor.transpose(p_hT[:, kb * P:(kb + 1) * P], h[:, kb * P:(kb + 1) * P], k["ident"][:])
                last.then_inc(s["hTp"], 1)
                e = pe.value_load(owner[0:1, bass.ds(i, 1)], min_val=0, max_val=E - 1)
                pe.wait_ge(s["hT"], done(i))
                pe.wait_ge(s["u"], before(i))
                for kb in range(KD):
                    for f in range(2):
                        last = nc.tensor.matmul(p_u[:, f, :], hT[:, kb, :],
                                                W1[:, bass.ds(e, 1), kb, f * 512:(f + 1) * 512],
                                                start=kb == 0, stop=kb == KD - 1)
                last.then_inc(s["up"], 1)

            def turn(i):
                pe.wait_ge(s["u"], done(i))
                pe.wait_ge(s["uT"], before(i))
                for f in range(FB):
                    last = nc.tensor.transpose(p_uT[:, f // 4, (f % 4) * P:(f % 4 + 1) * P],
                                               u[:, f * P:(f + 1) * P], k["ident"][:])
                last.then_inc(s["uTp"], 1)

            def second(i):
                e = pe.value_load(owner[0:1, bass.ds(i, 1)], min_val=0, max_val=E - 1)
                pe.wait_ge(s["uT"], done(i))
                pe.wait_ge(s["y"], before(i))
                for f in range(FB):
                    last = nc.tensor.matmul(p_y[:, 0:D], uT[:, f, :], W2[:, bass.ds(e, 1), f, :],
                                            start=f == 0, stop=f == FB - 1)
                last.then_inc(s["yp"], 1)

            pe.wait_ge(loaded, 32 * E)
            first(0)
            with pe.Fori(0, BLOCKS - 1) as i:
                turn(i)
                first(i + 1)
                second(i)
            turn(BLOCKS - 1)
            second(BLOCKS - 1)


def gather_rows(nc, X, place, ys_dram):
    with ExitStack() as ctx:
        y = ctx.enter_context(nc.sbuf_tensor("G_y", [P, NT, D], F32))
        fetched = list(semaphores(nc, ctx, "G", " ".join(f"fetched{n}" for n in range(NT))).values())
        block = ctx.enter_context(nc.Block())

        @block.gpsimd
        def _(pool):
            for n in range(NT):
                nc.gpsimd.indirect_dma_start(
                    out=y[:, n, :], out_offset=None, in_=ys_dram,
                    in_offset=bass.IndirectOffsetOnAxis(ap=place[:, n:n + 1].bitcast(U32), axis=0)
                ).then_inc(fetched[n], 16)

        @block.vector
        def _(dve):
            for n in range(NT):
                dve.wait_ge(fetched[n], 16)
                nc.vector.tensor_tensor(X[:, n, :], X[:, n, :], y[:, n, :], ALU.add)


def rwkv(nc, args, X, k):
    T, FF = B, 4 * D
    FB = FF // P
    COLUMNS = ("ln1_g", "ln1_b", "ln2_g", "ln2_b", "time_mix_k", "time_mix_v", "time_mix_r", "cmix_k", "cmix_r",
               "time_first", "time_decay")
    with ExitStack() as ctx:
        def sb(name, shape, dt=F32):
            return ctx.enter_context(nc.sbuf_tensor("D_" + name, shape, dt))

        def ps(name, shape):
            return ctx.enter_context(nc.psum_tensor("D_" + name, shape, F32))

        col = {c: sb(c, [P, KD]) for c in COLUMNS}
        decay = sb("decay", [P, KD])
        Wkvr, Wo = sb("Wkvr", [P, 3, KD, D]), sb("Wo", [P, KD, D])
        Wck, Wcv, Wcr = sb("Wck", [P, KD, FF]), sb("Wcv", [P, FB, D]), sb("Wcr", [P, KD, D])
        st, mv, var, rstd = sb("st", [P, 2, 6]), sb("mv", [P, 2, 2]), sb("var", [P, 2]), sb("rstd", [P, 2])
        v2, rstd2 = sb("v2", [P, 2]), sb("rstd2", [P, 2])
        st2, mv2, var2, rstd3 = sb("st2", [P, 2, 6]), sb("mv2", [P, 2, 2]), sb("var2", [P, 2]), sb("rstd3", [P, 2])
        h, n1, x1, n2 = (sb(n, [P, 2, D]) for n in ("h", "n1", "x1", "n2"))
        xx, xs, dx = (sb(n, [P, KD, S]) for n in ("xx", "xs", "dx"))
        yy, ys, dy = (sb(n, [P, KD, S]) for n in ("yy", "ys", "dy"))
        mix, cmix = sb("mix", [P, 3, KD, S]), sb("cmix", [P, 2, KD, S])
        key, val, gate = (sb(n, [P, KD, S]) for n in ("key", "val", "gate"))
        aa, bb, pp, ppn = (sb(n, [P, KD, S]) for n in ("aa", "bb", "pp", "ppn"))
        qq = sb("qq", [P, KD, S])
        d12, d34 = sb("d12", [P, 2, KD, S]), sb("d34", [P, 2, KD, S])
        e12, e34 = sb("e12", [P, 2, KD, S]), sb("e34", [P, 2, KD, S])
        num, nv, den, rw = (sb(n, [P, KD, S]) for n in ("num", "nv", "den", "rw"))
        av, bv = sb("av", [P, KD, S]), sb("bv", [P, KD, S])
        gate2, g2 = sb("gate2", [P, 2, D]), sb("g2", [P, 2, D])
        rl, kk = sb("rl", [P, 4, S]), sb("kk", [P, FB, S])
        p_T = ps("pT", [P, KD, S])
        p_kvr = ps("pkvr", [P, 3, KD, S])
        p_o = ps("po", [P, 2, D])
        p_kk, p_vv = ps("pkk", [P, 4, S]), ps("pvv", [P, 2, D])
        s = semaphores(nc, ctx, "D", NORM + " settled h v2a v2b v2 rstd2 n1 T1 xx dx mix xs kvr key val gate "
                       "qq d12 e12 ppn d34 e34 pp e1aa e2v num e1bb den inv nr rw e3aa av aa e3bb bb op x1")
        z = semaphores(nc, ctx, "Dc", NORM + " settled n2 T2 yy dy cmix ys rr gate2 kkp0 kkp1 rl0 rl1 kk0 kk1 vvp xx1 g2 x")
        ld = semaphores(nc, ctx, "Dld", "w cols exp decay init")
        block = ctx.enter_context(nc.Block())

        @block.sync
        def _(sp):
            give_credit(sp, s)
            give_credit(sp, z)
            with nc.allow_non_contiguous_dma(reason="a few columns of a value a channel"):
                for c in COLUMNS:
                    sp.dma_start(col[c][:], args["L1_attn_" + c].rearrange("(k p) -> p k", p=P)).then_inc(ld["cols"], 16)
            for m, w in enumerate(("Wk", "Wv", "Wr")):
                sp.dma_start(Wkvr[:, m], args["L1_attn_" + w].rearrange("(k p) o -> p k o", p=P)).then_inc(ld["w"], 16)
            for w, to in (("Wo", Wo), ("Wck", Wck), ("Wcv", Wcv), ("Wcr", Wcr)):
                sp.dma_start(to[:], args["L1_attn_" + w].rearrange("(k p) o -> p k o", p=P)).then_inc(ld["w"], 16)

        @block.gpsimd
        def _(pool):
            for x in (xs, ys, aa, bb):
                nc.gpsimd.memset(x[:], 0.0).then_inc(ld["init"], 1)
            nc.gpsimd.memset(pp[:], -1e38).then_inc(ld["init"], 1)
            pool.wait_ge(ld["init"], 5)

            def norm1(t):
                norm_rstd(nc, pool, s, mv, var, rstd, k, t)
                pool.wait_ge(s["rstd"], done(t))
                nc.gpsimd.tensor_tensor(v2[:], mv[:, :, 1], rstd[:], ALU.mult).then_inc(s["v2a"], 1)
                pool.wait_ge(s["v2a"], done(t))
                nc.gpsimd.tensor_tensor(v2[:], v2[:], rstd[:], ALU.mult).then_inc(s["v2b"], 1)
                pool.wait_ge(s["v2b"], done(t))
                settle(pool, s)
                nc.gpsimd.tensor_scalar(v2[:], v2[:], EPS, None, ALU.add).then_inc(s["v2"], 1)
                pool.wait_ge(s["v2"], done(t))
                pool.wait_ge(s["n1"], before(t))
                nc.gpsimd.tensor_tensor(rstd2[:], v2[:], k["minus_half"][:], ALU.pow).then_inc(s["rstd2"], 1)

            def keep_xx(t):
                pool.wait_ge(s["mix"], done(t))
                settle(pool, s)
                nc.gpsimd.tensor_copy(xs[:], xx[:]).then_inc(s["xs"], 1)

            def channel(t):
                norm_rstd(nc, pool, z, mv2, var2, rstd3, k, t)
                pool.wait_ge(z["cmix"], done(t))
                settle(pool, s)
                nc.gpsimd.tensor_copy(ys[:], yy[:]).then_inc(z["ys"], 1)

            def add_x1(t):
                x2 = X[:, bass.ds(2 * t, 2), :] if not isinstance(t, int) else X[:, 2 * t:2 * t + 2, :]
                pool.wait_ge(s["x1"], done(t))
                settle(pool, s)
                nc.gpsimd.tensor_tensor(x2, x2, x1[:], ALU.add).then_inc(z["xx1"], 1)

            def state(t):
                pool.wait_ge(s["e34"], done(t))
                pool.wait_ge(s["val"], done(t))
                nc.gpsimd.tensor_tensor(av[:], e34[:, 1], val[:], ALU.mult).then_inc(s["av"], 1)
                pool.wait_ge(s["e1bb"], done(t))
                nc.gpsimd.tensor_tensor(bb[:], e34[:, 0], bb[:], ALU.mult).then_inc(s["e3bb"], 1)
                pool.wait_ge(s["e1aa"], done(t))
                nc.gpsimd.tensor_tensor(aa[:], e34[:, 0], aa[:], ALU.mult).then_inc(s["e3aa"], 1)
                pool.wait_ge(s["e3bb"], done(t))
                nc.gpsimd.tensor_tensor(bb[:], bb[:], e34[:, 1], ALU.add).then_inc(s["bb"], 1)
                pool.wait_ge(s["e3aa"], done(t))
                pool.wait_ge(s["av"], done(t))
                nc.gpsimd.tensor_tensor(aa[:], aa[:], av[:], ALU.add).then_inc(s["aa"], 1)
                settle(pool, s)
                nc.gpsimd.tensor_copy(pp[:], ppn[:]).then_inc(s["pp"], 1)

            def round(t, last_t, next_t):
                if last_t is not None:
                    channel(last_t)
                    add_x1(last_t)
                state(t)
                if next_t is not None:
                    norm1(next_t)
                    keep_xx(next_t)

            norm1(0)
            keep_xx(0)
            round(0, None, 1)
            with pool.Fori(1, T - 1) as t:
                round(t, t - 1, t + 1)
            round(T - 1, T - 2, None)
            channel(T - 1)
            add_x1(T - 1)

        @block.vector
        def _(dve):
            dve.wait_ge(ld["exp"], 1)
            nc.vector.tensor_scalar(decay[:], decay[:], -1.0, None, ALU.mult).then_inc(ld["decay"], 1)
            dve.wait_ge(ld["decay"], 1)
            dve.wait_ge(ld["init"], 5)

            def norm1(t):
                norm_stats(nc, dve, s, [X[:, 2 * t, :], X[:, 2 * t + 1, :]], st, mv, t)
                dve.wait_ge(s["rstd"], done(t))
                dve.wait_ge(s["x1"], before(t))
                for a in range(2):
                    last = nc.vector.tensor_scalar(h[:, a, :], X[:, 2 * t + a, :], mv[:, a, 0:1], rstd[:, a:a + 1],
                                                   ALU.subtract, ALU.mult)
                last.then_inc(s["h"], 1)
                dve.wait_ge(s["h"], done(t))
                dve.wait_ge(s["rstd2"], done(t))
                dve.wait_ge(s["T1"], before(t))
                for a in range(2):
                    last = nc.vector.tensor_scalar(n1[:, a, :], h[:, a, :], rstd2[:, a:a + 1], None, ALU.mult)
                last.then_inc(s["n1"], 1)

            def mixes(t):
                dve.wait_ge(s["xx"], done(t))
                dve.wait_ge(s["xs"], before(t))
                nc.vector.tensor_tensor(dx[:], xx[:], xs[:], ALU.subtract).then_inc(s["dx"], 1)
                dve.wait_ge(s["dx"], done(t))
                dve.wait_ge(s["kvr"], before(t))
                for m, c in enumerate(("time_mix_k", "time_mix_v", "time_mix_r")):
                    for kb in range(KD):
                        last = nc.vector.scalar_tensor_tensor(
                            out=mix[:, m, kb, :], in0=dx[:, kb, :], scalar=col[c][:, kb:kb + 1], in1=xs[:, kb, :],
                            op0=ALU.mult, op1=ALU.add)
                last.then_inc(s["mix"], 1)

            def wkv(t):
                dve.wait_ge(s["key"], done(t))
                dve.wait_ge(s["pp"], before(t))
                for kb in range(KD):
                    last = nc.vector.scalar_tensor_tensor(
                        out=qq[:, kb, :], in0=key[:, kb, :], scalar=col["time_first"][:, kb:kb + 1],
                        in1=pp[:, kb, :], op0=ALU.add, op1=ALU.max)
                last.then_inc(s["qq"], 1)
                for kb in range(KD):
                    last = nc.vector.scalar_tensor_tensor(
                        out=ppn[:, kb, :], in0=pp[:, kb, :], scalar=decay[:, kb:kb + 1], in1=key[:, kb, :],
                        op0=ALU.add, op1=ALU.max)
                last.then_inc(s["ppn"], 1)
                dve.wait_ge(s["qq"], done(t))
                dve.wait_ge(s["e12"], before(t))
                nc.vector.tensor_tensor(d12[:, 0], pp[:], qq[:], ALU.subtract)
                for kb in range(KD):
                    last = nc.vector.scalar_tensor_tensor(
                        out=d12[:, 1, kb, :], in0=key[:, kb, :], scalar=col["time_first"][:, kb:kb + 1],
                        in1=qq[:, kb, :], op0=ALU.add, op1=ALU.subtract)
                last.then_inc(s["d12"], 1)
                dve.wait_ge(s["ppn"], done(t))
                dve.wait_ge(s["e34"], before(t))
                nc.vector.tensor_tensor(d34[:, 1], key[:], ppn[:], ALU.subtract)
                for kb in range(KD):
                    last = nc.vector.scalar_tensor_tensor(
                        out=d34[:, 0, kb, :], in0=pp[:, kb, :], scalar=decay[:, kb:kb + 1],
                        in1=ppn[:, kb, :], op0=ALU.add, op1=ALU.subtract)
                last.then_inc(s["d34"], 1)
                dve.wait_ge(s["e12"], done(t))
                dve.wait_ge(s["bb"], before(t))
                nc.vector.tensor_tensor(den[:], e12[:, 0], bb[:], ALU.mult).then_inc(s["e1bb"], 1)
                dve.wait_ge(s["aa"], before(t))
                nc.vector.tensor_tensor(num[:], e12[:, 0], aa[:], ALU.mult).then_inc(s["e1aa"], 1)
                dve.wait_ge(s["e1bb"], done(t))
                nc.vector.tensor_tensor(den[:], den[:], e12[:, 1], ALU.add).then_inc(s["den"], 1)
                dve.wait_ge(s["val"], done(t))
                nc.vector.tensor_tensor(nv[:], e12[:, 1], val[:], ALU.mult).then_inc(s["e2v"], 1)
                dve.wait_ge(s["den"], done(t))
                nc.vector.reciprocal(den[:], den[:]).then_inc(s["inv"], 1)
                dve.wait_ge(s["e1aa"], done(t))
                dve.wait_ge(s["e2v"], done(t))
                nc.vector.tensor_tensor(num[:], num[:], nv[:], ALU.add).then_inc(s["num"], 1)
                dve.wait_ge(s["inv"], done(t))
                dve.wait_ge(s["num"], done(t))
                nc.vector.tensor_tensor(num[:], num[:], den[:], ALU.mult).then_inc(s["nr"], 1)
                dve.wait_ge(s["nr"], done(t))
                dve.wait_ge(s["gate"], done(t))
                dve.wait_ge(s["op"], before(t))
                nc.vector.scalar_tensor_tensor(out=rw[:], in0=gate[:], scalar=1.0, in1=num[:], op0=ALU.add,
                                               op1=ALU.mult).then_inc(s["rw"], 1)

            def residual(t):
                dve.wait_ge(s["op"], done(t))
                dve.wait_ge(z["xx1"], before(t))
                dve.wait_ge(z["n2"], before(t))
                nc.vector.scalar_tensor_tensor(out=x1[:], in0=p_o[:], scalar=0.5, in1=h[:], op0=ALU.mult,
                                               op1=ALU.add).then_inc(s["x1"], 1)

            def channel(t):
                dve.wait_ge(s["x1"], done(t))
                norm_stats(nc, dve, z, [x1[:, 0, :], x1[:, 1, :]], st2, mv2, t)
                dve.wait_ge(z["rstd"], done(t))
                dve.wait_ge(z["T2"], before(t))
                for a in range(2):
                    last = nc.vector.tensor_scalar(n2[:, a, :], x1[:, a, :], mv2[:, a, 0:1], rstd3[:, a:a + 1],
                                                   ALU.subtract, ALU.mult)
                last.then_inc(z["n2"], 1)
                dve.wait_ge(z["yy"], done(t))
                dve.wait_ge(z["ys"], before(t))
                nc.vector.tensor_tensor(dy[:], yy[:], ys[:], ALU.subtract).then_inc(z["dy"], 1)
                dve.wait_ge(z["dy"], done(t))
                dve.wait_ge(z["vvp"], before(t))
                for m, c in enumerate(("cmix_k", "cmix_r")):
                    for kb in range(KD):
                        last = nc.vector.scalar_tensor_tensor(
                            out=cmix[:, m, kb, :], in0=dy[:, kb, :], scalar=col[c][:, kb:kb + 1], in1=ys[:, kb, :],
                            op0=ALU.mult, op1=ALU.add)
                last.then_inc(z["cmix"], 1)

            def finish(t):
                x2 = X[:, bass.ds(2 * t, 2), :] if not isinstance(t, int) else X[:, 2 * t:2 * t + 2, :]
                dve.wait_ge(z["vvp"], done(t))
                dve.wait_ge(z["gate2"], done(t))
                nc.vector.scalar_tensor_tensor(out=g2[:], in0=gate2[:], scalar=1.0, in1=p_vv[:], op0=ALU.add,
                                               op1=ALU.mult).then_inc(z["g2"], 1)
                dve.wait_ge(z["g2"], done(t))
                dve.wait_ge(z["xx1"], done(t))
                nc.vector.scalar_tensor_tensor(out=x2, in0=g2[:], scalar=0.5, in1=x2, op0=ALU.mult,
                                               op1=ALU.add).then_inc(z["x"], 1)

            def round(t, last_t, next_t):
                if last_t is not None:
                    channel(last_t)
                wkv(t)
                if last_t is not None:
                    finish(last_t)
                residual(t)
                if next_t is not None:
                    norm1(next_t)
                    mixes(next_t)

            norm1(0)
            mixes(0)
            round(0, None, 1)
            with dve.Fori(1, T - 1) as t:
                round(t, t - 1, t + 1)
            round(T - 1, T - 2, None)
            channel(T - 1)
            finish(T - 1)

        @block.scalar
        def _(act):
            act.wait_ge(ld["cols"], 16 * len(COLUMNS))
            nc.scalar.activation(decay[:], col["time_decay"][:], ACT.Exp).then_inc(ld["exp"], 1)

            def copy_xx(t):
                act.wait_ge(s["T1"], done(t))
                act.wait_ge(s["xs"], before(t))
                for kb in range(KD):
                    last = nc.scalar.activation(xx[:, kb, :], p_T[:, kb, :], ACT.Identity,
                                                bias=col["ln1_b"][:, kb:kb + 1], scale=col["ln1_g"][:, kb:kb + 1])
                last.then_inc(s["xx"], 1)

            def copy_yy(t):
                act.wait_ge(z["T2"], done(t))
                act.wait_ge(z["ys"], before(t))
                for kb in range(KD):
                    last = nc.scalar.activation(yy[:, kb, :], p_T[:, kb, :], ACT.Identity,
                                                bias=col["ln2_b"][:, kb:kb + 1], scale=col["ln2_g"][:, kb:kb + 1])
                last.then_inc(z["yy"], 1)

            def copy_kvr(t):
                act.wait_ge(s["kvr"], done(t))
                act.wait_ge(s["d34"], before(t))
                nc.scalar.activation(key[:], p_kvr[:, 0], ACT.Copy).then_inc(s["key"], 1)
                act.wait_ge(s["av"], before(t))
                act.wait_ge(s["e2v"], before(t))
                nc.scalar.activation(val[:], p_kvr[:, 1], ACT.Copy).then_inc(s["val"], 1)
                act.wait_ge(s["rw"], before(t))
                nc.scalar.activation(gate[:], p_kvr[:, 2], ACT.Tanh, scale=0.5).then_inc(s["gate"], 1)

            def exps(t):
                act.wait_ge(s["d12"], done(t))
                act.wait_ge(s["nr"], before(t))
                nc.scalar.activation(e12[:], d12[:], ACT.Exp).then_inc(s["e12"], 1)
                act.wait_ge(s["d34"], done(t))
                act.wait_ge(s["aa"], before(t))
                nc.scalar.activation(e34[:], d34[:], ACT.Exp).then_inc(s["e34"], 1)

            def gate_channel(t):
                act.wait_ge(z["rr"], done(t))
                act.wait_ge(z["g2"], before(t))
                nc.scalar.activation(gate2[:], p_o[:], ACT.Tanh, scale=0.5).then_inc(z["gate2"], 1)

            def squares(t):
                for half in range(2):
                    act.wait_ge(z[f"kkp{half}"], done(t))
                    if half:
                        act.wait_ge(z["kk0"], done(t))
                    else:
                        act.wait_ge(z["kk1"], before(t))
                    nc.scalar.activation(rl[:], p_kk[:], ACT.Relu).then_inc(z[f"rl{half}"], 1)
                    act.wait_ge(z[f"rl{half}"], done(t))
                    act.wait_ge(z["vvp"], before(t))
                    nc.scalar.activation(kk[:, 4 * half:4 * half + 4, :], rl[:], ACT.Square).then_inc(z[f"kk{half}"], 1)

            def round(t, last_t, next_t):
                if last_t is not None:
                    copy_yy(last_t)
                copy_kvr(t)
                exps(t)
                if last_t is not None:
                    gate_channel(last_t)
                    squares(last_t)
                if next_t is not None:
                    copy_xx(next_t)

            copy_xx(0)
            round(0, None, 1)
            with act.Fori(1, T - 1) as t:
                round(t, t - 1, t + 1)
            round(T - 1, T - 2, None)
            copy_yy(T - 1)
            gate_channel(T - 1)
            squares(T - 1)

        @block.tensor
        def _(pe):
            pe.wait_ge(ld["w"], 16 * 7)

            def transposes(out, x):
                for a in range(2):
                    for kb in range(KD):
                        last = nc.tensor.transpose(out[:, kb, a * P:(a + 1) * P], x[:, a, kb * P:(kb + 1) * P],
                                                   k["ident"][:])
                return last

            def turn_n1(t, last_t):
                pe.wait_ge(s["n1"], done(t))
                if last_t is not None:
                    pe.wait_ge(z["yy"], done(last_t))
                else:
                    pe.wait_ge(s["xx"], before(t))
                transposes(p_T, n1).then_inc(s["T1"], 1)

            def kvr(t):
                pe.wait_ge(s["mix"], done(t))
                pe.wait_ge(s["gate"], before(t))
                for m in range(3):
                    for o in range(KD):
                        for kb in range(KD):
                            last = nc.tensor.matmul(p_kvr[:, m, o, :], Wkvr[:, m, kb, o * P:(o + 1) * P],
                                                    mix[:, m, kb, :], start=kb == 0, stop=kb == KD - 1)
                last.then_inc(s["kvr"], 1)

            def out_product(t, last_t):
                pe.wait_ge(s["rw"], done(t))
                if last_t is not None:
                    pe.wait_ge(z["gate2"], done(last_t))
                for a in range(2):
                    for kb in range(KD):
                        last = nc.tensor.matmul(p_o[:, a, :], rw[:, kb, a * P:(a + 1) * P], Wo[:, kb, :],
                                                start=kb == 0, stop=kb == KD - 1)
                last.then_inc(s["op"], 1)

            def channel(t, xx_t):
                pe.wait_ge(z["n2"], done(t))
                pe.wait_ge(s["xx"], done(xx_t))
                transposes(p_T, n2).then_inc(z["T2"], 1)
                pe.wait_ge(z["cmix"], done(t))
                for a in range(2):
                    for kb in range(KD):
                        last = nc.tensor.matmul(p_o[:, a, :], cmix[:, 1, kb, a * P:(a + 1) * P], Wcr[:, kb, :],
                                                start=kb == 0, stop=kb == KD - 1)
                last.then_inc(z["rr"], 1)
                for half in range(2):
                    if half:
                        pe.wait_ge(z["rl0"], done(t))
                    else:
                        pe.wait_ge(z["rl1"], before(t))
                    for f in range(4):
                        for kb in range(KD):
                            fb = 4 * half + f
                            last = nc.tensor.matmul(p_kk[:, f, :], Wck[:, kb, fb * P:(fb + 1) * P],
                                                    cmix[:, 0, kb, :], start=kb == 0, stop=kb == KD - 1)
                    last.then_inc(z[f"kkp{half}"], 1)
                pe.wait_ge(z["kk1"], done(t))
                pe.wait_ge(z["g2"], before(t))
                for a in range(2):
                    for fb in range(FB):
                        last = nc.tensor.matmul(p_vv[:, a, :], kk[:, fb, a * P:(a + 1) * P], Wcv[:, fb, :],
                                                start=fb == 0, stop=fb == FB - 1)
                last.then_inc(z["vvp"], 1)

            def round(t, last_t, next_t):
                if last_t is not None:
                    channel(last_t, t)
                out_product(t, last_t)
                if next_t is not None:
                    turn_n1(next_t, last_t)
                    kvr(next_t)

            turn_n1(0, None)
            kvr(0)
            round(0, None, 1)
            with pe.Fori(1, T - 1) as t:
                round(t, t - 1, t + 1)
            round(T - 1, T - 2, None)
            channel(T - 1, T - 1)


def ssm_spectrum(nc, args, k, w, fourier, C, INNER):
    N, NA, NC = 64, 32, 8
    C1 = C - P
    G4, Q4 = 32, 4
    TWO_PI = 2.0 * np.pi
    PI_1 = 6.28125
    PI_2 = float(np.float32(np.round((TWO_PI - PI_1) * 2 ** 21) / 2 ** 21))
    PI_3 = float(TWO_PI - PI_1 - PI_2)
    F2 = 2 * D
    with ExitStack() as ctx:
        def sb(name, shape, dt=F32):
            return ctx.enter_context(nc.sbuf_tensor("K_" + name, shape, dt))

        def ps(name, shape):
            return ctx.enter_context(nc.psum_tensor("K_" + name, shape, F32))

        small = {n: sb(n, [P, P]) for n in ("ldt", "Are", "Aim", "Cre", "Cim", "dt", "ar", "ai", "turns", "r", "rc",
                                            "mag", "sin", "cos", "pm", "nre", "nim", "a2", "t1", "t2")}
        turns_i = sb("turns_i", [P, P], I32)
        pw = sb("pw", [P, 2, G4, Q4, NC + 1])
        gp = sb("gp", [P, 2, G4, Q4, NA])
        base = sb("base", [P, 2, G4, Q4])
        t4 = sb("t4", [P, 4, G4, Q4, NA // 2])
        Ks = sb("Ks", [P, NC, 2, G4])
        KT, skip = sb("KT", [P, 2, D]), sb("skip", [1, D])
        WvT, Wf = sb("WvT", [P, KD, C]), sb("Wf", [P, KD, 2 * F2])
        row = sb("row", [1, 2 * F2])
        kdram = nc.dram_tensor("ssm_kernel", (S, D), F32).ap()
        p_K = ps("pK", [P, 2, 2, 16, Q4, NC])
        p_f, p_v = ps("pf", [P, 4, D]), ps("pv", [P, 2, 512])
        c = semaphores(nc, ctx, "K", "load w act step kp ks stored again spec vf done")
        block = ctx.enter_context(nc.Block())

        @block.sync
        def _(sp):
            for half in range(2):
                rows = slice(N * half, N * half + N)
                cols = slice(P * half, P * half + P)
                for n in ("A_re", "A_im", "C_re", "C_im"):
                    sp.dma_start(small[n.replace("_", "")][rows, :], args["L1_xattn_" + n][:, cols]).then_inc(c["load"], 16)
                sp.dma_start(small["ldt"][rows, :], args["L1_xattn_log_dt"][cols].partition_broadcast(N)).then_inc(c["load"], 16)
            sp.dma_start(skip[:], args["L1_xattn_D_skip"].rearrange("(a d) -> a d", a=1)).then_inc(c["w"], 16)
            sp.dma_start(WvT[:], args["L1_xattn_Wv"].rearrange("(k p) c -> p k c", p=P)).then_inc(c["w"], 16)
            for j, n in enumerate(("film_in", "film_out")):
                sp.dma_start(Wf[:, :, j * F2:(j + 1) * F2],
                             args["L1_xattn_W_" + n].rearrange("(k p) f -> p k f", p=P)).then_inc(c["w"], 16)
                sp.dma_start(row[:, j * F2:(j + 1) * F2],
                             args["L1_xattn_b_" + n].rearrange("(a f) -> a f", a=1)).then_inc(c["w"], 16)
            sp.dma_start(w["gate"][:], args["L1_xattn_mod_gate"].partition_broadcast(P)).then_inc(c["w"], 16)
            sp.dma_start(fourier["fwd"][:], args["fourier"].rearrange("(k p) f -> p k f", p=P)).then_inc(c["w"], 16)
            sp.dma_start(w["sign"][:], args["L1_ffn_weights"].rearrange("(k p) o -> p k o", p=P)).then_inc(c["w"], 16)
            sp.wait_ge(c["ks"], 8)
            for q in range(Q4):
                sp.dma_start(kdram.rearrange("(a c) (h q g) -> q a c h g", c=NC, h=2, q=Q4)[q],
                             Ks[32 * q:32 * q + 32]).then_inc(c["stored"], 16)
            sp.wait_ge(c["stored"], 16 * Q4)
            sp.dma_start(KT[:], kdram.rearrange("(k p) d -> p k d", p=P)).then_inc(c["again"], 16)
            sp.wait_ge(c["done"], 1)
            sp.dma_start(w["VW"][77:78, :], row[:]).then_inc(c["stored"], 16)
            sp.wait_ge(c["stored"], 16 * (Q4 + 1))

        @block.vector
        def _(dve):
            steps = 0

            def step(instruction):
                nonlocal steps
                steps += 1
                instruction.then_inc(c["step"], 1)
                dve.wait_ge(c["step"], steps)

            v = nc.vector
            m = {n: t[:] for n, t in small.items()}
            dve.wait_ge(c["load"], 160)
            dve.wait_ge(c["act"], 1)
            step(v.tensor_tensor(m["ar"], m["dt"], m["Are"], ALU.mult))
            step(v.tensor_tensor(m["ai"], m["dt"], m["Aim"], ALU.mult))
            step(v.tensor_scalar(turns_i[:], m["ai"], 1.0 / TWO_PI, None, ALU.mult))
            step(v.tensor_copy(m["turns"], turns_i[:]))
            for part in (PI_1, PI_2, PI_3):
                step(v.scalar_tensor_tensor(out=m["ai"], in0=m["turns"], scalar=-part, in1=m["ai"],
                                            op0=ALU.mult, op1=ALU.add))
            step(v.tensor_scalar(m["r"], m["ai"], 3.1415925, -3.1415925, ALU.min, ALU.max))
            step(v.scalar_tensor_tensor(out=m["rc"], in0=m["r"], scalar=-1.0, in1=m["r"], op0=ALU.mult, op1=ALU.max))
            step(v.tensor_scalar(m["rc"], m["rc"], -1.0, float(np.pi / 2), ALU.mult, ALU.add))
            dve.wait_ge(c["act"], 2)
            dve.wait_ge(c["act"], 4)

            def gq(x):
                return x.rearrange("p (q g) -> p g q", g=G4)

            step(v.memset(pw[:, 0, :, :, 0], 1.0))
            step(v.memset(pw[:, 1, :, :, 0], 0.0))
            step(v.tensor_tensor(pw[:, 0, :, :, 1], gq(m["mag"]), gq(m["cos"]), ALU.mult))
            step(v.tensor_tensor(pw[:, 1, :, :, 1], gq(m["mag"]), gq(m["sin"]), ALU.mult))

            def product(out, x, y, count):
                yr = y[:, 0].unsqueeze(3).to_broadcast([P, G4, Q4, count])
                yi = y[:, 1].unsqueeze(3).to_broadcast([P, G4, Q4, count])
                v.tensor_tensor(t4[:, 0, :, :, 0:count], x[:, 0], yr, ALU.mult)
                v.tensor_tensor(t4[:, 1, :, :, 0:count], x[:, 1], yi, ALU.mult)
                v.tensor_tensor(t4[:, 2, :, :, 0:count], x[:, 0], yi, ALU.mult)
                step(v.tensor_tensor(t4[:, 3, :, :, 0:count], x[:, 1], yr, ALU.mult))
                v.tensor_tensor(out[:, 0], t4[:, 0, :, :, 0:count], t4[:, 1, :, :, 0:count], ALU.subtract)
                step(v.tensor_tensor(out[:, 1], t4[:, 2, :, :, 0:count], t4[:, 3, :, :, 0:count], ALU.add))

            for have in (1, 2, 4):
                product(pw[:, :, :, :, have + 1:2 * have + 1], pw[:, :, :, :, 1:have + 1], pw[:, :, :, :, have], have)
            step(v.tensor_scalar(gq(m["pm"]), pw[:, 0, :, :, 1], -1.0, None, ALU.add))
            step(v.tensor_copy(gq(m["r"]), pw[:, 1, :, :, 1]))

            def complex_product(re, im, a, b, cc, d, conj=1.0):
                step(v.tensor_tensor(m["t1"], m[a], m[cc], ALU.mult))
                step(v.tensor_tensor(m["t2"], m[b], m[d], ALU.mult))
                step(v.scalar_tensor_tensor(out=re, in0=m["t2"], scalar=-conj, in1=m["t1"], op0=ALU.mult, op1=ALU.add))
                step(v.tensor_tensor(m["t1"], m[a], m[d], ALU.mult))
                step(v.tensor_tensor(m["t2"], m[b], m[cc], ALU.mult))
                step(v.scalar_tensor_tensor(out=im, in0=m["t1"], scalar=conj, in1=m["t2"], op0=ALU.mult, op1=ALU.add))

            complex_product(m["nre"], m["nim"], "Cre", "Cim", "pm", "r")
            complex_product(m["mag"], m["cos"], "nre", "nim", "Are", "Aim", conj=-1.0)
            step(v.tensor_tensor(m["t1"], m["Are"], m["Are"], ALU.mult))
            step(v.tensor_tensor(m["t2"], m["Aim"], m["Aim"], ALU.mult))
            step(v.tensor_tensor(m["a2"], m["t1"], m["t2"], ALU.add))
            step(v.reciprocal(m["a2"], m["a2"]))
            for part, n in enumerate(("mag", "cos")):
                step(v.scalar_tensor_tensor(out=gp[:, part, :, :, 0], in0=gq(m[n]), scalar=2.0, in1=gq(m["a2"]),
                                            op0=ALU.mult, op1=ALU.mult))
            step(v.tensor_copy(base[:], pw[:, :, :, :, NC]))
            have = 1
            while have < NA:
                product(gp[:, :, :, :, have:2 * have], gp[:, :, :, :, 0:have], base, have)
                have *= 2
                if have < NA:
                    product(t4[:, 0:2, :, :, 15:16], base[:].unsqueeze(4), base, 1)
                    step(v.tensor_copy(base[:].unsqueeze(4), t4[:, 0:2, :, :, 15:16]))
            v.tensor_scalar(pw[:, 1], pw[:, 1], -1.0, None, ALU.mult).then_inc(c["vf"], 1)
            dve.wait_ge(c["w"], 16 * 9)
            step(v.tensor_scalar(w["sign"][:], w["sign"][:], 0.0, 2.0, ALU.is_ge, ALU.mult))
            step(v.tensor_scalar(w["sign"][:], w["sign"][:], -1.0, None, ALU.add))
            step(v.tensor_scalar(row[:], row[:], w["gate"][0:1, 0:1], None, ALU.mult))
            for j in range(2):
                last = v.tensor_scalar(row[:, j * F2:j * F2 + D], row[:, j * F2:j * F2 + D], 1.0, None, ALU.add)
            last.then_inc(c["done"], 1)
            dve.wait_ge(c["kp"], 1)
            for q in range(Q4):
                for half in range(2):
                    v.tensor_copy(
                        Ks[32 * q:32 * q + 32, :, half, :].rearrange("a c (b g) -> a b g c", b=2),
                        p_K[32 * q:32 * q + 32, half, :, :, q, :]).then_inc(c["ks"], 1)
            dve.wait_ge(c["again"], 16)
            v.tensor_tensor(KT[0:1, 0, :], KT[0:1, 0, :], skip[:], ALU.add).then_inc(c["done"], 1)
            dve.wait_ge(c["spec"], 1)
            step(v.tensor_copy(fourier["spec"][:], p_f[:]))

        @block.scalar
        def _(act):
            act.wait_ge(c["load"], 160)
            nc.scalar.activation(small["dt"][:], small["ldt"][:], ACT.Exp).then_inc(c["act"], 1)
            act.wait_ge(c["step"], 1)
            nc.scalar.activation(small["mag"][:], small["ar"][:], ACT.Exp).then_inc(c["act"], 1)
            act.wait_ge(c["step"], 10)
            nc.scalar.activation(small["sin"][:], small["r"][:], ACT.Sin).then_inc(c["act"], 1)
            nc.scalar.activation(small["cos"][:], small["rc"][:], ACT.Sin).then_inc(c["act"], 1)
            act.wait_ge(c["vf"], 3)
            act.wait_ge(c["w"], 16 * 9)
            for kb in range(2):
                rows = P if kb == 0 else C1
                last = nc.scalar.activation(w["Wvf"][0:rows, kb, :].rearrange("p (a f) -> p a f", a=2),
                                            (p_v if kb == 0 else p_f[:].rearrange("p (a b) d -> p a (b d)", a=2))[0:rows],
                                            ACT.Copy, scale=w["gate"][0:rows, 0:1])
            last.then_inc(c["act"], 1)

        @block.tensor
        def _(pe):
            pe.wait_ge(c["w"], 16 * 9)
            for kb in range(2):
                rows = P if kb == 0 else C1
                out = p_v if kb == 0 else p_f[:].rearrange("p (a b) d -> p a (b d)", a=2)
                for f in range(2):
                    for db in range(KD):
                        last = nc.tensor.matmul(out[0:rows, f, :], WvT[:, db, kb * P:kb * P + rows],
                                                Wf[:, db, f * 512:(f + 1) * 512], start=db == 0, stop=db == KD - 1)
                last.then_inc(c["vf"], 1)
            pe.wait_ge(c["vf"], 3)
            for half in range(2):
                rows = slice(N * half, N * half + N)
                for g in range(G4):
                    for part in range(2):
                        last = nc.tensor.matmul(p_K[:, half, g // 16, g % 16].rearrange("p q c -> p (q c)"),
                                                gp[rows, part, g].rearrange("p q a -> p (q a)"),
                                                pw[rows, part, g, :, 0:NC], start=part == 0, stop=part == 1)
            last.then_inc(c["kp"], 1)
            pe.wait_ge(c["done"], 2)
            pe.wait_ge(c["act"], 5)
            for f in range(4):
                for kb in range(2):
                    last = nc.tensor.matmul(p_f[:, f, :], fourier["fwd"][:, kb, f * P:(f + 1) * P], KT[:, kb, :],
                                            start=kb == 0, stop=kb == 1)
            last.then_inc(c["spec"], 1)


def state_space(nc, args, X, k, out):
    J, C, H, DH, TOP = 77, 192, 4, 32, 32
    C1 = C - P
    FF = 4 * D
    FB = FF // P
    TAKEN = float(np.float32(-3e38))
    with ExitStack() as ctx:
        def sb(name, shape, dt=F32):
            return ctx.enter_context(nc.sbuf_tensor("E_" + name, shape, dt))

        w = {"gate": sb("gate", [P, 1]), "sign": sb("sign", [P, KD, D]), "Wvf": sb("Wvf", [P, 2, 4 * D]),
             "VW": sb("VW", [J + 1, 4 * D])}
        fourier = {"fwd": sb("fwd", [P, 2, 2 * S]), "spec": sb("spec", [P, 4, D])}
        ssm_spectrum(nc, args, k, w, fourier, C, H * DH)

        def ps(name, shape):
            return ctx.enter_context(nc.psum_tensor("E_" + name, shape, F32))

        inv = sb("inv", [P, 4, S])
        Wq, Wk = sb("Wq", [P, KD, P]), sb("Wk", [P, 2, P])
        W1, W2 = sb("W1", [P, KD, FF]), sb("W2", [P, FB, D])
        ROWS = ("L1_xattn_g_norm_in", "L1_xattn_b_norm_in", "L1_xattn_g_norm_out", "L1_xattn_b_norm_out",
                "L1_xattn_b2", "L1_ffn_scale", "L1_ffn_bias")
        rowb = {n: sb(n, [P, D]) for n in ROWS}
        gf, bf, b1 = sb("gf", [P, KD]), sb("bf", [P, KD]), sb("b1", [P, FB])
        vmask, vbias = sb("vmask", [P, B * J], U8), sb("vbias", [P, B, J])
        tmask, tm = sb("tmask", [P, NT], U8), sb("tm", [P, NT])
        cx, cxT = sb("cx", [J, C]), sb("cxT", [P, 2, J])
        st, mv, var, rstd = sb("st", [P, 2, 6]), sb("mv", [P, 2, 2]), sb("var", [P, 2]), sb("rstd", [P, 2])
        v2, rstd2 = sb("v2", [P, 2]), sb("rstd2", [P, 2])
        h, n1, nb, u, hk = (sb(n, [P, 2, D]) for n in ("h", "n1", "nb", "u", "hk"))
        hT, qT, kTz = sb("hT", [P, KD, S]), sb("qT", [P, S]), sb("kTz", [P, H, J])
        sc, wk, ex = sb("sc", [P, 2, H, J]), sb("wk", [P, 2, H, J]), sb("ex", [P, 2, H, J])
        m8 = sb("m8", [P, 4, 2, H, 8])
        nmx, sm, rs = sb("nmx", [P, 2, H]), sb("sm", [P, 2, H]), sb("rs", [P, 2, H])
        am, amT = sb("am", [P, 2, J]), sb("amT", [J + 1, S])
        fo = sb("fo", [P, 2, 2 * D])
        tA, tB, Y = sb("tA", [P, 4, D]), sb("tB", [P, 4, D]), sb("Y", [P, 4, D])
        y2, xt, n3 = (sb(n, [P, 2, D]) for n in ("y2", "xt", "n3"))
        n3T, gT = sb("n3T", [P, KD, S]), sb("gT", [P, FB, S])
        xf, n4, h6, z, ob = (sb(n, [P, 2, D]) for n in ("xf", "n4", "h6", "z", "ob"))
        h6T = sb("h6T", [P, KD, S])
        norms = {n: (sb("st" + n, [P, 2, 6]), sb("mv" + n, [P, 2, 2]), sb("var" + n, [P, 2]), sb("rstd" + n, [P, 2]))
                 for n in ("3", "4", "6")}
        p_A, p_B = ps("pA", [P, 2, 256]), ps("pB", [P, 512])
        p_S = ps("pS", [P, 2, 512])
        p_U, p_Y, p_T = ps("pU", [P, 4, 256]), ps("pY", [P, 2, 256]), ps("pT", [P, 2, 256])
        s = semaphores(nc, ctx, "E", NORM + " settled h v2a v2b v2 rstd2 n1 nbg nb cxp cxT hTp hT kqp kT qT vwp vw scp "
                       "sc m80 m81 m82 m83 r0 r1 r2 r3 nmx ex sel sm rs rt pn am amp amT fp0 fp1 u0 u1 ui0 ui1 fo0 fo1 hk")
        z2 = semaphores(nc, ctx, "Ez", "settled Up tAB Yr Yi yp y2 ysh xt n3 T3 n3T gp0 gp1 g0 g1 ffp xfp xf n4 n4g "
                        "n4b x h6 T6 h6T zp zs zb zc ob")
        nrm = {n: semaphores(nc, ctx, "E" + n, NORM + " settled") for n in ("3", "4", "6")}
        ld = semaphores(nc, ctx, "Eld", "w masks init cxl out")
        block = ctx.enter_context(nc.Block())

        @block.sync
        def _(sp):
            for group in (s, z2, *nrm.values()):
                give_credit(sp, group)
            sp.sem_inc(ld["out"], 16)
            for n in ROWS:
                sp.dma_start(rowb[n][:], args[n].partition_broadcast(P)).then_inc(ld["w"], 16)
            sp.dma_start(inv[:], args["fourier_inverse"].rearrange("(k p) l -> p k l", p=P)).then_inc(ld["w"], 16)
            sp.dma_start(Wq[:], args["L1_xattn_Wq"].rearrange("(k p) n -> p k n", p=P)).then_inc(ld["w"], 16)
            sp.dma_start(Wk[:, 0, :], args["L1_xattn_Wk"][0:P]).then_inc(ld["w"], 16)
            sp.dma_start(Wk[0:C1, 1, :], args["L1_xattn_Wk"][P:C]).then_inc(ld["w"], 16)
            sp.dma_start(W1[:], args["L1_xattn_W1"].rearrange("(k p) n -> p k n", p=P)).then_inc(ld["w"], 16)
            sp.dma_start(W2[:], args["L1_xattn_W2"].rearrange("(k p) n -> p k n", p=P)).then_inc(ld["w"], 16)
            with nc.allow_non_contiguous_dma(reason="columns of a value a channel"):
                sp.dma_start(gf[:], args["L1_xattn_g_ffn"].rearrange("(k p) -> p k", p=P)).then_inc(ld["w"], 16)
                sp.dma_start(bf[:], args["L1_xattn_b_ffn"].rearrange("(k p) -> p k", p=P)).then_inc(ld["w"], 16)
                sp.dma_start(b1[:], args["L1_xattn_b1"].rearrange("(k p) -> p k", p=P)).then_inc(ld["w"], 16)
                sp.dma_start(tmask[:], args["mask_BxS_bf1"].rearrange("b (s p) -> p (b s)", p=P)).then_inc(ld["masks"], 16)
            sp.dma_start(vmask[:], args["mask_BxS2_bf1"].rearrange("b j -> (b j)").partition_broadcast(P)).then_inc(ld["masks"], 16)

            def context(i):
                sp.wait_ge(s["cxp"], before(i))
                src = args["ctx_768"][i] if isinstance(i, int) else args["ctx_768"][bass.ds(i, 1)].rearrange("a j c -> (a j) c")
                sp.dma_start(cx[:], src).then_inc(ld["cxl"], 16)

            def store(i):
                sp.wait_ge(z2["ob"], done(i))
                dst = out[i] if isinstance(i, int) else out[bass.ds(i, 1)].rearrange("a s d -> (a s) d")
                sp.dma_start(dst.rearrange("(s p) d -> p s d", p=P), ob[:]).then_inc(ld["out"], 16)

            context(0)
            with sp.Fori(0, B - 1) as i:
                context(i + 1)
                store(i)
            store(B - 1)
            sp.wait_ge(ld["out"], 16 * (B + 1))

        @block.gpsimd
        def _(pool):
            g = nc.gpsimd
            g.memset(kTz[:], 0.0).then_inc(ld["init"], 1)
            pool.wait_ge(ld["init"], 1)
            g.memset(amT[64:J + 1, :], 1.0).then_inc(ld["init"], 1)
            pool.wait_ge(ld["init"], 2)
            pool.wait_ge(ld["w"], 16 * 16)

            def both(row):
                return rowb[row][:].unsqueeze(1).to_broadcast([P, 2, D])

            def first_a(j):
                norm_rstd(nc, pool, s, mv, var, rstd, k, j)
                pool.wait_ge(s["rstd"], done(j))
                g.tensor_tensor(v2[:], mv[:, :, 1], rstd[:], ALU.mult).then_inc(s["v2a"], 1)
                pool.wait_ge(s["v2a"], done(j))
                g.tensor_tensor(v2[:], v2[:], rstd[:], ALU.mult).then_inc(s["v2b"], 1)
                pool.wait_ge(s["v2b"], done(j))
                settle(pool, s)
                g.tensor_scalar(v2[:], v2[:], EPS, None, ALU.add).then_inc(s["v2"], 1)
                pool.wait_ge(s["v2"], done(j))
                pool.wait_ge(s["n1"], before(j))
                g.tensor_tensor(rstd2[:], v2[:], k["minus_half"][:], ALU.pow).then_inc(s["rstd2"], 1)
                pool.wait_ge(s["n1"], done(j))
                pool.wait_ge(s["u1"], before(j))
                g.tensor_tensor(nb[:], n1[:], both("L1_xattn_g_norm_in"), ALU.mult).then_inc(s["nbg"], 1)
                pool.wait_ge(s["nbg"], done(j))
                g.tensor_tensor(nb[:], nb[:], both("L1_xattn_b_norm_in"), ALU.add).then_inc(s["nb"], 1)

            def spectrum(i):
                pool.wait_ge(z2["tAB"], done(i))
                pool.wait_ge(z2["yp"], before(i))
                g.tensor_tensor(Y[:, 0:2], tA[:, 0:2], tB[:, 2:4], ALU.subtract).then_inc(z2["Yr"], 1)
                g.tensor_tensor(Y[:, 2:4], tA[:, 2:4], tB[:, 0:2], ALU.add).then_inc(z2["Yi"], 1)

            def mid(i):
                pool.wait_ge(z2["y2"], done(i))
                g.tensor_tensor(y2[:], y2[:], fo[:, :, D:2 * D], ALU.add).then_inc(z2["ysh"], 1)
                pool.wait_ge(z2["ysh"], done(i))
                pool.wait_ge(z2["xfp"], before(i))
                pool.wait_ge(s["hk"], done(i))
                g.tensor_tensor(xt[:], y2[:], hk[:], ALU.add).then_inc(z2["xt"], 1)
                norm_rstd(nc, pool, nrm["3"], *norms["3"][1:], k, i)

            def late(i):
                pool.wait_ge(z2["xfp"], done(i))
                g.tensor_tensor(xf[:], xf[:], both("L1_xattn_b2"), ALU.add).then_inc(z2["xf"], 1)
                norm_rstd(nc, pool, nrm["4"], *norms["4"][1:], k, i)
                pool.wait_ge(z2["n4"], done(i))
                g.tensor_tensor(n4[:], n4[:], both("L1_xattn_g_norm_out"), ALU.mult).then_inc(z2["n4g"], 1)
                pool.wait_ge(z2["n4g"], done(i))
                g.tensor_tensor(n4[:], n4[:], both("L1_xattn_b_norm_out"), ALU.add).then_inc(z2["n4b"], 1)
                pool.wait_ge(z2["n4b"], done(i))
                settle(pool, z2)
                x2 = X[:, 2 * i:2 * i + 2, :] if isinstance(i, int) else X[:, bass.ds(2 * i, 2), :]
                g.tensor_tensor(x2, x2, n4[:], ALU.add).then_inc(z2["x"], 1)
                norm_rstd(nc, pool, nrm["6"], *norms["6"][1:], k, i)

            def last(i):
                pool.wait_ge(z2["zs"], done(i))
                g.tensor_tensor(z[:], z[:], both("L1_ffn_bias"), ALU.add).then_inc(z2["zb"], 1)

            def round(i, j):
                if j is not None:
                    first_a(j)
                spectrum(i)
                mid(i)
                late(i)
                last(i)

            first_a(0)
            with pool.Fori(0, B - 1) as i:
                round(i, i + 1)
            round(B - 1, None)

        @block.vector
        def _(dve):
            v = nc.vector
            dve.wait_ge(ld["masks"], 32)
            dve.wait_ge(ld["w"], 16 * 16)
            v.tensor_scalar(vbias[:].rearrange("p b j -> p (b j)"), vmask[:], 1.0, 1e30, ALU.subtract,
                            ALU.mult).then_inc(ld["masks"], 1)
            v.tensor_scalar(tm[:], tmask[:], 1.0 / H, None, ALU.mult).then_inc(ld["masks"], 1)
            dve.wait_ge(ld["masks"], 34)

            def normalise(sems, stats, product, x, y, i, read_by):
                norm_stats(nc, dve, sems, x, stats[0], stats[1], i)
                dve.wait_ge(sems["rstd"], done(i))
                for sem, value in read_by:
                    dve.wait_ge(sem, value)
                for a in range(2):
                    ins = v.tensor_scalar(y[:, a, :], x[a], stats[1][:, a, 0:1], stats[3][:, a:a + 1],
                                          ALU.subtract, ALU.mult)
                product_inc(ins, product)

            def product_inc(ins, sem):
                ins.then_inc(sem, 1)

            def first_a(j):
                normalise(s, (st, mv, var, rstd), s["h"], [X[:, 2 * j, :], X[:, 2 * j + 1, :]], h, j,
                          [(s["hTp"], before(j)), (s["hk"], before(j))])
                dve.wait_ge(s["h"], done(j))
                dve.wait_ge(s["rstd2"], done(j))
                dve.wait_ge(s["nbg"], before(j))
                for a in range(2):
                    ins = v.tensor_scalar(n1[:, a, :], h[:, a, :], rstd2[:, a:a + 1], None, ALU.mult)
                ins.then_inc(s["n1"], 1)

            def scores(j):
                dve.wait_ge(s["scp"], done(j))
                dve.wait_ge(s["ex"], before(j))
                bias = vbias[:, bass.ds(j, 1), :].to_broadcast([P, H, J])
                for t in range(2):
                    ins = v.scalar_tensor_tensor(out=sc[:, t], in0=p_S[:, t, 0:H * J].rearrange("p (h j) -> p h j", h=H),
                                                 scalar=float(DH) ** -0.5, in1=bias, op0=ALU.mult, op1=ALU.add)
                ins.then_inc(s["sc"], 1)
                dve.wait_ge(s["sc"], done(j))

            def take(j, turn):
                src = sc if turn == 0 else wk
                if turn:
                    dve.wait_ge(s[f"r{turn - 1}"], done(j))
                settle(dve, s)
                for t in range(2):
                    for hd in range(H):
                        ins = v.max(m8[:, turn, t, hd, :], src[:, t, hd, :])
                ins.then_inc(s[f"m8{turn}"], 1)
                dve.wait_ge(s[f"m8{turn}"], done(j))
                settle(dve, s)
                for t in range(2):
                    for hd in range(H):
                        ins = v.match_replace(wk[:, t, hd, :], m8[:, turn, t, hd, :], src[:, t, hd, :], TAKEN)
                ins.then_inc(s[f"r{turn}"], 1)
                if turn == 0:
                    dve.wait_ge(s["ex"], before(j))
                    v.tensor_scalar(nmx[:], m8[:, 0, :, :, 0], -1.0, None, ALU.mult).then_inc(s["nmx"], 1)

            def average(j):
                dve.wait_ge(s["r3"], done(j))
                dve.wait_ge(s["ex"], done(j))
                v.scalar_tensor_tensor(out=ex[:], in0=wk[:], scalar=TAKEN, in1=ex[:], op0=ALU.is_equal,
                                       op1=ALU.mult).then_inc(s["sel"], 1)
                dve.wait_ge(s["sel"], done(j))
                v.tensor_reduce(sm[:], ex[:], AX.X, ALU.add).then_inc(s["sm"], 1)
                dve.wait_ge(s["sm"], done(j))
                v.reciprocal(rs[:], sm[:]).then_inc(s["rs"], 1)
                dve.wait_ge(s["rs"], done(j))
                v.tensor_tensor(rs[:], rs[:], tm[:, bass.ds(2 * j, 2)].unsqueeze(2).to_broadcast([P, 2, H]),
                                ALU.mult).then_inc(s["rt"], 1)
                dve.wait_ge(s["rt"], done(j))
                v.tensor_tensor(ex[:], ex[:], rs[:].unsqueeze(3).to_broadcast([P, 2, H, J]), ALU.mult).then_inc(s["pn"], 1)
                dve.wait_ge(s["pn"], done(j))
                dve.wait_ge(s["amp"], before(j))
                v.tensor_reduce(am[:], ex[:].rearrange("p t h j -> p t j h"), AX.X, ALU.add).then_inc(s["am"], 1)

            def film(j):
                dve.wait_ge(s["nb"], done(j))
                for t in range(2):
                    dve.wait_ge(s[f"fp{t}"], done(j))
                    if t == 0:
                        dve.wait_ge(z2["Up"], before(j))
                    v.tensor_tensor(u[:, t, :], nb[:, t, :], p_S[:, 0, 0:D], ALU.mult).then_inc(s[f"ui{t}"], 1)
                    dve.wait_ge(s[f"ui{t}"], done(j))
                    v.tensor_tensor(u[:, t, :], u[:, t, :], p_S[:, 0, D:2 * D], ALU.add).then_inc(s[f"u{t}"], 1)
                dve.wait_ge(z2["xt"], before(j))
                v.tensor_copy(hk[:], h[:]).then_inc(s["hk"], 1)

            def spectrum(i):
                dve.wait_ge(z2["Up"], done(i))
                dve.wait_ge(z2["Yi"], before(i))
                for part, dst in ((0, tA), (1, tB)):
                    kf = fourier["spec"][:, 2 * part:2 * part + 2, :].rearrange("p b d -> p (b d)")
                    ins = v.tensor_tensor(dst[:].rearrange("p (a b) d -> p a (b d)", a=2),
                                          p_U[:].rearrange("p (a b) d -> p a (b d)", a=2),
                                          kf.unsqueeze(1).to_broadcast([P, 2, 2 * D]), ALU.mult)
                ins.then_inc(z2["tAB"], 1)

            def mid(i):
                dve.wait_ge(z2["yp"], done(i))
                dve.wait_ge(s["fo1"], done(i))
                dve.wait_ge(z2["xt"], before(i))
                v.tensor_tensor(y2[:], p_Y[:], fo[:, :, 0:D], ALU.mult).then_inc(z2["y2"], 1)
                dve.wait_ge(z2["xt"], done(i))
                normalise(nrm["3"], norms["3"], z2["n3"], [xt[:, 0, :], xt[:, 1, :]], n3, i, [(z2["T3"], before(i))])

            def late(i):
                dve.wait_ge(z2["ffp"], done(i))
                dve.wait_ge(z2["n4"], before(i))
                v.tensor_tensor(xf[:], p_Y[:], xt[:], ALU.add).then_inc(z2["xfp"], 1)
                dve.wait_ge(z2["xf"], done(i))
                normalise(nrm["4"], norms["4"], z2["n4"], [xf[:, 0, :], xf[:, 1, :]], n4, i, [(z2["x"], before(i))])
                dve.wait_ge(z2["x"], done(i))
                normalise(nrm["6"], norms["6"], z2["h6"], [X[:, 2 * i, :], X[:, 2 * i + 1, :]], h6, i,
                          [(z2["T6"], before(i))])

            def last(i):
                dve.wait_ge(z2["zp"], done(i))
                dve.wait_ge(z2["ob"], before(i))
                v.tensor_tensor(z[:], p_Y[:], rowb["L1_ffn_scale"][:].unsqueeze(1).to_broadcast([P, 2, D]),
                                ALU.mult).then_inc(z2["zs"], 1)
                dve.wait_ge(z2["zb"], done(i))
                v.tensor_scalar(z[:], z[:], 100.0, -100.0, ALU.min, ALU.max).then_inc(z2["zc"], 1)
                dve.wait_ge(z2["zc"], done(i))
                dve.wait_ge(ld["out"], 16 * i + 16)
                x2 = X[:, 2 * i:2 * i + 2, :] if isinstance(i, int) else X[:, bass.ds(2 * i, 2), :]
                v.tensor_tensor(ob[:], x2, z[:], ALU.add).then_inc(z2["ob"], 1)

            def round(i, j):
                if j is not None:
                    first_a(j)
                spectrum(i)
                if j is not None:
                    scores(j)
                    take(j, 0)
                    take(j, 1)
                mid(i)
                if j is not None:
                    take(j, 2)
                    take(j, 3)
                    average(j)
                late(i)
                if j is not None:
                    film(j)
                last(i)

            first_a(0)
            scores(0)
            for turn in range(4):
                take(0, turn)
            average(0)
            film(0)
            with dve.Fori(0, B - 1) as i:
                round(i, i + 1)
            round(B - 1, None)

        @block.scalar
        def _(act):
            a_ = nc.scalar
            act.wait_ge(ld["w"], 16 * 16)
            act.wait_ge(ld["init"], 2)

            def first_a(j):
                act.wait_ge(s["cxp"], done(j))
                act.wait_ge(s["vwp"], before(j))
                a_.activation(cxT[:, 0, :], p_A[:, 0, 0:J], ACT.Copy)
                a_.activation(cxT[0:C1, 1, :], p_A[0:C1, 1, 0:J], ACT.Copy).then_inc(s["cxT"], 1)
                act.wait_ge(s["hTp"], done(j))
                act.wait_ge(s["kqp"], before(j))
                a_.activation(hT[:], p_A[:], ACT.Copy).then_inc(s["hT"], 1)
                act.wait_ge(s["kqp"], done(j))
                act.wait_ge(s["scp"], before(j))
                for hd in range(H):
                    ins = a_.activation(kTz[DH * hd:DH * hd + DH, hd, :], p_B[DH * hd:DH * hd + DH, 256:256 + J], ACT.Copy)
                ins.then_inc(s["kT"], 1)
                a_.activation(qT[:], p_B[:, 0:256], ACT.Copy).then_inc(s["qT"], 1)
                act.wait_ge(s["vwp"], done(j))
                act.wait_ge(s["fp1"], before(j))
                a_.activation(w["VW"][0:J, :].rearrange("j (a f) -> j a f", a=2), p_S[0:J], ACT.Copy).then_inc(s["vw"], 1)

            def exps(j):
                act.wait_ge(s["nmx"], done(j))
                act.wait_ge(s["am"], before(j))
                for t in range(2):
                    for hd in range(H):
                        ins = a_.activation(ex[:, t, hd, :], sc[:, t, hd, :], ACT.Exp, bias=nmx[:, t, hd:hd + 1])
                ins.then_inc(s["ex"], 1)

            def film(j):
                act.wait_ge(s["amp"], done(j))
                act.wait_ge(s["fp1"], before(j))
                a_.activation(amT[0:J, :], p_A[0:J].rearrange("j a q -> j (a q)")[:, 0:S], ACT.Copy).then_inc(s["amT"], 1)
                for t in range(2):
                    act.wait_ge(s[f"fp{t}"], done(j))
                    if t == 0:
                        act.wait_ge(z2["ysh"], before(j))
                    a_.activation(fo[:, t, :], p_S[:, 1, :], ACT.Copy).then_inc(s[f"fo{t}"], 1)

            def mid(i):
                act.wait_ge(z2["T3"], done(i))
                act.wait_ge(z2["gp1"], before(i))
                for kb in range(KD):
                    ins = a_.activation(n3T[:, kb, :], p_T[:, kb, :], ACT.Identity, bias=bf[:, kb:kb + 1],
                                        scale=gf[:, kb:kb + 1])
                ins.then_inc(z2["n3T"], 1)
                for half in range(2):
                    act.wait_ge(z2[f"gp{half}"], done(i))
                    if half == 0:
                        act.wait_ge(z2["ffp"], before(i))
                    for f in range(4):
                        fb = 4 * half + f
                        ins = a_.activation(gT[:, fb, :], p_U[:, f, :], ACT.Gelu, bias=b1[:, fb:fb + 1])
                    ins.then_inc(z2[f"g{half}"], 1)

            def last(i):
                act.wait_ge(z2["T6"], done(i))
                act.wait_ge(z2["zp"], before(i))
                a_.activation(h6T[:], p_T[:], ACT.Copy).then_inc(z2["h6T"], 1)

            def round(i, j):
                if j is not None:
                    first_a(j)
                    exps(j)
                mid(i)
                if j is not None:
                    film(j)
                last(i)

            first_a(0)
            exps(0)
            film(0)
            with act.Fori(0, B - 1) as i:
                round(i, i + 1)
            round(B - 1, None)

        @block.tensor
        def _(pe):
            pe.wait_ge(ld["w"], 16 * 16)
            pe.wait_ge(ld["init"], 2)

            def transposes(out, x):
                for a in range(2):
                    for kb in range(KD):
                        ins = nc.tensor.transpose(out[:, kb, a * P:(a + 1) * P], x[:, a, kb * P:(kb + 1) * P],
                                                  k["ident"][:])
                return ins

            def first_a(j):
                pe.wait_ge(ld["cxl"], 16 * j + 16)
                pe.wait_ge(s["amT"], before(j))
                nc.tensor.transpose(p_A[:, 0, 0:J], cx[:, 0:P], k["ident"][0:J, 0:J])
                nc.tensor.transpose(p_A[0:C1, 1, 0:J], cx[:, P:C], k["ident"][0:J, 0:J]).then_inc(s["cxp"], 1)
                pe.wait_ge(s["h"], done(j))
                pe.wait_ge(s["cxT"], done(j))
                transposes(p_A, h).then_inc(s["hTp"], 1)
                pe.wait_ge(s["u1"], before(j))
                pe.wait_ge(s["fo1"], before(j))
                for f in range(2):
                    for kb in range(2):
                        rows = P if kb == 0 else C1
                        ins = nc.tensor.matmul(p_S[0:J, f, :], cxT[0:rows, kb, :], w["Wvf"][0:rows, kb, f * 512:(f + 1) * 512],
                                               start=kb == 0, stop=kb == 1)
                ins.then_inc(s["vwp"], 1)
                pe.wait_ge(s["hT"], done(j))
                pe.wait_ge(s["qT"], before(j))
                for kb in range(KD):
                    nc.tensor.matmul(p_B[:, 0:S], Wq[:, kb, :], hT[:, kb, :], start=kb == 0, stop=kb == KD - 1)
                for kb in range(2):
                    rows = P if kb == 0 else C1
                    ins = nc.tensor.matmul(p_B[:, S:S + J], Wk[0:rows, kb, :], cxT[0:rows, kb, :], start=kb == 0, stop=kb == 1)
                ins.then_inc(s["kqp"], 1)
                pe.wait_ge(s["kT"], done(j))
                pe.wait_ge(s["qT"], done(j))
                pe.wait_ge(s["vw"], done(j))
                for t in range(2):
                    ins = nc.tensor.matmul(p_S[:, t, 0:H * J], qT[:, t * P:(t + 1) * P], kTz[:].rearrange("p h j -> p (h j)"),
                                           start=True, stop=True)
                ins.then_inc(s["scp"], 1)

            def film(j):
                pe.wait_ge(s["am"], done(j))
                pe.wait_ge(s["hT"], done(j))
                for t in range(2):
                    ins = nc.tensor.transpose(p_A[0:J].rearrange("j a q -> j (a q)")[:, t * P:(t + 1) * P], am[:, t, :],
                                              k["ident"][:])
                ins.then_inc(s["amp"], 1)
                pe.wait_ge(s["amT"], done(j))
                pe.wait_ge(s["sc"], done(j))
                for t in range(2):
                    if t:
                        pe.wait_ge(s["u0"], done(j))
                        pe.wait_ge(s["fo0"], done(j))
                    for f in range(2):
                        ins = nc.tensor.matmul(p_S[:, f, :], amT[:, t * P:(t + 1) * P], w["VW"][:, f * 512:(f + 1) * 512],
                                               start=True, stop=True)
                    ins.then_inc(s[f"fp{t}"], 1)

            def forward(i):
                pe.wait_ge(s["u1"], done(i))
                pe.wait_ge(z2["g1"], before(i))
                for f in range(4):
                    for a in range(2):
                        ins = nc.tensor.matmul(p_U[:, f, :], fourier["fwd"][:, a, f * P:(f + 1) * P], u[:, a, :],
                                               start=a == 0, stop=a == 1)
                ins.then_inc(z2["Up"], 1)

            def inverse(i):
                pe.wait_ge(z2["Yr"], done(i))
                pe.wait_ge(z2["Yi"], done(i))
                pe.wait_ge(z2["zs"], before(i))
                for a in range(2):
                    for f in range(4):
                        ins = nc.tensor.matmul(p_Y[:, a, :], inv[:, f, a * P:(a + 1) * P], Y[:, f, :],
                                               start=f == 0, stop=f == 3)
                ins.then_inc(z2["yp"], 1)

            def network(i):
                pe.wait_ge(z2["n3"], done(i))
                pe.wait_ge(z2["h6T"], before(i))
                transposes(p_T, n3).then_inc(z2["T3"], 1)
                pe.wait_ge(z2["n3T"], done(i))
                pe.wait_ge(z2["tAB"], done(i))
                for half in range(2):
                    if half:
                        pe.wait_ge(z2["g0"], done(i))
                    for f in range(4):
                        fb = 4 * half + f
                        for kb in range(KD):
                            ins = nc.tensor.matmul(p_U[:, f, :], W1[:, kb, fb * P:(fb + 1) * P], n3T[:, kb, :],
                                                   start=kb == 0, stop=kb == KD - 1)
                    ins.then_inc(z2[f"gp{half}"], 1)
                pe.wait_ge(z2["g1"], done(i))
                pe.wait_ge(z2["y2"], done(i))
                for a in range(2):
                    for fb in range(FB):
                        ins = nc.tensor.matmul(p_Y[:, a, :], gT[:, fb, a * P:(a + 1) * P], W2[:, fb, :],
                                               start=fb == 0, stop=fb == FB - 1)
                ins.then_inc(z2["ffp"], 1)

            def project(i):
                pe.wait_ge(z2["h6"], done(i))
                pe.wait_ge(z2["n3T"], done(i))
                transposes(p_T, h6).then_inc(z2["T6"], 1)
                pe.wait_ge(z2["h6T"], done(i))
                pe.wait_ge(z2["xfp"], done(i))
                for a in range(2):
                    for kb in range(KD):
                        ins = nc.tensor.matmul(p_Y[:, a, :], h6T[:, kb, a * P:(a + 1) * P], w["sign"][:, kb, :],
                                               start=kb == 0, stop=kb == KD - 1)
                ins.then_inc(z2["zp"], 1)

            def round(i, j):
                forward(i)
                if j is not None:
                    first_a(j)
                inverse(i)
                network(i)
                if j is not None:
                    film(j)
                project(i)

            first_a(0)
            film(0)
            with pe.Fori(0, B - 1) as i:
                round(i, i + 1)
            round(B - 1, None)


def build(nc, args, out):
    with ExitStack() as ctx:
        def sb(name, shape, dt=F32):
            return ctx.enter_context(nc.sbuf_tensor(name, shape, dt))

        X = sb("X", [P, NT, D])
        k = {"ident": sb("ident", [P, P]), "zero": sb("zero", [P, P]), "minus_half": sb("minus_half", [P, 2])}
        setup_constants(nc, args, X, k, ctx)
        self_attention(nc, args, X, k)
        cross_attention(nc, args, X, k)
        experts(nc, args, X, k)
        rwkv(nc, args, X, k)
        state_space(nc, args, X, k, out)


TRANSPOSED = ("L1_attn_Wk", "L1_attn_Wv", "L1_attn_Wr", "L1_attn_Wo", "L1_attn_Wck", "L1_attn_Wcv", "L1_attn_Wcr",
              "L1_ffn_weights", "L1_xattn_A_re", "L1_xattn_A_im", "L1_xattn_C_re", "L1_xattn_C_im",
              "L1_xattn_Wv")


def kernel(**inputs):
    import numpy as _np
    import concourse.bacc as _bacc
    from concourse import mybir as _mybir
    from concourse.bass_utils import run_bass_kernel_spmd as _run

    nc = _bacc.Bacc("TRN2", target_bir_lowering=False, num_devices=1)
    arrays, args = {}, {}
    for name, value in inputs.items():
        a = _np.asarray(value)
        if name in TRANSPOSED:
            a = a.T
        if a.ndim == 0:
            a = a.reshape(1)
        a = _np.ascontiguousarray(a)
        arrays["in_" + name] = a
        args[name] = nc.dram_tensor("in_" + name, a.shape, _mybir.dt.from_np(a.dtype), kind="ExternalInput").ap()
    angle = _np.outer(_np.arange(S), (_np.pi / 2 + 2 * _np.pi * _np.arange(S)) / S)
    forward = _np.concatenate([_np.cos(angle), _np.sin(angle)], axis=1)
    for name, a in (("fourier", forward), ("fourier_inverse", forward.T / S)):
        arrays["in_" + name] = _np.ascontiguousarray(a.astype(_np.float32))
        args[name] = nc.dram_tensor("in_" + name, a.shape, F32, kind="ExternalInput").ap()
    out = nc.dram_tensor("out_0", (B, S, D), F32, kind="ExternalOutput").ap()
    build(nc, args, out)
    r = _run(nc, [arrays], core_ids=[0])
    return r.results[0]["out_0"]
```

```python
from contextlib import ExitStack

import numpy as np

import concourse.bass as bass
from concourse import mybir

F32 = mybir.dt.float32
I32 = mybir.dt.int32
U32 = mybir.dt.uint32
U8 = mybir.dt.uint8
ALU = mybir.AluOpType
ACT = mybir.ActivationFunctionType
AX = mybir.AxisListType

P = 128
B, S, D = 16, 256, 256
KD = D // P
NT = B * S // P
EPS = 1e-5
LOWEST = -3.4028234663852886e38


def done(i):
    return i + 2


def before(i):
    return i + 1


def settle(engine, s):
    engine.sem_inc(s["settled"], 1)


def semaphores(nc, ctx, prefix, names):
    sems = {n: nc.alloc_semaphore(f"{prefix}_{n}") for n in names.split()}

    def clear():
        nc.clear_and_free_semaphores(list(sems.values()))
        nc.all_engine_barrier()

    ctx.callback(clear)
    return sems


def give_credit(engine, sems):
    for s in sems.values():
        engine.sem_inc(s, 1)


def setup_constants(nc, args, X, k, lasting):
    with ExitStack() as ctx:
        s = semaphores(nc, ctx, "set", "zero ident eps load")
        block = ctx.enter_context(nc.Block())

        @block.sync
        def _(sp):
            for b in range(0, B, 4):
                sp.dma_start(X[:, 2 * b:2 * b + 8, :],
                             args["x"][b:b + 4].rearrange("b (s p) d -> p (b s) d", p=P)).then_inc(s["load"], 16)
            sp.wait_ge(s["load"], 16 * 4)

        @block.gpsimd
        def _(pool):
            nc.gpsimd.memset(k["zero"][:], 0.0).then_inc(s["zero"], 1)
            nc.gpsimd.memset(k["minus_half"][:], -0.5).then_inc(s["eps"], 1)
            pool.wait_ge(s["zero"], 1)
            nc.gpsimd.affine_select(out=k["ident"][:], in_=k["zero"][:], compare_op=ALU.not_equal, fill=1.0,
                                    base=0, pattern=[[-1, P]], channel_multiplier=1).then_inc(s["ident"], 1)
            pool.wait_ge(s["ident"], 1)


def norm_stats(nc, dve, s, x_tiles, st, mv, i):
    dve.wait_ge(s["rstd"], before(i))
    settle(dve, s)
    for t, x in enumerate(x_tiles):
        last = nc.vector.bn_stats(st[:, t, :], x)
    last.then_inc(s["stats"], 1)
    dve.wait_ge(s["stats"], done(i))
    settle(dve, s)
    for t in range(len(x_tiles)):
        last = nc.vector.bn_aggr(mv[:, t, :], st[:, t, :])
    last.then_inc(s["aggr"], 1)


def norm_rstd(nc, pool, s, mv, var, rstd, k, i):
    pool.wait_ge(s["aggr"], done(i))
    settle(pool, s)
    nc.gpsimd.tensor_scalar(var[:], mv[:, :, 1], EPS, None, ALU.add).then_inc(s["var"], 1)
    pool.wait_ge(s["var"], done(i))
    settle(pool, s)
    nc.gpsimd.tensor_tensor(rstd[:], var[:], k["minus_half"][:, 0:var.shape[1]], ALU.pow).then_inc(s["rstd"], 1)


NORM = "stats aggr var rstd"


def self_attention(nc, args, X, k):
    WINDOW = 64
    with ExitStack() as ctx:
        def sb(name, shape, dt=F32):
            return ctx.enter_context(nc.sbuf_tensor("A_" + name, shape, dt))

        def ps(name, shape):
            return ctx.enter_context(nc.psum_tensor("A_" + name, shape, F32))

        W = sb("W", [P, KD, D])
        band = sb("band", [P, 2, S])
        st, mv = sb("st", [P, 2, 6]), sb("mv", [P, 2, 2])
        var, rstd = sb("var", [P, 2]), sb("rstd", [P, 2])
        h, hT, qT = sb("h", [P, 2, D]), sb("hT", [P, KD, S]), sb("qT", [P, KD, S])
        sc, pr, prT = sb("sc", [P, 2, S]), sb("pr", [P, 2, S]), sb("prT", [P, 2, S])
        mx, nmx, sm, rs = sb("mx", [P, 2]), sb("nmx", [P, 2]), sb("sm", [P, 2]), sb("rs", [P, 2])
        ra = sb("ra", [P, 2, D])
        p_hT, p_q, p_s, p_prT, p_o = (ps(n, [P, 2, 256]) for n in ("phT", "pq", "ps", "pprT", "po"))
        s = semaphores(nc, ctx, "A", NORM + " settled h xh hTp hT qp q scp sc nmx pr rs prTp prT op ra xa")
        ld = semaphores(nc, ctx, "Ald", "w band")
        block = ctx.enter_context(nc.Block())

        @block.sync
        def _(sp):
            sp.dma_start(W[:], args["L0_attn_W"].rearrange("(k p) n -> p k n", p=P)).then_inc(ld["w"], 16)
            give_credit(sp, s)

        @block.gpsimd
        def _(pool):
            nc.gpsimd.memset(band[:], 0.0).then_inc(ld["band"], 1)
            pool.wait_ge(ld["band"], 1)
            nc.gpsimd.affine_select(out=band[:], in_=band[:], compare_op=ALU.is_ge, fill=-1e9, base=WINDOW,
                                    pattern=[[P, 2], [-1, S]], channel_multiplier=1).then_inc(ld["band"], 1)
            pool.wait_ge(ld["band"], 2)
            nc.gpsimd.affine_select(out=band[:], in_=band[:], compare_op=ALU.is_ge, fill=-1e9, base=WINDOW,
                                    pattern=[[-P, 2], [1, S]], channel_multiplier=-1).then_inc(ld["band"], 1)
            def residual(i, j):
                x2 = X[:, bass.ds(2 * i, 2), :]
                pool.wait_ge(s["h"], done(i))
                settle(pool, s)
                nc.gpsimd.tensor_tensor(x2, x2, h[:], ALU.add).then_inc(s["xh"], 1)
                if j is not None:
                    norm_rstd(nc, pool, s, mv, var, rstd, k, j)
                pool.wait_ge(s["xh"], done(i))
                pool.wait_ge(s["ra"], done(i))
                settle(pool, s)
                nc.gpsimd.tensor_tensor(x2, x2, ra[:], ALU.add).then_inc(s["xa"], 1)

            norm_rstd(nc, pool, s, mv, var, rstd, k, 0)
            with pool.Fori(0, B - 1) as i:
                residual(i, i + 1)
            residual(B - 1, None)
            pool.wait_ge(s["xa"], done(B - 1))

        @block.vector
        def _(dve):
            dve.wait_ge(ld["band"], 3)

            def stats(j):
                norm_stats(nc, dve, s, [X[:, 2 * j, :], X[:, 2 * j + 1, :]], st, mv, j)

            def attend(i, j):
                dve.wait_ge(s["rstd"], done(i))
                dve.wait_ge(s["op"], before(i))
                dve.wait_ge(s["xh"], before(i))
                for t in range(2):
                    last = nc.vector.tensor_scalar(h[:, t, :], X[:, 2 * i + t, :], mv[:, t, 0:1],
                                                   rstd[:, t:t + 1], ALU.subtract, ALU.mult)
                last.then_inc(s["h"], 1)
                dve.wait_ge(s["scp"], done(i))
                dve.wait_ge(s["pr"], before(i))
                settle(dve, s)
                for t in range(2):
                    last = nc.vector.tensor_tensor_reduce(sc[:, t, :], p_s[:, t, :], band[:, t, :], 1.0, LOWEST,
                                                          ALU.add, ALU.max, mx[:, t:t + 1])
                last.then_inc(s["sc"], 1)
                dve.wait_ge(s["sc"], done(i))
                nc.vector.tensor_scalar(nmx[:], mx[:], -1.0, None, ALU.mult).then_inc(s["nmx"], 1)
                if j is not None:
                    stats(j)
                dve.wait_ge(s["pr"], done(i))
                dve.wait_ge(s["ra"], before(i))
                nc.vector.reciprocal(rs[:], sm[:]).then_inc(s["rs"], 1)
                dve.wait_ge(s["prTp"], done(i))
                nc.vector.tensor_copy(prT[:], p_prT[:]).then_inc(s["prT"], 1)

            stats(0)
            with dve.Fori(0, B - 1) as i:
                attend(i, i + 1)
            attend(B - 1, None)

        @block.scalar
        def _(act):
            with act.Fori(0, B) as i:
                act.wait_ge(s["hTp"], done(i))
                nc.scalar.activation(hT[:], p_hT[:], ACT.Copy).then_inc(s["hT"], 1)
                act.wait_ge(s["qp"], done(i))
                nc.scalar.activation(qT[:], p_q[:], ACT.Copy).then_inc(s["q"], 1)
                act.wait_ge(s["nmx"], done(i))
                act.wait_ge(s["prTp"], before(i))
                act.wait_ge(s["rs"], before(i))
                for t in range(2):
                    last = nc.scalar.activation(pr[:, t, :], sc[:, t, :], ACT.Exp, bias=nmx[:, t:t + 1],
                                                accum_out=sm[:, t:t + 1])
                last.then_inc(s["pr"], 1)
                act.wait_ge(s["op"], done(i))
                act.wait_ge(s["rs"], done(i))
                act.wait_ge(s["xa"], before(i))
                for t in range(2):
                    last = nc.scalar.activation(ra[:, t, :], p_o[:, t, :], ACT.Relu, scale=rs[:, t:t + 1])
                last.then_inc(s["ra"], 1)

        @block.tensor
        def _(pe):
            pe.wait_ge(ld["w"], 16)
            with pe.Fori(0, B) as i:
                pe.wait_ge(s["h"], done(i))
                pe.wait_ge(s["hT"], before(i))
                for t in range(2):
                    for kb in range(KD):
                        last = nc.tensor.transpose(p_hT[:, kb, t * P:(t + 1) * P], h[:, t, kb * P:(kb + 1) * P],
                                                   k["ident"][:])
                last.then_inc(s["hTp"], 1)
                pe.wait_ge(s["hT"], done(i))
                for e in range(KD):
                    for kb in range(KD):
                        last = nc.tensor.matmul(p_q[:, e, :], W[:, kb, e * P:(e + 1) * P], hT[:, kb, :],
                                                start=kb == 0, stop=kb == KD - 1)
                last.then_inc(s["qp"], 1)
                pe.wait_ge(s["q"], done(i))
                pe.wait_ge(s["sc"], before(i))
                for t in range(2):
                    for e in range(KD):
                        last = nc.tensor.matmul(p_s[:, t, :], qT[:, e, t * P:(t + 1) * P], hT[:, e, :],
                                                start=e == 0, stop=e == KD - 1)
                last.then_inc(s["scp"], 1)
                pe.wait_ge(s["pr"], done(i))
                pe.wait_ge(s["prT"], before(i))
                for t in range(2):
                    for kb in range(2):
                        last = nc.tensor.transpose(p_prT[:, kb, t * P:(t + 1) * P], pr[:, t, kb * P:(kb + 1) * P],
                                                   k["ident"][:])
                last.then_inc(s["prTp"], 1)
                pe.wait_ge(s["prT"], done(i))
                pe.wait_ge(s["ra"], before(i))
                for t in range(2):
                    for kb in range(2):
                        last = nc.tensor.matmul(p_o[:, t, :], prT[:, kb, t * P:(t + 1) * P], h[:, kb, :],
                                                start=kb == 0, stop=kb == 1)
                last.then_inc(s["op"], 1)


def cross_attention(nc, args, X, k):
    J, C, H, DH = 77, 192, 8, 64
    C1 = C - P
    INNER = H * DH
    MB = INNER // P
    with ExitStack() as ctx:
        def sb(name, shape, dt=F32):
            return ctx.enter_context(nc.sbuf_tensor("B_" + name, shape, dt))

        def ps(name, shape):
            return ctx.enter_context(nc.psum_tensor("B_" + name, shape, F32))

        Wq, Wo, bo = sb("Wq", [P, KD, INNER]), sb("Wo", [P, MB, D]), sb("bo", [P, 2, D])
        Wk, Wv = sb("Wk", [P, 2, INNER]), sb("Wv", [P, 2, INNER])
        mask, bias = sb("mask", [P, B * J], U8), sb("bias", [P, B, J])
        cx, cxT = sb("cx", [J, C]), sb("cxT", [P, 2, J])
        st, mv = sb("st", [P, 2, 6]), sb("mv", [P, 2, 2])
        var, rstd = sb("var", [P, 2]), sb("rstd", [P, 2])
        h, hT, qT = sb("h", [P, 2, D]), sb("hT", [P, KD, S]), sb("qT", [P, MB, S])
        kT, v = sb("kT", [P, MB, J]), sb("v", [J, INNER])
        sc, pr, prT = sb("sc", [P, 2, H, J]), sb("pr", [P, 2, H, J]), sb("prT", [J, 2, H, P])
        mx, sm, rs = sb("mx", [P, 2, H]), sb("sm", [P, 2, H]), sb("rs", [P, 2, H])
        av, aT = sb("av", [P, 2, INNER]), sb("aT", [P, 2, MB, P])
        p_hT = ps("phT", [P, 2, 256])
        p_q = ps("pq", [P, 2, 512])
        p_s = ps("ps", [P, 2, 512])
        p_k = ps("pk", [P, 512])
        p_av, p_o = ps("pav", [P, INNER]), ps("po", [P, 512])
        s = semaphores(nc, ctx, "B", NORM + " settled h xb hTp hT cxp cxT kp kT vp v qp q")
        t_ = semaphores(nc, ctx, "Bt", "settled simp sc mx sub pr sm rs prTp prT avp av aTp aT op x")
        ld = semaphores(nc, ctx, "Bld", "w mask")
        cxl = semaphores(nc, ctx, "B", "cxl")["cxl"]
        block = ctx.enter_context(nc.Block())

        @block.sync
        def _(sp):
            give_credit(sp, s)
            give_credit(sp, t_)
            sp.dma_start(mask[:], args["mask_BxS2_bk0"].rearrange("b j -> (b j)").partition_broadcast(P)).then_inc(ld["mask"], 16)
            sp.dma_start(Wk[:, 0, :], args["L0_xattn_W_k"][0:P]).then_inc(ld["w"], 16)
            sp.dma_start(Wk[0:C1, 1, :], args["L0_xattn_W_k"][P:C]).then_inc(ld["w"], 16)
            sp.dma_start(Wv[:, 0, :], args["L0_xattn_W_v"][0:P]).then_inc(ld["w"], 16)
            sp.dma_start(Wv[0:C1, 1, :], args["L0_xattn_W_v"][P:C]).then_inc(ld["w"], 16)
            sp.dma_start(Wq[:], args["L0_xattn_W_q"].rearrange("(k p) n -> p k n", p=P)).then_inc(ld["w"], 16)
            sp.dma_start(Wo[:], args["L0_xattn_W_o"].rearrange("(k p) n -> p k n", p=P)).then_inc(ld["w"], 16)
            for t in range(2):
                sp.dma_start(bo[:, t, :], args["L0_xattn_b_o"].partition_broadcast(P)).then_inc(ld["w"], 16)
            with sp.Fori(0, B) as i:
                sp.wait_ge(s["cxp"], before(i))
                sp.dma_start(cx[:], args["ctx_768"][bass.ds(i, 1)].rearrange("a j c -> (a j) c")).then_inc(cxl, 16)

        @block.gpsimd
        def _(pool):
            pool.wait_ge(ld["w"], 16 * 8)
            with pool.Fori(0, B) as i:
                norm_rstd(nc, pool, s, mv, var, rstd, k, i)
                x2 = X[:, bass.ds(2 * i, 2), :]
                pool.wait_ge(s["h"], done(i))
                settle(pool, s)
                nc.gpsimd.tensor_tensor(x2, x2, bo[:], ALU.add).then_inc(s["xb"], 1)

        @block.vector
        def _(dve):
            dve.wait_ge(ld["mask"], 16)
            nc.vector.tensor_scalar(bias[:].rearrange("p b j -> p (b j)"), mask[:], 1.0, -LOWEST,
                                    ALU.subtract, ALU.mult).then_inc(ld["mask"], 1)
            dve.wait_ge(ld["mask"], 17)
            def front(j):
                norm_stats(nc, dve, s, [X[:, 2 * j, :], X[:, 2 * j + 1, :]], st, mv, j)
                dve.wait_ge(s["rstd"], done(j))
                dve.wait_ge(s["hTp"], before(j))
                for t in range(2):
                    last = nc.vector.tensor_scalar(h[:, t, :], X[:, 2 * j + t, :], mv[:, t, 0:1],
                                                   rstd[:, t:t + 1], ALU.subtract, ALU.mult)
                last.then_inc(s["h"], 1)

            def attend(i, j):
                dve.wait_ge(s["kp"], done(i))
                nc.vector.tensor_copy(kT[:], p_k[:, 0:MB * J].rearrange("p (m j) -> p m j", m=MB)).then_inc(s["kT"], 1)
                for t in range(2):
                    n = 2 * i + t
                    dve.wait_ge(t_["simp"], done(n))
                    if t == 0:
                        dve.wait_ge(t_["pr"], before(n))
                    mb = bias[:, bass.ds(i, 1), :].to_broadcast([P, 4, J])
                    for g in range(2):
                        last = nc.vector.tensor_tensor(
                            sc[:, t].rearrange("p (m g) j -> p g m j", g=2)[:, g],
                            p_s[:, g, 0:4 * J].rearrange("p (h j) -> p h j", h=4), mb, ALU.add)
                    last.then_inc(t_["sc"], 1)
                    dve.wait_ge(t_["sc"], done(n))
                    nc.vector.tensor_reduce(mx[:, t, :], sc[:, t], AX.X, ALU.max).then_inc(t_["mx"], 1)
                    dve.wait_ge(t_["mx"], done(n))
                    nc.vector.tensor_tensor(sc[:, t], sc[:, t], mx[:, t, :].unsqueeze(2).to_broadcast([P, H, J]),
                                            ALU.subtract).then_inc(t_["sub"], 1)
                if j is not None:
                    front(j)
                for t in range(2):
                    n = 2 * i + t
                    dve.wait_ge(t_["pr"], done(n))
                    nc.vector.tensor_reduce(sm[:, t, :], pr[:, t], AX.X, ALU.add).then_inc(t_["sm"], 1)
                    dve.wait_ge(t_["sm"], done(n))
                    nc.vector.reciprocal(rs[:, t, :], sm[:, t, :]).then_inc(t_["rs"], 1)
                for t in range(2):
                    n = 2 * i + t
                    dve.wait_ge(t_["rs"], done(n))
                    dve.wait_ge(t_["avp"], done(n))
                    if t == 0:
                        dve.wait_ge(t_["aTp"], before(n))
                    nc.vector.tensor_tensor(av[:, t, :].rearrange("p (h d) -> p h d", h=H),
                                            p_av[:].rearrange("p (h d) -> p h d", h=H),
                                            rs[:, t, :].unsqueeze(2).to_broadcast([P, H, DH]),
                                            ALU.mult).then_inc(t_["av"], 1)
                dve.wait_ge(s["xb"], done(i))
                for t in range(2):
                    n = 2 * i + t
                    dve.wait_ge(t_["op"], done(n))
                    xt = X[:, 2 * i + t, :]
                    nc.vector.tensor_tensor(xt, xt, p_o[:, t * D:(t + 1) * D], ALU.add).then_inc(t_["x"], 1)

            front(0)
            with dve.Fori(0, B - 1) as i:
                attend(i, i + 1)
            attend(B - 1, None)

        @block.scalar
        def _(act):
            def front(j):
                act.wait_ge(s["cxp"], done(j))
                act.wait_ge(s["vp"], before(j))
                nc.scalar.activation(cxT[:, 0, :], p_hT[:, 0, 0:J], ACT.Copy)
                nc.scalar.activation(cxT[0:C1, 1, :], p_hT[0:C1, 1, 0:J], ACT.Copy).then_inc(s["cxT"], 1)
                act.wait_ge(s["hTp"], done(j))
                nc.scalar.activation(hT[:], p_hT[:], ACT.Copy).then_inc(s["hT"], 1)

            def attend(i, j):
                act.wait_ge(s["vp"], done(i))
                nc.scalar.activation(v[:], p_s[0:J, 0, :], ACT.Copy).then_inc(s["v"], 1)
                act.wait_ge(s["qp"], done(i))
                nc.scalar.activation(qT[:].rearrange("p (a b) c -> p a (b c)", a=2), p_q[:], ACT.Copy,
                                     scale=float(DH) ** -0.5).then_inc(s["q"], 1)
                for t in range(2):
                    n = 2 * i + t
                    act.wait_ge(t_["sub"], done(n))
                    if t == 0:
                        act.wait_ge(t_["sm"], before(n))
                    nc.scalar.activation(pr[:, t], sc[:, t], ACT.Exp).then_inc(t_["pr"], 1)
                for t in range(2):
                    n = 2 * i + t
                    act.wait_ge(t_["prTp"], done(n))
                    if t == 0:
                        act.wait_ge(t_["avp"], before(n))
                    nc.scalar.activation(prT[:, t].rearrange("j (a b) q -> j a (b q)", a=2), p_q[0:J],
                                         ACT.Copy).then_inc(t_["prT"], 1)
                    if t == 0 and j is not None:
                        front(j)
                for t in range(2):
                    n = 2 * i + t
                    act.wait_ge(t_["aTp"], done(n))
                    if t == 0:
                        act.wait_ge(t_["op"], before(n))
                    nc.scalar.activation(aT[:, t], p_k[:].rearrange("p (m q) -> p m q", m=MB),
                                         ACT.Copy).then_inc(t_["aT"], 1)

            front(0)
            with act.Fori(0, B - 1) as i:
                attend(i, i + 1)
            attend(B - 1, None)

        @block.tensor
        def _(pe):
            pe.wait_ge(ld["w"], 16 * 8)

            def transposed_probs(n, t):
                pe.wait_ge(t_["pr"], done(n))
                pe.wait_ge(t_["prT"], before(n))
                for hd in range(H):
                    last = nc.tensor.transpose(p_q[0:J, hd // 4, (hd % 4) * P:(hd % 4 + 1) * P], pr[:, t, hd, :],
                                               k["ident"][:])
                last.then_inc(t_["prTp"], 1)

            def head_outputs(n, t):
                pe.wait_ge(t_["prT"], done(n))
                pe.wait_ge(t_["av"], before(n))
                for hd in range(H):
                    last = nc.tensor.matmul(p_av[:, hd * DH:(hd + 1) * DH], prT[:, t, hd, :],
                                            v[:, hd * DH:(hd + 1) * DH], start=True, stop=True)
                last.then_inc(t_["avp"], 1)

            def transposed_outputs(n, t):
                pe.wait_ge(t_["av"], done(n))
                pe.wait_ge(t_["aT"], before(n))
                for m in range(MB):
                    last = nc.tensor.transpose(p_k[:, m * P:(m + 1) * P], av[:, t, m * P:(m + 1) * P],
                                               k["ident"][:])
                last.then_inc(t_["aTp"], 1)

            def project(n, t):
                pe.wait_ge(t_["aT"], done(n))
                pe.wait_ge(t_["x"], before(n))
                for m in range(MB):
                    last = nc.tensor.matmul(p_o[:, t * D:(t + 1) * D], aT[:, t, m, :], Wo[:, m, :],
                                            start=m == 0, stop=m == MB - 1)
                last.then_inc(t_["op"], 1)

            def front_context(j):
                pe.wait_ge(cxl, 16 * j + 16)
                pe.wait_ge(s["hT"], before(j))
                nc.tensor.transpose(p_hT[:, 0, 0:J], cx[:, 0:P], k["ident"][0:J, 0:J])
                nc.tensor.transpose(p_hT[0:C1, 1, 0:J], cx[:, P:C], k["ident"][0:J, 0:J]).then_inc(s["cxp"], 1)

            def front(j):
                pe.wait_ge(s["h"], done(j))
                pe.wait_ge(s["cxT"], done(j))
                for t in range(2):
                    for kb in range(KD):
                        last = nc.tensor.transpose(p_hT[:, kb, t * P:(t + 1) * P], h[:, t, kb * P:(kb + 1) * P],
                                                   k["ident"][:])
                last.then_inc(s["hTp"], 1)

            def attend(i, j):
                pe.wait_ge(s["cxT"], done(i))
                pe.wait_ge(t_["aT"], before(2 * i))
                for m in range(MB):
                    for kb in range(2):
                        rows = P if kb == 0 else C1
                        last = nc.tensor.matmul(p_k[:, m * J:(m + 1) * J], Wk[0:rows, kb, m * P:(m + 1) * P],
                                                cxT[0:rows, kb, :], start=kb == 0, stop=kb == 1)
                last.then_inc(s["kp"], 1)
                pe.wait_ge(t_["sc"], before(2 * i))
                for kb in range(2):
                    rows = P if kb == 0 else C1
                    last = nc.tensor.matmul(p_s[0:J, 0, :], cxT[0:rows, kb, :], Wv[0:rows, kb, :],
                                            start=kb == 0, stop=kb == 1)
                last.then_inc(s["vp"], 1)
                pe.wait_ge(s["hT"], done(i))
                pe.wait_ge(t_["prT"], before(2 * i))
                for m in range(MB):
                    for kb in range(KD):
                        last = nc.tensor.matmul(p_q[:, m // 2, (m % 2) * S:(m % 2 + 1) * S],
                                                Wq[:, kb, m * P:(m + 1) * P], hT[:, kb, :],
                                                start=kb == 0, stop=kb == KD - 1)
                last.then_inc(s["qp"], 1)
                pe.wait_ge(s["q"], done(i))
                pe.wait_ge(s["kT"], done(i))
                pe.wait_ge(s["v"], done(i))
                for t in range(2):
                    n = 2 * i + t
                    if t:
                        pe.wait_ge(t_["sc"], before(n))
                    for hd in range(H):
                        r = DH * (hd % 2)
                        last = nc.tensor.matmul(p_s[:, hd % 2, (hd // 2) * J:(hd // 2 + 1) * J],
                                                qT[r:r + DH, hd // 2, t * P:(t + 1) * P], kT[r:r + DH, hd // 2, :],
                                                start=True, stop=True)
                    last.then_inc(t_["simp"], 1)
                transposed_probs(2 * i, 0)
                if j is not None:
                    front_context(j)
                head_outputs(2 * i, 0)
                if j is not None:
                    front(j)
                transposed_probs(2 * i + 1, 1)
                transposed_outputs(2 * i, 0)
                head_outputs(2 * i + 1, 1)
                project(2 * i, 0)
                transposed_outputs(2 * i + 1, 1)
                project(2 * i + 1, 1)

            front_context(0)
            front(0)
            with pe.Fori(0, B - 1) as i:
                attend(i, i + 1)
            attend(B - 1, None)

def experts(nc, args, X, k):
    E, F = 8, 1024
    BLOCKS = (B * S + E * (P - 1)) // P
    FB = F // P
    with ExitStack() as ctx:
        def sb(name, shape, dt=F32):
            return ctx.enter_context(nc.sbuf_tensor("C_" + name, shape, dt))

        place = sb("place", [P, NT], I32)
        owner = sb("owner", [P, BLOCKS], I32)
        xs_dram = nc.dram_tensor("sorted_x", (BLOCKS * P, D), F32).ap()
        ys_dram = nc.dram_tensor("sorted_y", (BLOCKS * P, D), F32).ap()
        with ExitStack() as weights:
            W1 = weights.enter_context(nc.sbuf_tensor("C_W1", [P, E, KD, F], F32))
            W2 = weights.enter_context(nc.sbuf_tensor("C_W2", [P, E, FB, D], F32))
            loaded = semaphores(nc, weights, "C", "loaded")["loaded"]
            route(nc, args, X, k, place, owner, xs_dram, W1, W2, loaded, E, F, BLOCKS)
            expert_blocks(nc, args, k, owner, xs_dram, ys_dram, W1, W2, loaded, E, F, BLOCKS)
        gather_rows(nc, X, place, ys_dram)


def route(nc, args, X, k, place, owner, xs_dram, W1, W2, loaded, E, F, BLOCKS):
    with ExitStack() as ctx:
        def sb(name, shape, dt=F32):
            return ctx.enter_context(nc.sbuf_tensor("R_" + name, shape, dt))

        def ps(name, shape):
            return ctx.enter_context(nc.psum_tensor("R_" + name, shape, F32))

        rw, rb = sb("rw", [P, KD, E]), sb("rb", [P, E])
        st, mv = sb("st", [P, 2, 6]), sb("mv", [P, 2, 2])
        var, rstd = sb("var", [P, 2]), sb("rstd", [P, 2])
        h, hT = sb("h", [P, 2, D]), sb("hT", [P, KD, S])
        lg, top, at, atf = sb("lg", [P, 2, E]), sb("top", [P, 2, 8]), sb("at", [P, 2, 8], U32), sb("atf", [P, 2])
        number = sb("number", [P, E])
        hot = sb("hot", [P, NT, E])
        ones, tri = sb("ones", [P, P]), sb("tri", [P, P])
        tot, cum, row = sb("tot", [P, NT, E]), sb("cum", [P, NT, E]), sb("row", [P, NT, E])
        nbi, nb, nbx, end = sb("nbi", [P, E], I32), sb("nb", [P, E]), sb("nbx", [P, E]), sb("end", [P, E])
        start = sb("start", [P, E])
        number_b, past = sb("number_b", [P, BLOCKS, E]), sb("past", [P, BLOCKS, E])
        placef, ownerf = sb("placef", [P, NT]), sb("ownerf", [P, BLOCKS])
        p_hT, p_lg = ps("phT", [P, 2, 256]), ps("plg", [P, 512])
        p_in, p_tot = ps("pin", [P, 512]), ps("ptot", [P, 512])
        s = semaphores(nc, ctx, "R", NORM + " settled h hTp hT lgp lg top at atf hot")
        c = semaphores(nc, ctx, "Rc", "number ones tri counts_in counts_tot tot cum step place owner zeroed scattered")
        ld = semaphores(nc, ctx, "R", "ld")["ld"]
        block = ctx.enter_context(nc.Block())

        @block.sync
        def _(sp):
            give_credit(sp, s)
            sp.dma_start(rw[:], args["L0_ffn_router_w"].rearrange("(k p) e -> p k e", p=P)).then_inc(ld, 16)
            sp.dma_start(rb[:], args["L0_ffn_router_b"].partition_broadcast(P)).then_inc(ld, 16)
            sp.dma_start(xs_dram.rearrange("(p b) d -> p (b d)", p=P).rearrange("p (c z) -> p c z", z=P),
                         k["zero"][:].unsqueeze(1).to_broadcast([P, 2 * BLOCKS, P])).then_inc(c["zeroed"], 16)
            for e in range(E):
                sp.dma_start(W1[:, e], args["L0_ffn_W1"][e].rearrange("(k p) f -> p k f", p=P)).then_inc(loaded, 16)
                sp.dma_start(W2[:, e], args["L0_ffn_W2"][e].rearrange("(k p) d -> p k d", p=P)).then_inc(loaded, 16)

        @block.gpsimd
        def _(pool):
            nc.gpsimd.iota(number[:], [[1, E]], base=0, channel_multiplier=0,
                           allow_small_or_imprecise_dtypes=True).then_inc(c["number"], 1)
            nc.gpsimd.iota(number_b[:], [[1, BLOCKS], [0, E]], base=0, channel_multiplier=0,
                           allow_small_or_imprecise_dtypes=True).then_inc(c["number"], 1)
            nc.gpsimd.memset(ones[:], 1.0).then_inc(c["ones"], 1)
            pool.wait_ge(c["ones"], 1)
            nc.gpsimd.affine_select(out=tri[:], in_=ones[:], compare_op=ALU.is_gt, fill=0.0, base=0,
                                    pattern=[[1, P]], channel_multiplier=-1).then_inc(c["tri"], 1)
            with pool.Fori(0, B) as i:
                norm_rstd(nc, pool, s, mv, var, rstd, k, i)
            pool.wait_ge(c["place"], 2)
            pool.wait_ge(c["zeroed"], 16)
            for n in range(NT):
                nc.gpsimd.indirect_dma_start(
                    out=xs_dram, out_offset=bass.IndirectOffsetOnAxis(ap=place[:, n:n + 1].bitcast(U32), axis=0),
                    in_=X[:, n, :], in_offset=None).then_inc(c["scattered"], 16)
            pool.wait_ge(c["scattered"], 16 * NT)

        @block.vector
        def _(dve):
            dve.wait_ge(ld, 32)
            dve.wait_ge(c["number"], 2)

            def stats(j):
                norm_stats(nc, dve, s, [X[:, 2 * j, :], X[:, 2 * j + 1, :]], st, mv, j)

            def normalise(j):
                dve.wait_ge(s["rstd"], done(j))
                dve.wait_ge(s["hTp"], before(j))
                for t in range(2):
                    last = nc.vector.tensor_scalar(h[:, t, :], X[:, 2 * j + t, :], mv[:, t, 0:1],
                                                   rstd[:, t:t + 1], ALU.subtract, ALU.mult)
                last.then_inc(s["h"], 1)

            def choose(i, j):
                if j is not None:
                    stats(j)
                dve.wait_ge(s["lgp"], done(i))
                nc.vector.tensor_tensor(lg[:], p_lg[:, 0:2 * E].rearrange("p (t e) -> p t e", t=2),
                                        rb[:].unsqueeze(1).to_broadcast([P, 2, E]), ALU.add).then_inc(s["lg"], 1)
                dve.wait_ge(s["lg"], done(i))
                settle(dve, s)
                for t in range(2):
                    last = nc.vector.max(top[:, t, :], lg[:, t, :])
                last.then_inc(s["top"], 1)
                if j is not None:
                    normalise(j)
                dve.wait_ge(s["top"], done(i))
                settle(dve, s)
                for t in range(2):
                    last = nc.vector.max_index(at[:, t, :], top[:, t, :], lg[:, t, :])
                last.then_inc(s["at"], 1)
                dve.wait_ge(s["at"], done(i))
                nc.vector.tensor_copy(atf[:], at[:, :, 0]).then_inc(s["atf"], 1)
                dve.wait_ge(s["atf"], done(i))
                for t in range(2):
                    last = nc.vector.tensor_scalar(hot[:, 2 * i + t, :], number[:], atf[:, t:t + 1], None,
                                                   ALU.is_equal)
                last.then_inc(s["hot"], 1)

            stats(0)
            normalise(0)
            with dve.Fori(0, B - 1) as i:
                choose(i, i + 1)
            choose(B - 1, None)
            steps = 0

            def step(instruction):
                nonlocal steps
                steps += 1
                instruction.then_inc(c["step"], 1)
                dve.wait_ge(c["step"], steps)

            dve.wait_ge(c["counts_tot"], 1)
            step(nc.vector.tensor_copy(tot[:], p_tot[:, 0:NT * E].rearrange("p (n e) -> p n e", e=E)))
            for e in range(E):
                last = nc.vector.tensor_tensor_scan(cum[:, :, e], ones[:, 0:NT], tot[:, :, e], 0.0, ALU.mult, ALU.add)
            step(last)
            step(nc.vector.tensor_scalar(nbx[:], cum[:, NT - 1, :], float(P - 1), 1.0 / P, ALU.add, ALU.mult))
            step(nc.vector.tensor_scalar(nbi[:], nbx[:], -(P - 1) / (2.0 * P), None, ALU.add))
            step(nc.vector.tensor_copy(nb[:], nbi[:]))
            step(nc.vector.tensor_tensor_scan(end[:], ones[:, 0:E], nb[:], 0.0, ALU.mult, ALU.add))
            step(nc.vector.tensor_tensor(start[:], end[:], nb[:], ALU.subtract))
            step(nc.vector.tensor_scalar(start[:], start[:], float(P), None, ALU.mult))
            step(nc.vector.tensor_tensor(row[:], cum[:], tot[:], ALU.subtract))
            step(nc.vector.tensor_tensor(row[:], row[:], p_in[:, 0:NT * E].rearrange("p (n e) -> p n e", e=E), ALU.add))
            step(nc.vector.tensor_tensor(row[:], row[:], start[:].unsqueeze(1).to_broadcast([P, NT, E]), ALU.add))
            step(nc.vector.tensor_tensor(row[:], row[:], hot[:], ALU.mult))
            nc.vector.tensor_reduce(placef[:], row[:], AX.X, ALU.add).then_inc(c["place"], 1)
            dve.wait_ge(c["place"], 1)
            nc.vector.tensor_copy(place[:], placef[:]).then_inc(c["place"], 1)
            step(nc.vector.tensor_tensor(past[:], number_b[:], end[:].unsqueeze(1).to_broadcast([P, BLOCKS, E]),
                                         ALU.is_ge))
            step(nc.vector.tensor_reduce(ownerf[:], past[:], AX.X, ALU.add))
            nc.vector.tensor_scalar(owner[:], ownerf[:], float(E - 1), None, ALU.min).then_inc(c["owner"], 1)
            dve.wait_ge(c["owner"], 1)

        @block.scalar
        def _(act):
            with act.Fori(0, B) as i:
                act.wait_ge(s["hTp"], done(i))
                act.wait_ge(s["lgp"], before(i))
                nc.scalar.activation(hT[:], p_hT[:], ACT.Copy).then_inc(s["hT"], 1)

        @block.tensor
        def _(pe):
            pe.wait_ge(ld, 32)

            def turn(j):
                pe.wait_ge(s["h"], done(j))
                pe.wait_ge(s["hT"], before(j))
                for t in range(2):
                    for kb in range(KD):
                        last = nc.tensor.transpose(p_hT[:, kb, t * P:(t + 1) * P], h[:, t, kb * P:(kb + 1) * P],
                                                   k["ident"][:])
                last.then_inc(s["hTp"], 1)

            def logits(i):
                pe.wait_ge(s["hT"], done(i))
                pe.wait_ge(s["lg"], before(i))
                for t in range(2):
                    for kb in range(KD):
                        last = nc.tensor.matmul(p_lg[:, t * E:(t + 1) * E], hT[:, kb, t * P:(t + 1) * P],
                                                rw[:, kb, :], start=kb == 0, stop=kb == KD - 1)
                last.then_inc(s["lgp"], 1)

            turn(0)
            with pe.Fori(0, B - 1) as i:
                logits(i)
                turn(i + 1)
            logits(B - 1)
            pe.wait_ge(s["hot"], done(B - 1))
            pe.wait_ge(c["tri"], 1)
            every = hot[:].rearrange("p n e -> p (n e)")
            nc.tensor.matmul(p_in[:, 0:NT * E], tri[:], every, start=True, stop=True).then_inc(c["counts_in"], 1)
            nc.tensor.matmul(p_tot[:, 0:NT * E], ones[:], every, start=True, stop=True).then_inc(c["counts_tot"], 1)


def expert_blocks(nc, args, k, owner, xs_dram, ys_dram, W1, W2, loaded, E, F, BLOCKS):
    FB = F // P
    with ExitStack() as ctx:
        def sb(name, shape, dt=F32):
            return ctx.enter_context(nc.sbuf_tensor("F_" + name, shape, dt))

        def ps(name, shape):
            return ctx.enter_context(nc.psum_tensor("F_" + name, shape, F32))

        xs, b1, b2 = sb("xs", [P, D]), sb("b1", [P, F]), sb("b2", [P, D])
        st, mv = sb("st", [P, 1, 6]), sb("mv", [P, 1, 2])
        var, rstd = sb("var", [P, 1]), sb("rstd", [P, 1])
        h, hT = sb("h", [P, D]), sb("hT", [P, KD, P])
        u, uT, y = sb("u", [P, F]), sb("uT", [P, FB, P]), sb("y", [P, D])
        p_hT, p_u, p_uT, p_y = ps("phT", [P, 512]), ps("pu", [P, 2, 512]), ps("puT", [P, 2, 512]), ps("py", [P, 512])
        s = semaphores(nc, ctx, "F", NORM + " settled h hTp hT up u uTp uT yp y")
        dma = semaphores(nc, ctx, "Fd", "xs b1 b2 stored")
        block = ctx.enter_context(nc.Block())

        @block.sync
        def _(sp):
            give_credit(sp, s)
            sp.sem_inc(dma["stored"], 16)
            with sp.Fori(0, BLOCKS) as i:
                e = sp.value_load(owner[0:1, bass.ds(i, 1)], min_val=0, max_val=E - 1)
                sp.wait_ge(s["u"], before(i))
                sp.dma_start(b1[:], args["L0_ffn_b1"][bass.ds(e, 1)].rearrange("a f -> (a f)").partition_broadcast(P)
                             ).then_inc(dma["b1"], 16)
                sp.wait_ge(s["y"], before(i))
                sp.dma_start(b2[:], args["L0_ffn_b2"][bass.ds(e, 1)].rearrange("a f -> (a f)").partition_broadcast(P)
                             ).then_inc(dma["b2"], 16)

        @block.gpsimd
        def _(pool):
            pool.dma_start(xs[:], xs_dram[0:P]).then_inc(dma["xs"], 16)
            with pool.Fori(0, BLOCKS - 1) as i:
                norm_rstd(nc, pool, s, mv, var, rstd, k, i)
                pool.wait_ge(s["h"], done(i))
                pool.dma_start(xs[:], xs_dram[bass.ds((i + 1) * P, P)]).then_inc(dma["xs"], 16)
            norm_rstd(nc, pool, s, mv, var, rstd, k, BLOCKS - 1)

        @block.vector
        def _(dve):
            def normalise(i):
                dve.wait_ge(dma["xs"], 16 * i + 16)
                norm_stats(nc, dve, s, [xs[:]], st, mv, i)
                dve.wait_ge(s["rstd"], done(i))
                dve.wait_ge(s["hTp"], before(i))
                nc.vector.tensor_scalar(h[:], xs[:], mv[:, 0, 0:1], rstd[:, 0:1], ALU.subtract,
                                        ALU.mult).then_inc(s["h"], 1)

            def add_b1(i):
                dve.wait_ge(s["up"], done(i))
                dve.wait_ge(dma["b1"], 16 * i + 16)
                dve.wait_ge(s["uTp"], before(i))
                nc.vector.tensor_tensor(u[:].rearrange("p (a f) -> p a f", a=2), p_u[:],
                                        b1[:].rearrange("p (a f) -> p a f", a=2), ALU.add).then_inc(s["u"], 1)

            def add_b2(i):
                dve.wait_ge(s["yp"], done(i))
                dve.wait_ge(dma["b2"], 16 * i + 16)
                dve.wait_ge(dma["stored"], 16 * i + 16)
                nc.vector.tensor_tensor(y[:], p_y[:, 0:D], b2[:], ALU.add).then_inc(s["y"], 1)

            def copy_hT(i):
                dve.wait_ge(s["hTp"], done(i))
                dve.wait_ge(s["up"], before(i))
                nc.vector.tensor_copy(hT[:], p_hT[:, 0:D].rearrange("p (k q) -> p k q", k=KD)).then_inc(s["hT"], 1)

            normalise(0)
            copy_hT(0)
            normalise(1)
            add_b1(0)
            with dve.Fori(0, BLOCKS - 2) as i:
                copy_hT(i + 1)
                normalise(i + 2)
                add_b1(i + 1)
                add_b2(i)
            copy_hT(BLOCKS - 1)
            add_b1(BLOCKS - 1)
            add_b2(BLOCKS - 2)
            add_b2(BLOCKS - 1)

        @block.scalar
        def _(act):
            def gelu(i):
                act.wait_ge(s["uTp"], done(i))
                act.wait_ge(s["yp"], before(i))
                nc.scalar.activation(uT[:].rearrange("p (a b) q -> p a (b q)", a=2), p_uT[:],
                                     ACT.Gelu).then_inc(s["uT"], 1)

            def store(i):
                act.wait_ge(s["y"], done(i))
                act.dma_start(ys_dram[bass.ds(i * P, P)] if not isinstance(i, int) else ys_dram[i * P:(i + 1) * P],
                              y[:]).then_inc(dma["stored"], 16)

            gelu(0)
            with act.Fori(0, BLOCKS - 1) as i:
                gelu(i + 1)
                store(i)
            store(BLOCKS - 1)
            act.wait_ge(dma["stored"], 16 * (BLOCKS + 1))

        @block.tensor
        def _(pe):
            def first(i):
                pe.wait_ge(s["h"], done(i))
                pe.wait_ge(s["hT"], before(i))
                for kb in range(KD):
                    last = nc.tensor.transpose(p_hT[:, kb * P:(kb + 1) * P], h[:, kb * P:(kb + 1) * P], k["ident"][:])
                last.then_inc(s["hTp"], 1)
                e = pe.value_load(owner[0:1, bass.ds(i, 1)], min_val=0, max_val=E - 1)
                pe.wait_ge(s["hT"], done(i))
                pe.wait_ge(s["u"], before(i))
                for kb in range(KD):
                    for f in range(2):
                        last = nc.tensor.matmul(p_u[:, f, :], hT[:, kb, :],
                                                W1[:, bass.ds(e, 1), kb, f * 512:(f + 1) * 512],
                                                start=kb == 0, stop=kb == KD - 1)
                last.then_inc(s["up"], 1)

            def turn(i):
                pe.wait_ge(s["u"], done(i))
                pe.wait_ge(s["uT"], before(i))
                for f in range(FB):
                    last = nc.tensor.transpose(p_uT[:, f // 4, (f % 4) * P:(f % 4 + 1) * P],
                                               u[:, f * P:(f + 1) * P], k["ident"][:])
                last.then_inc(s["uTp"], 1)

            def second(i):
                e = pe.value_load(owner[0:1, bass.ds(i, 1)], min_val=0, max_val=E - 1)
                pe.wait_ge(s["uT"], done(i))
                pe.wait_ge(s["y"], before(i))
                for f in range(FB):
                    last = nc.tensor.matmul(p_y[:, 0:D], uT[:, f, :], W2[:, bass.ds(e, 1), f, :],
                                            start=f == 0, stop=f == FB - 1)
                last.then_inc(s["yp"], 1)

            pe.wait_ge(loaded, 32 * E)
            first(0)
            with pe.Fori(0, BLOCKS - 1) as i:
                turn(i)
                first(i + 1)
                second(i)
            turn(BLOCKS - 1)
            second(BLOCKS - 1)


def gather_rows(nc, X, place, ys_dram):
    with ExitStack() as ctx:
        y = ctx.enter_context(nc.sbuf_tensor("G_y", [P, NT, D], F32))
        fetched = list(semaphores(nc, ctx, "G", " ".join(f"fetched{n}" for n in range(NT))).values())
        block = ctx.enter_context(nc.Block())

        @block.gpsimd
        def _(pool):
            for n in range(NT):
                nc.gpsimd.indirect_dma_start(
                    out=y[:, n, :], out_offset=None, in_=ys_dram,
                    in_offset=bass.IndirectOffsetOnAxis(ap=place[:, n:n + 1].bitcast(U32), axis=0)
                ).then_inc(fetched[n], 16)

        @block.vector
        def _(dve):
            for n in range(NT):
                dve.wait_ge(fetched[n], 16)
                nc.vector.tensor_tensor(X[:, n, :], X[:, n, :], y[:, n, :], ALU.add)


def rwkv(nc, args, X, k):
    T, FF = B, 4 * D
    FB = FF // P
    COLUMNS = ("ln1_g", "ln1_b", "ln2_g", "ln2_b", "time_mix_k", "time_mix_v", "time_mix_r", "cmix_k", "cmix_r",
               "time_first", "time_decay")
    with ExitStack() as ctx:
        def sb(name, shape, dt=F32):
            return ctx.enter_context(nc.sbuf_tensor("D_" + name, shape, dt))

        def ps(name, shape):
            return ctx.enter_context(nc.psum_tensor("D_" + name, shape, F32))

        col = {c: sb(c, [P, KD]) for c in COLUMNS}
        decay = sb("decay", [P, KD])
        Wkvr, Wo = sb("Wkvr", [P, 3, KD, D]), sb("Wo", [P, KD, D])
        Wck, Wcv, Wcr = sb("Wck", [P, KD, FF]), sb("Wcv", [P, FB, D]), sb("Wcr", [P, KD, D])
        st, mv, var, rstd = sb("st", [P, 2, 6]), sb("mv", [P, 2, 2]), sb("var", [P, 2]), sb("rstd", [P, 2])
        v2, rstd2 = sb("v2", [P, 2]), sb("rstd2", [P, 2])
        st2, mv2, var2, rstd3 = sb("st2", [P, 2, 6]), sb("mv2", [P, 2, 2]), sb("var2", [P, 2]), sb("rstd3", [P, 2])
        h, hk, n1, x1, n2 = (sb(n, [P, 2, D]) for n in ("h", "hk", "n1", "x1", "n2"))
        xx, xs, dx = (sb(n, [P, KD, S]) for n in ("xx", "xs", "dx"))
        yy, ys, dy = (sb(n, [P, KD, S]) for n in ("yy", "ys", "dy"))
        mix, cmix = sb("mix", [P, 3, KD, S]), sb("cmix", [P, 2, KD, S])
        key, val, gate = (sb(n, [P, KD, S]) for n in ("key", "val", "gate"))
        aa, bb, pp, ppn = (sb(n, [P, KD, S]) for n in ("aa", "bb", "pp", "ppn"))
        qq = sb("qq", [P, KD, S])
        d12, d34 = sb("d12", [P, 2, KD, S]), sb("d34", [P, 2, KD, S])
        e12, e34 = sb("e12", [P, 2, KD, S]), sb("e34", [P, 2, KD, S])
        num, nv, den, rw = (sb(n, [P, KD, S]) for n in ("num", "nv", "den", "rw"))
        av, bv = sb("av", [P, KD, S]), sb("bv", [P, KD, S])
        gate2, g2 = sb("gate2", [P, 2, D]), sb("g2", [P, 2, D])
        rl, kk = sb("rl", [P, 4, S]), sb("kk", [P, FB, S])
        p_T = ps("pT", [P, KD, S])
        p_kvr = ps("pkvr", [P, 3, KD, S])
        p_o = ps("po", [P, 2, D])
        p_kk, p_vv = ps("pkk", [P, 4, S]), ps("pvv", [P, 2, D])
        s = semaphores(nc, ctx, "D", NORM + " settled h hk v2a v2b v2 rstd2 n1 T1 xx dx mix xs kvr key val gate "
                       "qq d12 e12 ppn d34 e34 pp e1aa e2v num e1bb den inv nr rw e3aa av aa e3bb bb op x1")
        z = semaphores(nc, ctx, "Dc", NORM + " settled n2 T2 yy dy cmix ys rr gate2 kkp0 kkp1 rl0 rl1 kk0 kk1 vvp xx1 g2 x")
        ld = semaphores(nc, ctx, "Dld", "w cols exp decay init")
        block = ctx.enter_context(nc.Block())

        @block.sync
        def _(sp):
            give_credit(sp, s)
            give_credit(sp, z)
            with nc.allow_non_contiguous_dma(reason="a few columns of a value a channel"):
                for c in COLUMNS:
                    sp.dma_start(col[c][:], args["L1_attn_" + c].rearrange("(k p) -> p k", p=P)).then_inc(ld["cols"], 16)
            for m, w in enumerate(("Wk", "Wv", "Wr")):
                sp.dma_start(Wkvr[:, m], args["L1_attn_" + w].rearrange("(k p) o -> p k o", p=P)).then_inc(ld["w"], 16)
            for w, to in (("Wo", Wo), ("Wck", Wck), ("Wcv", Wcv), ("Wcr", Wcr)):
                sp.dma_start(to[:], args["L1_attn_" + w].rearrange("(k p) o -> p k o", p=P)).then_inc(ld["w"], 16)

        @block.gpsimd
        def _(pool):
            for x in (xs, ys, aa, bb):
                nc.gpsimd.memset(x[:], 0.0).then_inc(ld["init"], 1)
            nc.gpsimd.memset(pp[:], -1e38).then_inc(ld["init"], 1)
            pool.wait_ge(ld["init"], 5)

            def norm1(t):
                norm_rstd(nc, pool, s, mv, var, rstd, k, t)
                pool.wait_ge(s["rstd"], done(t))
                nc.gpsimd.tensor_tensor(v2[:], mv[:, :, 1], rstd[:], ALU.mult).then_inc(s["v2a"], 1)
                pool.wait_ge(s["v2a"], done(t))
                nc.gpsimd.tensor_tensor(v2[:], v2[:], rstd[:], ALU.mult).then_inc(s["v2b"], 1)
                pool.wait_ge(s["v2b"], done(t))
                settle(pool, s)
                nc.gpsimd.tensor_scalar(v2[:], v2[:], EPS, None, ALU.add).then_inc(s["v2"], 1)
                pool.wait_ge(s["v2"], done(t))
                pool.wait_ge(s["n1"], before(t))
                nc.gpsimd.tensor_tensor(rstd2[:], v2[:], k["minus_half"][:], ALU.pow).then_inc(s["rstd2"], 1)

            def keep_xx(t):
                pool.wait_ge(s["mix"], done(t))
                settle(pool, s)
                nc.gpsimd.tensor_copy(xs[:], xx[:]).then_inc(s["xs"], 1)

            def keep_yy(t):
                pool.wait_ge(z["cmix"], done(t))
                settle(pool, s)
                nc.gpsimd.tensor_copy(ys[:], yy[:]).then_inc(z["ys"], 1)

            def add_x1(t):
                x2 = X[:, bass.ds(2 * t, 2), :] if not isinstance(t, int) else X[:, 2 * t:2 * t + 2, :]
                pool.wait_ge(s["x1"], done(t))
                settle(pool, s)
                nc.gpsimd.tensor_tensor(x2, x2, x1[:], ALU.add).then_inc(z["xx1"], 1)

            def numerator(t):
                pool.wait_ge(s["e12"], done(t))
                pool.wait_ge(s["val"], done(t))
                nc.gpsimd.tensor_tensor(nv[:], e12[:, 1], val[:], ALU.mult).then_inc(s["e2v"], 1)
                pool.wait_ge(s["e1aa"], done(t))
                pool.wait_ge(s["e2v"], done(t))
                nc.gpsimd.tensor_tensor(num[:], num[:], nv[:], ALU.add).then_inc(s["num"], 1)

            def state(t):
                pool.wait_ge(s["e34"], done(t))
                pool.wait_ge(s["val"], done(t))
                nc.gpsimd.tensor_tensor(av[:], e34[:, 1], val[:], ALU.mult).then_inc(s["av"], 1)
                pool.wait_ge(s["e1bb"], done(t))
                nc.gpsimd.tensor_tensor(bb[:], e34[:, 0], bb[:], ALU.mult).then_inc(s["e3bb"], 1)
                pool.wait_ge(s["e1aa"], done(t))
                nc.gpsimd.tensor_tensor(aa[:], e34[:, 0], aa[:], ALU.mult).then_inc(s["e3aa"], 1)
                pool.wait_ge(s["e3bb"], done(t))
                nc.gpsimd.tensor_tensor(bb[:], bb[:], e34[:, 1], ALU.add).then_inc(s["bb"], 1)
                pool.wait_ge(s["e3aa"], done(t))
                pool.wait_ge(s["av"], done(t))
                nc.gpsimd.tensor_tensor(aa[:], aa[:], av[:], ALU.add).then_inc(s["aa"], 1)
                settle(pool, s)
                nc.gpsimd.tensor_copy(pp[:], ppn[:]).then_inc(s["pp"], 1)

            def round(t, last_t, next_t):
                if last_t is not None:
                    norm_rstd(nc, pool, z, mv2, var2, rstd3, k, last_t)
                if next_t is not None:
                    norm1(next_t)
                if last_t is not None:
                    keep_yy(last_t)
                    add_x1(last_t)
                numerator(t)
                state(t)
                if next_t is not None:
                    keep_xx(next_t)

            norm1(0)
            keep_xx(0)
            round(0, None, 1)
            with pool.Fori(1, T - 1) as t:
                round(t, t - 1, t + 1)
            round(T - 1, T - 2, None)
            norm_rstd(nc, pool, z, mv2, var2, rstd3, k, T - 1)
            keep_yy(T - 1)
            add_x1(T - 1)

        @block.vector
        def _(dve):
            dve.wait_ge(ld["exp"], 1)
            nc.vector.tensor_scalar(decay[:], decay[:], -1.0, None, ALU.mult).then_inc(ld["decay"], 1)
            dve.wait_ge(ld["decay"], 1)
            dve.wait_ge(ld["init"], 5)

            def norm1(t):
                norm_stats(nc, dve, s, [X[:, 2 * t, :], X[:, 2 * t + 1, :]], st, mv, t)
                dve.wait_ge(s["rstd"], done(t))
                dve.wait_ge(s["hk"], before(t))
                for a in range(2):
                    last = nc.vector.tensor_scalar(h[:, a, :], X[:, 2 * t + a, :], mv[:, a, 0:1], rstd[:, a:a + 1],
                                                   ALU.subtract, ALU.mult)
                last.then_inc(s["h"], 1)
                dve.wait_ge(s["h"], done(t))
                dve.wait_ge(s["rstd2"], done(t))
                dve.wait_ge(s["T1"], before(t))
                for a in range(2):
                    last = nc.vector.tensor_scalar(n1[:, a, :], h[:, a, :], rstd2[:, a:a + 1], None, ALU.mult)
                last.then_inc(s["n1"], 1)

            def mixes(t):
                dve.wait_ge(s["xx"], done(t))
                dve.wait_ge(s["xs"], before(t))
                nc.vector.tensor_tensor(dx[:], xx[:], xs[:], ALU.subtract).then_inc(s["dx"], 1)
                dve.wait_ge(s["dx"], done(t))
                dve.wait_ge(s["kvr"], before(t))
                for m, c in enumerate(("time_mix_k", "time_mix_v", "time_mix_r")):
                    for kb in range(KD):
                        last = nc.vector.scalar_tensor_tensor(
                            out=mix[:, m, kb, :], in0=dx[:, kb, :], scalar=col[c][:, kb:kb + 1], in1=xs[:, kb, :],
                            op0=ALU.mult, op1=ALU.add)
                last.then_inc(s["mix"], 1)

            def wkv(t):
                dve.wait_ge(s["key"], done(t))
                dve.wait_ge(s["pp"], before(t))
                for kb in range(KD):
                    last = nc.vector.scalar_tensor_tensor(
                        out=qq[:, kb, :], in0=key[:, kb, :], scalar=col["time_first"][:, kb:kb + 1],
                        in1=pp[:, kb, :], op0=ALU.add, op1=ALU.max)
                last.then_inc(s["qq"], 1)
                for kb in range(KD):
                    last = nc.vector.scalar_tensor_tensor(
                        out=ppn[:, kb, :], in0=pp[:, kb, :], scalar=decay[:, kb:kb + 1], in1=key[:, kb, :],
                        op0=ALU.add, op1=ALU.max)
                last.then_inc(s["ppn"], 1)
                dve.wait_ge(s["qq"], done(t))
                dve.wait_ge(s["e12"], before(t))
                nc.vector.tensor_tensor(d12[:, 0], pp[:], qq[:], ALU.subtract)
                for kb in range(KD):
                    last = nc.vector.scalar_tensor_tensor(
                        out=d12[:, 1, kb, :], in0=key[:, kb, :], scalar=col["time_first"][:, kb:kb + 1],
                        in1=qq[:, kb, :], op0=ALU.add, op1=ALU.subtract)
                last.then_inc(s["d12"], 1)
                dve.wait_ge(s["ppn"], done(t))
                dve.wait_ge(s["e34"], before(t))
                nc.vector.tensor_tensor(d34[:, 1], key[:], ppn[:], ALU.subtract)
                for kb in range(KD):
                    last = nc.vector.scalar_tensor_tensor(
                        out=d34[:, 0, kb, :], in0=pp[:, kb, :], scalar=decay[:, kb:kb + 1],
                        in1=ppn[:, kb, :], op0=ALU.add, op1=ALU.subtract)
                last.then_inc(s["d34"], 1)
                dve.wait_ge(s["e12"], done(t))
                dve.wait_ge(s["bb"], before(t))
                nc.vector.tensor_tensor(den[:], e12[:, 0], bb[:], ALU.mult).then_inc(s["e1bb"], 1)
                dve.wait_ge(s["aa"], before(t))
                nc.vector.tensor_tensor(num[:], e12[:, 0], aa[:], ALU.mult).then_inc(s["e1aa"], 1)
                dve.wait_ge(s["e1bb"], done(t))
                nc.vector.tensor_tensor(den[:], den[:], e12[:, 1], ALU.add).then_inc(s["den"], 1)
                dve.wait_ge(s["den"], done(t))
                nc.vector.reciprocal(den[:], den[:]).then_inc(s["inv"], 1)
                dve.wait_ge(s["inv"], done(t))
                dve.wait_ge(s["num"], done(t))
                nc.vector.tensor_tensor(num[:], num[:], den[:], ALU.mult).then_inc(s["nr"], 1)
                dve.wait_ge(s["nr"], done(t))
                dve.wait_ge(s["gate"], done(t))
                dve.wait_ge(s["op"], before(t))
                nc.vector.scalar_tensor_tensor(out=rw[:], in0=gate[:], scalar=1.0, in1=num[:], op0=ALU.add,
                                               op1=ALU.mult).then_inc(s["rw"], 1)

            def residual(t):
                dve.wait_ge(s["op"], done(t))
                dve.wait_ge(z["xx1"], before(t))
                dve.wait_ge(z["n2"], before(t))
                dve.wait_ge(s["hk"], done(t))
                nc.vector.scalar_tensor_tensor(out=x1[:], in0=p_o[:], scalar=0.5, in1=hk[:], op0=ALU.mult,
                                               op1=ALU.add).then_inc(s["x1"], 1)

            def norm2(t):
                dve.wait_ge(s["x1"], done(t))
                norm_stats(nc, dve, z, [x1[:, 0, :], x1[:, 1, :]], st2, mv2, t)
                dve.wait_ge(z["rstd"], done(t))
                dve.wait_ge(z["T2"], before(t))
                for a in range(2):
                    last = nc.vector.tensor_scalar(n2[:, a, :], x1[:, a, :], mv2[:, a, 0:1], rstd3[:, a:a + 1],
                                                   ALU.subtract, ALU.mult)
                last.then_inc(z["n2"], 1)

            def channel_mixes(t):
                dve.wait_ge(z["yy"], done(t))
                dve.wait_ge(z["ys"], before(t))
                nc.vector.tensor_tensor(dy[:], yy[:], ys[:], ALU.subtract).then_inc(z["dy"], 1)
                dve.wait_ge(z["dy"], done(t))
                dve.wait_ge(z["vvp"], before(t))
                for m, c in enumerate(("cmix_k", "cmix_r")):
                    for kb in range(KD):
                        last = nc.vector.scalar_tensor_tensor(
                            out=cmix[:, m, kb, :], in0=dy[:, kb, :], scalar=col[c][:, kb:kb + 1], in1=ys[:, kb, :],
                            op0=ALU.mult, op1=ALU.add)
                last.then_inc(z["cmix"], 1)

            def finish(t):
                x2 = X[:, bass.ds(2 * t, 2), :] if not isinstance(t, int) else X[:, 2 * t:2 * t + 2, :]
                dve.wait_ge(z["vvp"], done(t))
                dve.wait_ge(z["gate2"], done(t))
                nc.vector.scalar_tensor_tensor(out=g2[:], in0=gate2[:], scalar=1.0, in1=p_vv[:], op0=ALU.add,
                                               op1=ALU.mult).then_inc(z["g2"], 1)
                dve.wait_ge(z["g2"], done(t))
                dve.wait_ge(z["xx1"], done(t))
                nc.vector.scalar_tensor_tensor(out=x2, in0=g2[:], scalar=0.5, in1=x2, op0=ALU.mult,
                                               op1=ALU.add).then_inc(z["x"], 1)

            def round(t, last_t, next_t):
                if last_t is not None:
                    norm2(last_t)
                nc.vector.tensor_copy(hk[:], h[:]).then_inc(s["hk"], 1)
                if next_t is not None:
                    norm1(next_t)
                if last_t is not None:
                    channel_mixes(last_t)
                wkv(t)
                if next_t is not None:
                    mixes(next_t)
                if last_t is not None:
                    finish(last_t)
                residual(t)

            norm1(0)
            mixes(0)
            round(0, None, 1)
            with dve.Fori(1, T - 1) as t:
                round(t, t - 1, t + 1)
            round(T - 1, T - 2, None)
            norm2(T - 1)
            channel_mixes(T - 1)
            finish(T - 1)

        @block.scalar
        def _(act):
            act.wait_ge(ld["cols"], 16 * len(COLUMNS))
            nc.scalar.activation(decay[:], col["time_decay"][:], ACT.Exp).then_inc(ld["exp"], 1)

            def copy_xx(t):
                act.wait_ge(s["T1"], done(t))
                act.wait_ge(s["xs"], before(t))
                for kb in range(KD):
                    last = nc.scalar.activation(xx[:, kb, :], p_T[:, kb, :], ACT.Identity,
                                                bias=col["ln1_b"][:, kb:kb + 1], scale=col["ln1_g"][:, kb:kb + 1])
                last.then_inc(s["xx"], 1)

            def copy_yy(t):
                act.wait_ge(z["T2"], done(t))
                act.wait_ge(z["ys"], before(t))
                for kb in range(KD):
                    last = nc.scalar.activation(yy[:, kb, :], p_T[:, kb, :], ACT.Identity,
                                                bias=col["ln2_b"][:, kb:kb + 1], scale=col["ln2_g"][:, kb:kb + 1])
                last.then_inc(z["yy"], 1)

            def copy_kvr(t):
                act.wait_ge(s["kvr"], done(t))
                act.wait_ge(s["d34"], before(t))
                nc.scalar.activation(key[:], p_kvr[:, 0], ACT.Copy).then_inc(s["key"], 1)
                act.wait_ge(s["av"], before(t))
                act.wait_ge(s["e2v"], before(t))
                nc.scalar.activation(val[:], p_kvr[:, 1], ACT.Copy).then_inc(s["val"], 1)
                act.wait_ge(s["rw"], before(t))
                nc.scalar.activation(gate[:], p_kvr[:, 2], ACT.Tanh, scale=0.5).then_inc(s["gate"], 1)

            def exps(t):
                act.wait_ge(s["d12"], done(t))
                act.wait_ge(s["nr"], before(t))
                nc.scalar.activation(e12[:], d12[:], ACT.Exp).then_inc(s["e12"], 1)
                act.wait_ge(s["d34"], done(t))
                act.wait_ge(s["aa"], before(t))
                nc.scalar.activation(e34[:], d34[:], ACT.Exp).then_inc(s["e34"], 1)

            def gate_channel(t):
                act.wait_ge(z["rr"], done(t))
                act.wait_ge(z["g2"], before(t))
                nc.scalar.activation(gate2[:], p_o[:], ACT.Tanh, scale=0.5).then_inc(z["gate2"], 1)

            def squares(t):
                for half in range(2):
                    act.wait_ge(z[f"kkp{half}"], done(t))
                    if half:
                        act.wait_ge(z["kk0"], done(t))
                    else:
                        act.wait_ge(z["kk1"], before(t))
                    nc.scalar.activation(rl[:], p_kk[:], ACT.Relu).then_inc(z[f"rl{half}"], 1)
                    act.wait_ge(z[f"rl{half}"], done(t))
                    act.wait_ge(z["vvp"], before(t))
                    nc.scalar.activation(kk[:, 4 * half:4 * half + 4, :], rl[:], ACT.Square).then_inc(z[f"kk{half}"], 1)

            def round(t, last_t, next_t):
                copy_kvr(t)
                if last_t is not None:
                    copy_yy(last_t)
                exps(t)
                if last_t is not None:
                    gate_channel(last_t)
                    squares(last_t)
                if next_t is not None:
                    copy_xx(next_t)

            copy_xx(0)
            round(0, None, 1)
            with act.Fori(1, T - 1) as t:
                round(t, t - 1, t + 1)
            round(T - 1, T - 2, None)
            copy_yy(T - 1)
            gate_channel(T - 1)
            squares(T - 1)

        @block.tensor
        def _(pe):
            pe.wait_ge(ld["w"], 16 * 7)

            def transposes(out, x):
                for a in range(2):
                    for kb in range(KD):
                        last = nc.tensor.transpose(out[:, kb, a * P:(a + 1) * P], x[:, a, kb * P:(kb + 1) * P],
                                                   k["ident"][:])
                return last

            def turn_n1(t, last_t):
                pe.wait_ge(s["n1"], done(t))
                if last_t is not None:
                    pe.wait_ge(z["yy"], done(last_t))
                else:
                    pe.wait_ge(s["xx"], before(t))
                transposes(p_T, n1).then_inc(s["T1"], 1)

            def kvr(t):
                pe.wait_ge(s["mix"], done(t))
                pe.wait_ge(s["gate"], before(t))
                for m in range(3):
                    for o in range(KD):
                        for kb in range(KD):
                            last = nc.tensor.matmul(p_kvr[:, m, o, :], Wkvr[:, m, kb, o * P:(o + 1) * P],
                                                    mix[:, m, kb, :], start=kb == 0, stop=kb == KD - 1)
                last.then_inc(s["kvr"], 1)

            def out_product(t, last_t):
                pe.wait_ge(s["rw"], done(t))
                if last_t is not None:
                    pe.wait_ge(z["gate2"], done(last_t))
                for a in range(2):
                    for kb in range(KD):
                        last = nc.tensor.matmul(p_o[:, a, :], rw[:, kb, a * P:(a + 1) * P], Wo[:, kb, :],
                                                start=kb == 0, stop=kb == KD - 1)
                last.then_inc(s["op"], 1)

            def channel(t, xx_t, next_t):
                pe.wait_ge(z["n2"], done(t))
                pe.wait_ge(s["xx"], done(xx_t))
                transposes(p_T, n2).then_inc(z["T2"], 1)
                pe.wait_ge(z["cmix"], done(t))
                for a in range(2):
                    for kb in range(KD):
                        last = nc.tensor.matmul(p_o[:, a, :], cmix[:, 1, kb, a * P:(a + 1) * P], Wcr[:, kb, :],
                                                start=kb == 0, stop=kb == KD - 1)
                last.then_inc(z["rr"], 1)
                for half in range(2):
                    if half:
                        pe.wait_ge(z["rl0"], done(t))
                    else:
                        pe.wait_ge(z["rl1"], before(t))
                    for f in range(4):
                        for kb in range(KD):
                            fb = 4 * half + f
                            last = nc.tensor.matmul(p_kk[:, f, :], Wck[:, kb, fb * P:(fb + 1) * P],
                                                    cmix[:, 0, kb, :], start=kb == 0, stop=kb == KD - 1)
                    last.then_inc(z[f"kkp{half}"], 1)
                if next_t is not None:
                    turn_n1(next_t, t)
                pe.wait_ge(z["kk1"], done(t))
                pe.wait_ge(z["g2"], before(t))
                for a in range(2):
                    for fb in range(FB):
                        last = nc.tensor.matmul(p_vv[:, a, :], kk[:, fb, a * P:(a + 1) * P], Wcv[:, fb, :],
                                                start=fb == 0, stop=fb == FB - 1)
                last.then_inc(z["vvp"], 1)

            def round(t, last_t, next_t):
                kvr(t)
                if last_t is not None:
                    channel(last_t, t, next_t)
                else:
                    turn_n1(next_t, None)
                out_product(t, last_t)

            turn_n1(0, None)
            round(0, None, 1)
            with pe.Fori(1, T - 1) as t:
                round(t, t - 1, t + 1)
            round(T - 1, T - 2, None)
            channel(T - 1, T - 1, None)


def ssm_spectrum(nc, args, k, w, fourier, C, INNER):
    N, NA, NC = 64, 32, 8
    C1 = C - P
    G4, Q4 = 32, 4
    TWO_PI = 2.0 * np.pi
    PI_1 = 6.28125
    PI_2 = float(np.float32(np.round((TWO_PI - PI_1) * 2 ** 21) / 2 ** 21))
    PI_3 = float(TWO_PI - PI_1 - PI_2)
    F2 = 2 * D
    with ExitStack() as ctx:
        def sb(name, shape, dt=F32):
            return ctx.enter_context(nc.sbuf_tensor("K_" + name, shape, dt))

        def ps(name, shape):
            return ctx.enter_context(nc.psum_tensor("K_" + name, shape, F32))

        small = {n: sb(n, [P, P]) for n in ("ldt", "Are", "Aim", "Cre", "Cim", "dt", "ar", "ai", "turns", "r", "rc",
                                            "mag", "sin", "cos", "pm", "nre", "nim", "a2", "t1", "t2")}
        turns_i = sb("turns_i", [P, P], I32)
        pw = sb("pw", [P, 2, G4, Q4, NC + 1])
        gp = sb("gp", [P, 2, G4, Q4, NA])
        base = sb("base", [P, 2, G4, Q4])
        t4 = sb("t4", [P, 4, G4, Q4, NA // 2])
        Ks = sb("Ks", [P, NC, 2, G4])
        KT, skip = sb("KT", [P, 2, D]), sb("skip", [1, D])
        WvT, Wf = sb("WvT", [P, KD, C]), sb("Wf", [P, KD, 2 * F2])
        row = sb("row", [1, 2 * F2])
        kdram = nc.dram_tensor("ssm_kernel", (S, D), F32).ap()
        p_K = ps("pK", [P, 2, 2, 16, Q4, NC])
        p_f, p_v = ps("pf", [P, 4, D]), ps("pv", [P, 2, 512])
        c = semaphores(nc, ctx, "K", "load w act step kp ks stored again spec vf done")
        block = ctx.enter_context(nc.Block())

        @block.sync
        def _(sp):
            for half in range(2):
                rows = slice(N * half, N * half + N)
                cols = slice(P * half, P * half + P)
                for n in ("A_re", "A_im", "C_re", "C_im"):
                    sp.dma_start(small[n.replace("_", "")][rows, :], args["L1_xattn_" + n][:, cols]).then_inc(c["load"], 16)
                sp.dma_start(small["ldt"][rows, :], args["L1_xattn_log_dt"][cols].partition_broadcast(N)).then_inc(c["load"], 16)
            sp.dma_start(skip[:], args["L1_xattn_D_skip"].rearrange("(a d) -> a d", a=1)).then_inc(c["w"], 16)
            sp.dma_start(WvT[:], args["L1_xattn_Wv"].rearrange("(k p) c -> p k c", p=P)).then_inc(c["w"], 16)
            for j, n in enumerate(("film_in", "film_out")):
                sp.dma_start(Wf[:, :, j * F2:(j + 1) * F2],
                             args["L1_xattn_W_" + n].rearrange("(k p) f -> p k f", p=P)).then_inc(c["w"], 16)
                sp.dma_start(row[:, j * F2:(j + 1) * F2],
                             args["L1_xattn_b_" + n].rearrange("(a f) -> a f", a=1)).then_inc(c["w"], 16)
            sp.dma_start(w["gate"][:], args["L1_xattn_mod_gate"].partition_broadcast(P)).then_inc(c["w"], 16)
            sp.dma_start(fourier["fwd"][:], args["fourier"].rearrange("(k p) f -> p k f", p=P)).then_inc(c["w"], 16)
            sp.dma_start(w["sign"][:], args["L1_ffn_weights"].rearrange("(k p) o -> p k o", p=P)).then_inc(c["w"], 16)
            sp.wait_ge(c["ks"], 8)
            for q in range(Q4):
                sp.dma_start(kdram.rearrange("(a c) (h q g) -> q a c h g", c=NC, h=2, q=Q4)[q],
                             Ks[32 * q:32 * q + 32]).then_inc(c["stored"], 16)
            sp.wait_ge(c["stored"], 16 * Q4)
            sp.dma_start(KT[:], kdram.rearrange("(k p) d -> p k d", p=P)).then_inc(c["again"], 16)
            sp.wait_ge(c["done"], 1)
            sp.dma_start(w["VW"][77:78, :], row[:]).then_inc(c["stored"], 16)
            sp.wait_ge(c["stored"], 16 * (Q4 + 1))

        @block.vector
        def _(dve):
            steps = 0

            def step(instruction):
                nonlocal steps
                steps += 1
                instruction.then_inc(c["step"], 1)
                dve.wait_ge(c["step"], steps)

            v = nc.vector
            m = {n: t[:] for n, t in small.items()}
            dve.wait_ge(c["load"], 160)
            dve.wait_ge(c["act"], 1)
            step(v.tensor_tensor(m["ar"], m["dt"], m["Are"], ALU.mult))
            step(v.tensor_tensor(m["ai"], m["dt"], m["Aim"], ALU.mult))
            step(v.tensor_scalar(turns_i[:], m["ai"], 1.0 / TWO_PI, None, ALU.mult))
            step(v.tensor_copy(m["turns"], turns_i[:]))
            for part in (PI_1, PI_2, PI_3):
                step(v.scalar_tensor_tensor(out=m["ai"], in0=m["turns"], scalar=-part, in1=m["ai"],
                                            op0=ALU.mult, op1=ALU.add))
            step(v.tensor_scalar(m["r"], m["ai"], 3.1415925, -3.1415925, ALU.min, ALU.max))
            step(v.scalar_tensor_tensor(out=m["rc"], in0=m["r"], scalar=-1.0, in1=m["r"], op0=ALU.mult, op1=ALU.max))
            step(v.tensor_scalar(m["rc"], m["rc"], -1.0, float(np.pi / 2), ALU.mult, ALU.add))
            dve.wait_ge(c["act"], 2)
            dve.wait_ge(c["act"], 4)

            def gq(x):
                return x.rearrange("p (q g) -> p g q", g=G4)

            step(v.memset(pw[:, 0, :, :, 0], 1.0))
            step(v.memset(pw[:, 1, :, :, 0], 0.0))
            step(v.tensor_tensor(pw[:, 0, :, :, 1], gq(m["mag"]), gq(m["cos"]), ALU.mult))
            step(v.tensor_tensor(pw[:, 1, :, :, 1], gq(m["mag"]), gq(m["sin"]), ALU.mult))

            def product(out, x, y, count):
                yr = y[:, 0].unsqueeze(3).to_broadcast([P, G4, Q4, count])
                yi = y[:, 1].unsqueeze(3).to_broadcast([P, G4, Q4, count])
                v.tensor_tensor(t4[:, 0, :, :, 0:count], x[:, 0], yr, ALU.mult)
                v.tensor_tensor(t4[:, 1, :, :, 0:count], x[:, 1], yi, ALU.mult)
                v.tensor_tensor(t4[:, 2, :, :, 0:count], x[:, 0], yi, ALU.mult)
                step(v.tensor_tensor(t4[:, 3, :, :, 0:count], x[:, 1], yr, ALU.mult))
                v.tensor_tensor(out[:, 0], t4[:, 0, :, :, 0:count], t4[:, 1, :, :, 0:count], ALU.subtract)
                step(v.tensor_tensor(out[:, 1], t4[:, 2, :, :, 0:count], t4[:, 3, :, :, 0:count], ALU.add))

            for have in (1, 2, 4):
                product(pw[:, :, :, :, have + 1:2 * have + 1], pw[:, :, :, :, 1:have + 1], pw[:, :, :, :, have], have)
            step(v.tensor_scalar(gq(m["pm"]), pw[:, 0, :, :, 1], -1.0, None, ALU.add))
            step(v.tensor_copy(gq(m["r"]), pw[:, 1, :, :, 1]))

            def complex_product(re, im, a, b, cc, d, conj=1.0):
                step(v.tensor_tensor(m["t1"], m[a], m[cc], ALU.mult))
                step(v.tensor_tensor(m["t2"], m[b], m[d], ALU.mult))
                step(v.scalar_tensor_tensor(out=re, in0=m["t2"], scalar=-conj, in1=m["t1"], op0=ALU.mult, op1=ALU.add))
                step(v.tensor_tensor(m["t1"], m[a], m[d], ALU.mult))
                step(v.tensor_tensor(m["t2"], m[b], m[cc], ALU.mult))
                step(v.scalar_tensor_tensor(out=im, in0=m["t1"], scalar=conj, in1=m["t2"], op0=ALU.mult, op1=ALU.add))

            complex_product(m["nre"], m["nim"], "Cre", "Cim", "pm", "r")
            complex_product(m["mag"], m["cos"], "nre", "nim", "Are", "Aim", conj=-1.0)
            step(v.tensor_tensor(m["t1"], m["Are"], m["Are"], ALU.mult))
            step(v.tensor_tensor(m["t2"], m["Aim"], m["Aim"], ALU.mult))
            step(v.tensor_tensor(m["a2"], m["t1"], m["t2"], ALU.add))
            step(v.reciprocal(m["a2"], m["a2"]))
            for part, n in enumerate(("mag", "cos")):
                step(v.scalar_tensor_tensor(out=gp[:, part, :, :, 0], in0=gq(m[n]), scalar=2.0, in1=gq(m["a2"]),
                                            op0=ALU.mult, op1=ALU.mult))
            step(v.tensor_copy(base[:], pw[:, :, :, :, NC]))
            have = 1
            while have < NA:
                product(gp[:, :, :, :, have:2 * have], gp[:, :, :, :, 0:have], base, have)
                have *= 2
                if have < NA:
                    product(t4[:, 0:2, :, :, 15:16], base[:].unsqueeze(4), base, 1)
                    step(v.tensor_copy(base[:].unsqueeze(4), t4[:, 0:2, :, :, 15:16]))
            v.tensor_scalar(pw[:, 1], pw[:, 1], -1.0, None, ALU.mult).then_inc(c["vf"], 1)
            dve.wait_ge(c["w"], 16 * 9)
            step(v.tensor_scalar(w["sign"][:], w["sign"][:], 0.0, 2.0, ALU.is_ge, ALU.mult))
            step(v.tensor_scalar(w["sign"][:], w["sign"][:], -1.0, None, ALU.add))
            step(v.tensor_scalar(row[:], row[:], w["gate"][0:1, 0:1], None, ALU.mult))
            for j in range(2):
                last = v.tensor_scalar(row[:, j * F2:j * F2 + D], row[:, j * F2:j * F2 + D], 1.0, None, ALU.add)
            last.then_inc(c["done"], 1)
            dve.wait_ge(c["kp"], 1)
            for q in range(Q4):
                for half in range(2):
                    v.tensor_copy(
                        Ks[32 * q:32 * q + 32, :, half, :].rearrange("a c (b g) -> a b g c", b=2),
                        p_K[32 * q:32 * q + 32, half, :, :, q, :]).then_inc(c["ks"], 1)
            dve.wait_ge(c["again"], 16)
            v.tensor_tensor(KT[0:1, 0, :], KT[0:1, 0, :], skip[:], ALU.add).then_inc(c["done"], 1)
            dve.wait_ge(c["spec"], 1)
            step(v.tensor_copy(fourier["spec"][:], p_f[:]))

        @block.scalar
        def _(act):
            act.wait_ge(c["load"], 160)
            nc.scalar.activation(small["dt"][:], small["ldt"][:], ACT.Exp).then_inc(c["act"], 1)
            act.wait_ge(c["step"], 1)
            nc.scalar.activation(small["mag"][:], small["ar"][:], ACT.Exp).then_inc(c["act"], 1)
            act.wait_ge(c["step"], 10)
            nc.scalar.activation(small["sin"][:], small["r"][:], ACT.Sin).then_inc(c["act"], 1)
            nc.scalar.activation(small["cos"][:], small["rc"][:], ACT.Sin).then_inc(c["act"], 1)
            act.wait_ge(c["vf"], 3)
            act.wait_ge(c["w"], 16 * 9)
            for kb in range(2):
                rows = P if kb == 0 else C1
                last = nc.scalar.activation(w["Wvf"][0:rows, kb, :].rearrange("p (a f) -> p a f", a=2),
                                            (p_v if kb == 0 else p_f[:].rearrange("p (a b) d -> p a (b d)", a=2))[0:rows],
                                            ACT.Copy, scale=w["gate"][0:rows, 0:1])
            last.then_inc(c["act"], 1)

        @block.tensor
        def _(pe):
            pe.wait_ge(c["w"], 16 * 9)
            for kb in range(2):
                rows = P if kb == 0 else C1
                out = p_v if kb == 0 else p_f[:].rearrange("p (a b) d -> p a (b d)", a=2)
                for f in range(2):
                    for db in range(KD):
                        last = nc.tensor.matmul(out[0:rows, f, :], WvT[:, db, kb * P:kb * P + rows],
                                                Wf[:, db, f * 512:(f + 1) * 512], start=db == 0, stop=db == KD - 1)
                last.then_inc(c["vf"], 1)
            pe.wait_ge(c["vf"], 3)
            for half in range(2):
                rows = slice(N * half, N * half + N)
                for g in range(G4):
                    for part in range(2):
                        last = nc.tensor.matmul(p_K[:, half, g // 16, g % 16].rearrange("p q c -> p (q c)"),
                                                gp[rows, part, g].rearrange("p q a -> p (q a)"),
                                                pw[rows, part, g, :, 0:NC], start=part == 0, stop=part == 1)
            last.then_inc(c["kp"], 1)
            pe.wait_ge(c["done"], 2)
            pe.wait_ge(c["act"], 5)
            for f in range(4):
                for kb in range(2):
                    last = nc.tensor.matmul(p_f[:, f, :], fourier["fwd"][:, kb, f * P:(f + 1) * P], KT[:, kb, :],
                                            start=kb == 0, stop=kb == 1)
            last.then_inc(c["spec"], 1)


def state_space(nc, args, X, k, out):
    J, C, H, DH, TOP = 77, 192, 4, 32, 32
    C1 = C - P
    FF = 4 * D
    FB = FF // P
    TAKEN = float(np.float32(-3e38))
    with ExitStack() as ctx:
        def sb(name, shape, dt=F32):
            return ctx.enter_context(nc.sbuf_tensor("E_" + name, shape, dt))

        w = {"gate": sb("gate", [P, 1]), "sign": sb("sign", [P, KD, D]), "Wvf": sb("Wvf", [P, 2, 4 * D]),
             "VW": sb("VW", [J + 1, 4 * D])}
        fourier = {"fwd": sb("fwd", [P, 2, 2 * S]), "spec": sb("spec", [P, 4, D])}
        ssm_spectrum(nc, args, k, w, fourier, C, H * DH)

        def ps(name, shape):
            return ctx.enter_context(nc.psum_tensor("E_" + name, shape, F32))

        inv = sb("inv", [P, 4, S])
        Wq, Wk = sb("Wq", [P, KD, P]), sb("Wk", [P, 2, P])
        W1, W2 = sb("W1", [P, KD, FF]), sb("W2", [P, FB, D])
        ROWS = ("L1_xattn_g_norm_in", "L1_xattn_b_norm_in", "L1_xattn_g_norm_out", "L1_xattn_b_norm_out",
                "L1_xattn_b2", "L1_ffn_scale", "L1_ffn_bias")
        rowb = {n: sb(n, [P, D]) for n in ROWS}
        gf, bf, b1 = sb("gf", [P, KD]), sb("bf", [P, KD]), sb("b1", [P, FB])
        vmask, vbias = sb("vmask", [P, B * J], U8), sb("vbias", [P, B, J])
        tmask, tm = sb("tmask", [P, NT], U8), sb("tm", [P, NT])
        cx, cxT = sb("cx", [J, C]), sb("cxT", [P, 2, J])
        st, mv, var, rstd = sb("st", [P, 2, 6]), sb("mv", [P, 2, 2]), sb("var", [P, 2]), sb("rstd", [P, 2])
        v2, rstd2 = sb("v2", [P, 2]), sb("rstd2", [P, 2])
        h, n1, nb, u, hk = (sb(n, [P, 2, D]) for n in ("h", "n1", "nb", "u", "hk"))
        hT, qT, kTz = sb("hT", [P, KD, S]), sb("qT", [P, S]), sb("kTz", [P, H, J])
        sc, wk, ex = sb("sc", [P, 2, H, J]), sb("wk", [P, 2, H, J]), sb("ex", [P, 2, H, J])
        m8 = sb("m8", [P, 4, 2, H, 8])
        nmx, sm, rs = sb("nmx", [P, 2, H]), sb("sm", [P, 2, H]), sb("rs", [P, 2, H])
        am, amT = sb("am", [P, 2, J]), sb("amT", [J + 1, S])
        fo = sb("fo", [P, 2, 2 * D])
        tA, tB, Y = sb("tA", [P, 4, D]), sb("tB", [P, 4, D]), sb("Y", [P, 4, D])
        y2, xt, n3 = (sb(n, [P, 2, D]) for n in ("y2", "xt", "n3"))
        n3T, gT = sb("n3T", [P, KD, S]), sb("gT", [P, FB, S])
        xf, n4, h6, z, ob = (sb(n, [P, 2, D]) for n in ("xf", "n4", "h6", "z", "ob"))
        h6T = sb("h6T", [P, KD, S])
        norms = {n: (sb("st" + n, [P, 2, 6]), sb("mv" + n, [P, 2, 2]), sb("var" + n, [P, 2]), sb("rstd" + n, [P, 2]))
                 for n in ("3", "4", "6")}
        p_A, p_B = ps("pA", [P, 2, 256]), ps("pB", [P, 512])
        p_S = ps("pS", [P, 2, 512])
        p_U, p_Y, p_T = ps("pU", [P, 4, 256]), ps("pY", [P, 2, 256]), ps("pT", [P, 2, 256])
        s = semaphores(nc, ctx, "E", NORM + " settled h v2a v2b v2 rstd2 n1 nbg nb cxp cxT hTp hT kqp kT qT vwp vw scp "
                       "sc m80 m81 m82 m83 r0 r1 r2 r3 nmx ex sel sm rs rt pn am amp amT fp0 fp1 u0 u1 ui0 ui1 fo0 fo1 hk")
        z2 = semaphores(nc, ctx, "Ez", "settled Up tAB Yr Yi yp y2 ysh xt n3 T3 n3T gp0 gp1 g0 g1 ffp xfp xf n4 n4g "
                        "n4b x h6 T6 h6T zp zs zb zc ob")
        nrm = {n: semaphores(nc, ctx, "E" + n, NORM + " settled") for n in ("3", "4", "6")}
        ld = semaphores(nc, ctx, "Eld", "w masks init cxl out")
        block = ctx.enter_context(nc.Block())

        @block.sync
        def _(sp):
            for group in (s, z2, *nrm.values()):
                give_credit(sp, group)
            sp.sem_inc(ld["out"], 16)
            for n in ROWS:
                sp.dma_start(rowb[n][:], args[n].partition_broadcast(P)).then_inc(ld["w"], 16)
            sp.dma_start(inv[:], args["fourier_inverse"].rearrange("(k p) l -> p k l", p=P)).then_inc(ld["w"], 16)
            sp.dma_start(Wq[:], args["L1_xattn_Wq"].rearrange("(k p) n -> p k n", p=P)).then_inc(ld["w"], 16)
            sp.dma_start(Wk[:, 0, :], args["L1_xattn_Wk"][0:P]).then_inc(ld["w"], 16)
            sp.dma_start(Wk[0:C1, 1, :], args["L1_xattn_Wk"][P:C]).then_inc(ld["w"], 16)
            sp.dma_start(W1[:], args["L1_xattn_W1"].rearrange("(k p) n -> p k n", p=P)).then_inc(ld["w"], 16)
            sp.dma_start(W2[:], args["L1_xattn_W2"].rearrange("(k p) n -> p k n", p=P)).then_inc(ld["w"], 16)
            with nc.allow_non_contiguous_dma(reason="columns of a value a channel"):
                sp.dma_start(gf[:], args["L1_xattn_g_ffn"].rearrange("(k p) -> p k", p=P)).then_inc(ld["w"], 16)
                sp.dma_start(bf[:], args["L1_xattn_b_ffn"].rearrange("(k p) -> p k", p=P)).then_inc(ld["w"], 16)
                sp.dma_start(b1[:], args["L1_xattn_b1"].rearrange("(k p) -> p k", p=P)).then_inc(ld["w"], 16)
                sp.dma_start(tmask[:], args["mask_BxS_bf1"].rearrange("b (s p) -> p (b s)", p=P)).then_inc(ld["masks"], 16)
            sp.dma_start(vmask[:], args["mask_BxS2_bf1"].rearrange("b j -> (b j)").partition_broadcast(P)).then_inc(ld["masks"], 16)

            def context(i):
                sp.wait_ge(s["cxp"], before(i))
                src = args["ctx_768"][i] if isinstance(i, int) else args["ctx_768"][bass.ds(i, 1)].rearrange("a j c -> (a j) c")
                sp.dma_start(cx[:], src).then_inc(ld["cxl"], 16)

            def store(i):
                sp.wait_ge(z2["ob"], done(i))
                dst = out[i] if isinstance(i, int) else out[bass.ds(i, 1)].rearrange("a s d -> (a s) d")
                sp.dma_start(dst.rearrange("(s p) d -> p s d", p=P), ob[:]).then_inc(ld["out"], 16)

            context(0)
            context(1)
            with sp.Fori(0, B - 2) as p:
                context(p + 2)
                store(p)
            store(B - 2)
            store(B - 1)
            sp.wait_ge(ld["out"], 16 * (B + 1))

        @block.gpsimd
        def _(pool):
            g = nc.gpsimd
            g.memset(kTz[:], 0.0).then_inc(ld["init"], 1)
            pool.wait_ge(ld["init"], 1)
            g.memset(amT[64:J + 1, :], 1.0).then_inc(ld["init"], 1)
            pool.wait_ge(ld["init"], 2)
            pool.wait_ge(ld["w"], 16 * 16)

            def both(row):
                return rowb[row][:].unsqueeze(1).to_broadcast([P, 2, D])

            def first_rstd(j):
                norm_rstd(nc, pool, s, mv, var, rstd, k, j)
                pool.wait_ge(s["rstd"], done(j))
                g.tensor_tensor(v2[:], mv[:, :, 1], rstd[:], ALU.mult).then_inc(s["v2a"], 1)
                pool.wait_ge(s["v2a"], done(j))
                g.tensor_tensor(v2[:], v2[:], rstd[:], ALU.mult).then_inc(s["v2b"], 1)
                pool.wait_ge(s["v2b"], done(j))
                settle(pool, s)
                g.tensor_scalar(v2[:], v2[:], EPS, None, ALU.add).then_inc(s["v2"], 1)
                pool.wait_ge(s["v2"], done(j))
                pool.wait_ge(s["n1"], before(j))
                g.tensor_tensor(rstd2[:], v2[:], k["minus_half"][:], ALU.pow).then_inc(s["rstd2"], 1)

            def first_affine(j):
                pool.wait_ge(s["n1"], done(j))
                pool.wait_ge(s["u1"], before(j))
                g.tensor_tensor(nb[:], n1[:], both("L1_xattn_g_norm_in"), ALU.mult).then_inc(s["nbg"], 1)
                pool.wait_ge(s["nbg"], done(j))
                g.tensor_tensor(nb[:], nb[:], both("L1_xattn_b_norm_in"), ALU.add).then_inc(s["nb"], 1)

            def spectrum(i):
                pool.wait_ge(z2["tAB"], done(i))
                pool.wait_ge(z2["yp"], before(i))
                g.tensor_tensor(Y[:, 0:2], tA[:, 0:2], tB[:, 2:4], ALU.subtract).then_inc(z2["Yr"], 1)
                g.tensor_tensor(Y[:, 2:4], tA[:, 2:4], tB[:, 0:2], ALU.add).then_inc(z2["Yi"], 1)

            def shift_out(i):
                pool.wait_ge(z2["y2"], done(i))
                g.tensor_tensor(y2[:], y2[:], fo[:, :, D:2 * D], ALU.add).then_inc(z2["ysh"], 1)
                pool.wait_ge(z2["ysh"], done(i))
                pool.wait_ge(z2["xfp"], before(i))
                pool.wait_ge(s["hk"], done(i))
                g.tensor_tensor(xt[:], y2[:], hk[:], ALU.add).then_inc(z2["xt"], 1)

            def add_b2(p):
                pool.wait_ge(z2["xfp"], done(p))
                g.tensor_tensor(xf[:], xf[:], both("L1_xattn_b2"), ALU.add).then_inc(z2["xf"], 1)

            def residual(p):
                pool.wait_ge(z2["n4"], done(p))
                g.tensor_tensor(n4[:], n4[:], both("L1_xattn_g_norm_out"), ALU.mult).then_inc(z2["n4g"], 1)
                pool.wait_ge(z2["n4g"], done(p))
                g.tensor_tensor(n4[:], n4[:], both("L1_xattn_b_norm_out"), ALU.add).then_inc(z2["n4b"], 1)
                pool.wait_ge(z2["n4b"], done(p))
                settle(pool, z2)
                x2 = X[:, 2 * p:2 * p + 2, :] if isinstance(p, int) else X[:, bass.ds(2 * p, 2), :]
                g.tensor_tensor(x2, x2, n4[:], ALU.add).then_inc(z2["x"], 1)

            def add_bias(p):
                pool.wait_ge(z2["zs"], done(p))
                g.tensor_tensor(z[:], z[:], both("L1_ffn_bias"), ALU.add).then_inc(z2["zb"], 1)

            def round(j, i, p):
                if j is not None:
                    first_rstd(j)
                if p is not None:
                    add_b2(p)
                if i is not None:
                    spectrum(i)
                if p is not None:
                    norm_rstd(nc, pool, nrm["4"], *norms["4"][1:], k, p)
                    residual(p)
                if i is not None:
                    shift_out(i)
                if p is not None:
                    norm_rstd(nc, pool, nrm["6"], *norms["6"][1:], k, p)
                if i is not None:
                    norm_rstd(nc, pool, nrm["3"], *norms["3"][1:], k, i)
                if j is not None:
                    first_affine(j)
                if p is not None:
                    add_bias(p)

            round(0, None, None)
            round(1, 0, None)
            with pool.Fori(0, B - 2) as p:
                round(p + 2, p + 1, p)
            round(None, B - 1, B - 2)
            round(None, None, B - 1)

        @block.vector
        def _(dve):
            v = nc.vector
            dve.wait_ge(ld["masks"], 32)
            dve.wait_ge(ld["w"], 16 * 16)
            v.tensor_scalar(vbias[:].rearrange("p b j -> p (b j)"), vmask[:], 1.0, 1e30, ALU.subtract,
                            ALU.mult).then_inc(ld["masks"], 1)
            v.tensor_scalar(tm[:], tmask[:], 1.0 / H, None, ALU.mult).then_inc(ld["masks"], 1)
            dve.wait_ge(ld["masks"], 34)

            def apply(sems, stats, product, x, y, i, read_by):
                dve.wait_ge(sems["rstd"], done(i))
                for sem, value in read_by:
                    dve.wait_ge(sem, value)
                for a in range(2):
                    ins = v.tensor_scalar(y[:, a, :], x[a], stats[1][:, a, 0:1], stats[3][:, a:a + 1],
                                          ALU.subtract, ALU.mult)
                ins.then_inc(product, 1)

            def x_of(b):
                return [X[:, 2 * b, :], X[:, 2 * b + 1, :]]

            def first_stats(j):
                norm_stats(nc, dve, s, x_of(j), st, mv, j)

            def first_apply(j):
                apply(s, (st, mv, var, rstd), s["h"], x_of(j), h, j, [(s["hTp"], before(j)), (s["hk"], before(j))])
                dve.wait_ge(s["h"], done(j))
                dve.wait_ge(s["rstd2"], done(j))
                dve.wait_ge(s["nbg"], before(j))
                for a in range(2):
                    ins = v.tensor_scalar(n1[:, a, :], h[:, a, :], rstd2[:, a:a + 1], None, ALU.mult)
                ins.then_inc(s["n1"], 1)

            def scores(j):
                dve.wait_ge(s["scp"], done(j))
                dve.wait_ge(s["ex"], before(j))
                bias = vbias[:, bass.ds(j, 1), :].to_broadcast([P, H, J])
                for t in range(2):
                    ins = v.scalar_tensor_tensor(out=sc[:, t], in0=p_S[:, t, 0:H * J].rearrange("p (h j) -> p h j", h=H),
                                                 scalar=float(DH) ** -0.5, in1=bias, op0=ALU.mult, op1=ALU.add)
                ins.then_inc(s["sc"], 1)
                dve.wait_ge(s["sc"], done(j))

            def take(j, turn):
                src = sc if turn == 0 else wk
                if turn:
                    dve.wait_ge(s[f"r{turn - 1}"], done(j))
                settle(dve, s)
                for t in range(2):
                    for hd in range(H):
                        ins = v.max(m8[:, turn, t, hd, :], src[:, t, hd, :])
                ins.then_inc(s[f"m8{turn}"], 1)
                dve.wait_ge(s[f"m8{turn}"], done(j))
                settle(dve, s)
                for t in range(2):
                    for hd in range(H):
                        ins = v.match_replace(wk[:, t, hd, :], m8[:, turn, t, hd, :], src[:, t, hd, :], TAKEN)
                ins.then_inc(s[f"r{turn}"], 1)
                if turn == 0:
                    dve.wait_ge(s["ex"], before(j))
                    v.tensor_scalar(nmx[:], m8[:, 0, :, :, 0], -1.0, None, ALU.mult).then_inc(s["nmx"], 1)

            def average(j):
                dve.wait_ge(s["r3"], done(j))
                dve.wait_ge(s["ex"], done(j))
                v.scalar_tensor_tensor(out=ex[:], in0=wk[:], scalar=TAKEN, in1=ex[:], op0=ALU.is_equal,
                                       op1=ALU.mult).then_inc(s["sel"], 1)
                dve.wait_ge(s["sel"], done(j))
                v.tensor_reduce(sm[:], ex[:], AX.X, ALU.add).then_inc(s["sm"], 1)
                dve.wait_ge(s["sm"], done(j))
                v.reciprocal(rs[:], sm[:]).then_inc(s["rs"], 1)
                dve.wait_ge(s["rs"], done(j))
                v.tensor_tensor(rs[:], rs[:], tm[:, bass.ds(2 * j, 2)].unsqueeze(2).to_broadcast([P, 2, H]),
                                ALU.mult).then_inc(s["rt"], 1)
                dve.wait_ge(s["rt"], done(j))
                v.tensor_tensor(ex[:], ex[:], rs[:].unsqueeze(3).to_broadcast([P, 2, H, J]), ALU.mult).then_inc(s["pn"], 1)
                dve.wait_ge(s["pn"], done(j))
                dve.wait_ge(s["amp"], before(j))
                v.tensor_reduce(am[:], ex[:].rearrange("p t h j -> p t j h"), AX.X, ALU.add).then_inc(s["am"], 1)

            def film(j):
                dve.wait_ge(s["nb"], done(j))
                for t in range(2):
                    dve.wait_ge(s[f"fp{t}"], done(j))
                    if t == 0:
                        dve.wait_ge(z2["Up"], before(j))
                    v.tensor_tensor(u[:, t, :], nb[:, t, :], p_S[:, 0, 0:D], ALU.mult).then_inc(s[f"ui{t}"], 1)
                    dve.wait_ge(s[f"ui{t}"], done(j))
                    v.tensor_tensor(u[:, t, :], u[:, t, :], p_S[:, 0, D:2 * D], ALU.add).then_inc(s[f"u{t}"], 1)
                dve.wait_ge(z2["xt"], before(j))
                v.tensor_copy(hk[:], h[:]).then_inc(s["hk"], 1)

            def spectrum(i):
                dve.wait_ge(z2["Up"], done(i))
                dve.wait_ge(z2["Yi"], before(i))
                for part, dst in ((0, tA), (1, tB)):
                    kf = fourier["spec"][:, 2 * part:2 * part + 2, :].rearrange("p b d -> p (b d)")
                    ins = v.tensor_tensor(dst[:].rearrange("p (a b) d -> p a (b d)", a=2),
                                          p_U[:].rearrange("p (a b) d -> p a (b d)", a=2),
                                          kf.unsqueeze(1).to_broadcast([P, 2, 2 * D]), ALU.mult)
                ins.then_inc(z2["tAB"], 1)

            def scale_out(i):
                dve.wait_ge(z2["yp"], done(i))
                dve.wait_ge(s["fo1"], done(i))
                dve.wait_ge(z2["xt"], before(i))
                v.tensor_tensor(y2[:], p_Y[:], fo[:, :, 0:D], ALU.mult).then_inc(z2["y2"], 1)

            def stats_3(i):
                dve.wait_ge(z2["xt"], done(i))
                norm_stats(nc, dve, nrm["3"], [xt[:, 0, :], xt[:, 1, :]], *norms["3"][0:2], i)

            def apply_3(i):
                apply(nrm["3"], norms["3"], z2["n3"], [xt[:, 0, :], xt[:, 1, :]], n3, i, [(z2["T3"], before(i))])

            def add_network(p):
                dve.wait_ge(z2["ffp"], done(p))
                dve.wait_ge(z2["n4"], before(p))
                v.tensor_tensor(xf[:], p_Y[:], xt[:], ALU.add).then_inc(z2["xfp"], 1)

            def stats_4(p):
                dve.wait_ge(z2["xf"], done(p))
                norm_stats(nc, dve, nrm["4"], [xf[:, 0, :], xf[:, 1, :]], *norms["4"][0:2], p)

            def apply_4(p):
                apply(nrm["4"], norms["4"], z2["n4"], [xf[:, 0, :], xf[:, 1, :]], n4, p, [(z2["x"], before(p))])

            def stats_6(p):
                dve.wait_ge(z2["x"], done(p))
                norm_stats(nc, dve, nrm["6"], x_of(p), *norms["6"][0:2], p)

            def apply_6(p):
                apply(nrm["6"], norms["6"], z2["h6"], x_of(p), h6, p, [(z2["T6"], before(p))])

            def scale_projection(p):
                dve.wait_ge(z2["zp"], done(p))
                dve.wait_ge(z2["ob"], before(p))
                v.tensor_tensor(z[:], p_B[:].rearrange("p (a d) -> p a d", a=2),
                                rowb["L1_ffn_scale"][:].unsqueeze(1).to_broadcast([P, 2, D]),
                                ALU.mult).then_inc(z2["zs"], 1)

            def clip(p):
                dve.wait_ge(z2["zb"], done(p))
                v.tensor_scalar(z[:], z[:], 100.0, -100.0, ALU.min, ALU.max).then_inc(z2["zc"], 1)
                dve.wait_ge(z2["zc"], done(p))
                dve.wait_ge(ld["out"], 16 * p + 16)
                x2 = X[:, 2 * p:2 * p + 2, :] if isinstance(p, int) else X[:, bass.ds(2 * p, 2), :]
                v.tensor_tensor(ob[:], x2, z[:], ALU.add).then_inc(z2["ob"], 1)

            def round(j, i, p):
                steps = ((first_stats, j), (first_apply, j), (add_network, p), (spectrum, i), (stats_4, p),
                         (apply_4, p), (scale_out, i), (stats_6, p), (scores, j), (stats_3, i), (apply_6, p),
                         (apply_3, i), (take_0, j), (take_1, j), (take_2, j), (take_3, j), (average, j),
                         (scale_projection, p), (film, j), (clip, p))
                for step, batch in steps:
                    if batch is not None:
                        step(batch)

            def take_0(j):
                take(j, 0)

            def take_1(j):
                take(j, 1)

            def take_2(j):
                take(j, 2)

            def take_3(j):
                take(j, 3)

            round(0, None, None)
            round(1, 0, None)
            with dve.Fori(0, B - 2) as p:
                round(p + 2, p + 1, p)
            round(None, B - 1, B - 2)
            round(None, None, B - 1)

        @block.scalar
        def _(act):
            a_ = nc.scalar
            act.wait_ge(ld["w"], 16 * 16)
            act.wait_ge(ld["init"], 2)

            def first_a(j):
                act.wait_ge(s["cxp"], done(j))
                act.wait_ge(s["vwp"], before(j))
                a_.activation(cxT[:, 0, :], p_A[:, 0, 0:J], ACT.Copy)
                a_.activation(cxT[0:C1, 1, :], p_A[0:C1, 1, 0:J], ACT.Copy).then_inc(s["cxT"], 1)
                act.wait_ge(s["hTp"], done(j))
                act.wait_ge(s["kqp"], before(j))
                a_.activation(hT[:], p_A[:], ACT.Copy).then_inc(s["hT"], 1)
                act.wait_ge(s["kqp"], done(j))
                act.wait_ge(s["scp"], before(j))
                for hd in range(H):
                    ins = a_.activation(kTz[DH * hd:DH * hd + DH, hd, :], p_B[DH * hd:DH * hd + DH, 256:256 + J], ACT.Copy)
                ins.then_inc(s["kT"], 1)
                a_.activation(qT[:], p_B[:, 0:256], ACT.Copy).then_inc(s["qT"], 1)
                act.wait_ge(s["vwp"], done(j))
                act.wait_ge(s["fp1"], before(j))
                a_.activation(w["VW"][0:J, :].rearrange("j (a f) -> j a f", a=2), p_S[0:J], ACT.Copy).then_inc(s["vw"], 1)

            def exps(j):
                act.wait_ge(s["nmx"], done(j))
                act.wait_ge(s["am"], before(j))
                for t in range(2):
                    for hd in range(H):
                        ins = a_.activation(ex[:, t, hd, :], sc[:, t, hd, :], ACT.Exp, bias=nmx[:, t, hd:hd + 1])
                ins.then_inc(s["ex"], 1)

            def film(j):
                act.wait_ge(s["amp"], done(j))
                act.wait_ge(s["fp1"], before(j))
                a_.activation(amT[0:J, :], p_A[0:J].rearrange("j a q -> j (a q)")[:, 0:S], ACT.Copy).then_inc(s["amT"], 1)
                for t in range(2):
                    act.wait_ge(s[f"fp{t}"], done(j))
                    if t == 0:
                        act.wait_ge(z2["ysh"], before(j))
                    a_.activation(fo[:, t, :], p_S[:, 1, :], ACT.Copy).then_inc(s[f"fo{t}"], 1)

            def turned(i):
                act.wait_ge(z2["T3"], done(i))
                act.wait_ge(z2["gp1"], before(i))
                for kb in range(KD):
                    ins = a_.activation(n3T[:, kb, :], p_T[:, kb, :], ACT.Identity, bias=bf[:, kb:kb + 1],
                                        scale=gf[:, kb:kb + 1])
                ins.then_inc(z2["n3T"], 1)

            def gelu(i, half):
                act.wait_ge(z2[f"gp{half}"], done(i))
                if half == 0:
                    act.wait_ge(z2["ffp"], before(i))
                for f in range(4):
                    fb = 4 * half + f
                    ins = a_.activation(gT[:, fb, :], p_U[:, f, :], ACT.Gelu, bias=b1[:, fb:fb + 1])
                ins.then_inc(z2[f"g{half}"], 1)

            def last(p):
                act.wait_ge(z2["T6"], done(p))
                act.wait_ge(z2["zp"], before(p))
                a_.activation(h6T[:], p_T[:], ACT.Copy).then_inc(z2["h6T"], 1)

            def round(j, i, p):
                if j is not None:
                    first_a(j)
                if i is not None:
                    turned(i)
                if j is not None:
                    exps(j)
                if i is not None:
                    gelu(i, 0)
                if p is not None:
                    last(p)
                if i is not None:
                    gelu(i, 1)
                if j is not None:
                    film(j)

            round(0, None, None)
            round(1, 0, None)
            with act.Fori(0, B - 2) as p:
                round(p + 2, p + 1, p)
            round(None, B - 1, B - 2)
            round(None, None, B - 1)

        @block.tensor
        def _(pe):
            pe.wait_ge(ld["w"], 16 * 16)
            pe.wait_ge(ld["init"], 2)

            def transposes(out, x):
                for a in range(2):
                    for kb in range(KD):
                        ins = nc.tensor.transpose(out[:, kb, a * P:(a + 1) * P], x[:, a, kb * P:(kb + 1) * P],
                                                  k["ident"][:])
                return ins

            def first_a(j, p):
                pe.wait_ge(ld["cxl"], 16 * j + 16)
                pe.wait_ge(s["amT"], before(j))
                nc.tensor.transpose(p_A[:, 0, 0:J], cx[:, 0:P], k["ident"][0:J, 0:J])
                nc.tensor.transpose(p_A[0:C1, 1, 0:J], cx[:, P:C], k["ident"][0:J, 0:J]).then_inc(s["cxp"], 1)
                pe.wait_ge(s["h"], done(j))
                pe.wait_ge(s["cxT"], done(j))
                transposes(p_A, h).then_inc(s["hTp"], 1)
                pe.wait_ge(s["u1"], before(j))
                pe.wait_ge(s["fo1"], before(j))
                for f in range(2):
                    for kb in range(2):
                        rows = P if kb == 0 else C1
                        ins = nc.tensor.matmul(p_S[0:J, f, :], cxT[0:rows, kb, :], w["Wvf"][0:rows, kb, f * 512:(f + 1) * 512],
                                               start=kb == 0, stop=kb == 1)
                ins.then_inc(s["vwp"], 1)
                pe.wait_ge(s["hT"], done(j))
                if p is not None:
                    pe.wait_ge(z2["zs"], before(p))
                for kb in range(KD):
                    nc.tensor.matmul(p_B[:, 0:S], Wq[:, kb, :], hT[:, kb, :], start=kb == 0, stop=kb == KD - 1)
                for kb in range(2):
                    rows = P if kb == 0 else C1
                    ins = nc.tensor.matmul(p_B[:, S:S + J], Wk[0:rows, kb, :], cxT[0:rows, kb, :], start=kb == 0, stop=kb == 1)
                ins.then_inc(s["kqp"], 1)

            def scores(j):
                pe.wait_ge(s["kT"], done(j))
                pe.wait_ge(s["qT"], done(j))
                pe.wait_ge(s["vw"], done(j))
                for t in range(2):
                    ins = nc.tensor.matmul(p_S[:, t, 0:H * J], qT[:, t * P:(t + 1) * P], kTz[:].rearrange("p h j -> p (h j)"),
                                           start=True, stop=True)
                ins.then_inc(s["scp"], 1)

            def film(j):
                pe.wait_ge(s["am"], done(j))
                pe.wait_ge(s["hT"], done(j))
                for t in range(2):
                    ins = nc.tensor.transpose(p_A[0:J].rearrange("j a q -> j (a q)")[:, t * P:(t + 1) * P], am[:, t, :],
                                              k["ident"][:])
                ins.then_inc(s["amp"], 1)
                pe.wait_ge(s["amT"], done(j))
                pe.wait_ge(s["sc"], done(j))
                for t in range(2):
                    if t:
                        pe.wait_ge(s["u0"], done(j))
                        pe.wait_ge(s["fo0"], done(j))
                    for f in range(2):
                        ins = nc.tensor.matmul(p_S[:, f, :], amT[:, t * P:(t + 1) * P], w["VW"][:, f * 512:(f + 1) * 512],
                                               start=True, stop=True)
                    ins.then_inc(s[f"fp{t}"], 1)

            def forward(i):
                pe.wait_ge(s["u1"], done(i))
                pe.wait_ge(z2["g1"], before(i))
                for f in range(4):
                    for a in range(2):
                        ins = nc.tensor.matmul(p_U[:, f, :], fourier["fwd"][:, a, f * P:(f + 1) * P], u[:, a, :],
                                               start=a == 0, stop=a == 1)
                ins.then_inc(z2["Up"], 1)

            def inverse(i):
                pe.wait_ge(z2["Yr"], done(i))
                pe.wait_ge(z2["Yi"], done(i))
                pe.wait_ge(z2["xfp"], before(i))
                for a in range(2):
                    for f in range(4):
                        ins = nc.tensor.matmul(p_Y[:, a, :], inv[:, f, a * P:(a + 1) * P], Y[:, f, :],
                                               start=f == 0, stop=f == 3)
                ins.then_inc(z2["yp"], 1)

            def turned(i):
                pe.wait_ge(z2["n3"], done(i))
                pe.wait_ge(z2["h6T"], before(i - 1) if not isinstance(i, int) or i else 1)
                transposes(p_T, n3).then_inc(z2["T3"], 1)
                pe.wait_ge(z2["n3T"], done(i))

            def hidden(i, half):
                if half:
                    pe.wait_ge(z2["g0"], done(i))
                else:
                    pe.wait_ge(z2["tAB"], done(i))
                for f in range(4):
                    fb = 4 * half + f
                    for kb in range(KD):
                        ins = nc.tensor.matmul(p_U[:, f, :], W1[:, kb, fb * P:(fb + 1) * P], n3T[:, kb, :],
                                               start=kb == 0, stop=kb == KD - 1)
                ins.then_inc(z2[f"gp{half}"], 1)

            def network(i):
                pe.wait_ge(z2["g1"], done(i))
                pe.wait_ge(z2["y2"], done(i))
                for a in range(2):
                    for fb in range(FB):
                        ins = nc.tensor.matmul(p_Y[:, a, :], gT[:, fb, a * P:(a + 1) * P], W2[:, fb, :],
                                               start=fb == 0, stop=fb == FB - 1)
                ins.then_inc(z2["ffp"], 1)

            def project(i):
                pe.wait_ge(z2["h6"], done(i))
                transposes(p_T, h6).then_inc(z2["T6"], 1)
                pe.wait_ge(z2["h6T"], done(i))
                for a in range(2):
                    for kb in range(KD):
                        ins = nc.tensor.matmul(p_B[:, a * D:(a + 1) * D], h6T[:, kb, a * P:(a + 1) * P], w["sign"][:, kb, :],
                                               start=kb == 0, stop=kb == KD - 1)
                ins.then_inc(z2["zp"], 1)

            def round(j, i, p):
                if i is not None:
                    forward(i)
                if j is not None:
                    first_a(j, p)
                if i is not None:
                    inverse(i)
                if j is not None:
                    scores(j)
                if i is not None:
                    turned(i)
                    hidden(i, 0)
                if p is not None:
                    project(p)
                if i is not None:
                    hidden(i, 1)
                if j is not None:
                    film(j)
                if i is not None:
                    network(i)

            round(0, None, None)
            round(1, 0, None)
            with pe.Fori(0, B - 2) as p:
                round(p + 2, p + 1, p)
            round(None, B - 1, B - 2)
            round(None, None, B - 1)

def build(nc, args, out):
    with ExitStack() as ctx:
        def sb(name, shape, dt=F32):
            return ctx.enter_context(nc.sbuf_tensor(name, shape, dt))

        X = sb("X", [P, NT, D])
        k = {"ident": sb("ident", [P, P]), "zero": sb("zero", [P, P]), "minus_half": sb("minus_half", [P, 2])}
        setup_constants(nc, args, X, k, ctx)
        self_attention(nc, args, X, k)
        cross_attention(nc, args, X, k)
        experts(nc, args, X, k)
        rwkv(nc, args, X, k)
        state_space(nc, args, X, k, out)


TRANSPOSED = ("L1_attn_Wk", "L1_attn_Wv", "L1_attn_Wr", "L1_attn_Wo", "L1_attn_Wck", "L1_attn_Wcv", "L1_attn_Wcr",
              "L1_ffn_weights", "L1_xattn_A_re", "L1_xattn_A_im", "L1_xattn_C_re", "L1_xattn_C_im",
              "L1_xattn_Wv")


def kernel(**inputs):
    import numpy as _np
    import concourse.bacc as _bacc
    from concourse import mybir as _mybir
    from concourse.bass_utils import run_bass_kernel_spmd as _run

    nc = _bacc.Bacc("TRN2", target_bir_lowering=False, num_devices=1)
    arrays, args = {}, {}
    for name, value in inputs.items():
        a = _np.asarray(value)
        if name in TRANSPOSED:
            a = a.T
        if a.ndim == 0:
            a = a.reshape(1)
        a = _np.ascontiguousarray(a)
        arrays["in_" + name] = a
        args[name] = nc.dram_tensor("in_" + name, a.shape, _mybir.dt.from_np(a.dtype), kind="ExternalInput").ap()
    angle = _np.outer(_np.arange(S), (_np.pi / 2 + 2 * _np.pi * _np.arange(S)) / S)
    forward = _np.concatenate([_np.cos(angle), _np.sin(angle)], axis=1)
    for name, a in (("fourier", forward), ("fourier_inverse", forward.T / S)):
        arrays["in_" + name] = _np.ascontiguousarray(a.astype(_np.float32))
        args[name] = nc.dram_tensor("in_" + name, a.shape, F32, kind="ExternalInput").ap()
    out = nc.dram_tensor("out_0", (B, S, D), F32, kind="ExternalOutput").ap()
    build(nc, args, out)
    r = _run(nc, [arrays], core_ids=[0])
    return r.results[0]["out_0"]
```
